# Optimizing a Trainium2 kernel written in Bass

```python
import numpy as np
import jax
import jax.numpy as jnp

def _softmax(x, axis=-1):
    return jax.nn.softmax(x, axis=axis)

def _gelu(x):
    return jax.nn.gelu(x, approximate=True)

def _silu(x):
    return jax.nn.silu(x)

def _sigmoid(x):
    return jax.nn.sigmoid(x)

def _layernorm(x, axis=-1, eps=1e-05):
    m = jnp.mean(x, axis=axis, keepdims=True)
    v = jnp.var(x, axis=axis, keepdims=True)
    return (x - m) / jnp.sqrt(v + eps)

def _scatter_add(tgt, idx, src, axis=0):
    return tgt.at[idx].add(src)

def _segment_sum(src, seg, n):
    return jax.ops.segment_sum(src, seg, n)
kernel_name = 'mk_seq_preln_d2_jaxref_r8_206927'

def setup_inputs(seed: int=0):
    np.random.seed(seed)
    _w = jnp.asarray

    def _L0_attn_setup():
        import jax, jax.numpy as jnp
        import numpy as np
        DIM_IN, DIM_K, DIM_V, NH = (128, 128, 128, 16)
        DK, DV = (DIM_K // NH, DIM_V // NH)
        key = jax.random.key(seed)
        kx, kq, kk, kv = jax.random.split(key, 4)
        x = jax.random.normal(kx, (4, 256, DIM_IN), dtype=jnp.float32)
        Wq = jax.random.normal(kq, (DIM_K, DIM_IN), dtype=jnp.float32) / np.sqrt(DIM_IN)
        Wk = jax.random.normal(kk, (DK, DIM_IN), dtype=jnp.float32) / np.sqrt(DIM_IN)
        Wv = jax.random.normal(kv, (DV, DIM_IN), dtype=jnp.float32) / np.sqrt(DIM_IN)
        return {'x': x, 'Wq': Wq, 'Wk': Wk, 'Wv': Wv}
    _L0_attn_in = _L0_attn_setup()

    def _L0_ffn_setup():
        import jax, jax.numpy as jnp
        import numpy as np
        D_MODEL = 128
        D_INNER = 256
        N_EXPERTS = 8
        TOP_K = 2
        INIT_STD = 0.02
        key = jax.random.key(seed)
        ks = jax.random.split(key, 6)
        B, S = (2, 256)
        x = jax.random.normal(ks[0], (B, S, D_MODEL), dtype=jnp.float32)
        router_w = jax.random.normal(ks[1], (N_EXPERTS, D_MODEL), dtype=jnp.float32) * (INIT_STD * 0.1)
        router_b = jnp.zeros((N_EXPERTS,), dtype=jnp.float32)
        gate_w = jax.random.normal(ks[2], (N_EXPERTS, D_MODEL, D_INNER), dtype=jnp.float32) * INIT_STD
        up_w = jax.random.normal(ks[3], (N_EXPERTS, D_MODEL, D_INNER), dtype=jnp.float32) * INIT_STD
        down_w = jax.random.normal(ks[4], (N_EXPERTS, D_INNER, D_MODEL), dtype=jnp.float32) * INIT_STD
        return {'x': x, 'router_w': router_w, 'router_b': router_b, 'gate_w': gate_w, 'up_w': up_w, 'down_w': down_w}
    _L0_ffn_in = _L0_ffn_setup()

    def _L1_attn_setup():
        import jax, jax.numpy as jnp
        import numpy as np
        FEATURE_DIM = 16
        NUM_HEADS = 16
        HEAD_DIM = 64
        R2 = float(np.sqrt(2.0))
        RD = float(np.sqrt(FEATURE_DIM))
        RRD = float(np.sqrt(RD))
        RMS_EPS = 1e-05

        def taylor_exp(x):
            x2 = (x[..., :, None] * x[..., None, :]).reshape(*x.shape[:-1], FEATURE_DIM * FEATURE_DIM) / R2
            ones = jnp.ones_like(x[..., :1])
            return jnp.concatenate([ones, x / RRD, x2 / RD], axis=-1)

        def _reference_tuple_inner(hidden_states, Wq, Wk, Wv, Wo, g_weight):
            b, l, _ = hidden_states.shape
            q = (hidden_states @ Wq.T).reshape(b, l, NUM_HEADS, FEATURE_DIM).transpose(0, 2, 1, 3)
            k = (hidden_states @ Wk.T).reshape(b, l, NUM_HEADS, FEATURE_DIM).transpose(0, 2, 1, 3)
            v = (hidden_states @ Wv.T).reshape(b, l, NUM_HEADS, HEAD_DIM).transpose(0, 2, 1, 3)
            qf = taylor_exp(q)
            kf = taylor_exp(k)
            A_qk = jnp.einsum('bhnd,bhmd->bhnm', qf, kf)
            A_qk = jnp.tril(A_qk)
            y = jnp.einsum('bhnm,bhme->bhne', A_qk, v)
            kv_state = jnp.einsum('bhnd,bhnf->bhfd', kf, v)[:, :, None]
            rms = jax.lax.rsqrt(jnp.mean(y * y, axis=-1, keepdims=True) + RMS_EPS)
            y = y * rms * g_weight
            y = y.transpose(0, 2, 1, 3).reshape(b, l, NUM_HEADS * HEAD_DIM)
            out = y @ Wo.T
            return (out, kv_state)
        key = jax.random.key(seed)
        ks = jax.random.split(key, 5)
        b, l, d_model = (4, 256, 128)
        inp = {'hidden_states': jax.random.normal(ks[0], (b, l, d_model), dtype=jnp.float32), 'Wq': jax.random.normal(ks[1], (FEATURE_DIM * NUM_HEADS, d_model), dtype=jnp.float32) * 0.02, 'Wk': jax.random.normal(ks[2], (FEATURE_DIM * NUM_HEADS, d_model), dtype=jnp.float32) * 0.02, 'Wv': jax.random.normal(ks[3], (NUM_HEADS * HEAD_DIM, d_model), dtype=jnp.float32) * 0.02, 'Wo': jax.random.normal(ks[4], (d_model, NUM_HEADS * HEAD_DIM), dtype=jnp.float32) * 0.02, 'g_weight': jnp.ones((HEAD_DIM,), dtype=jnp.float32)}
        return inp
    _L1_attn_in = _L1_attn_setup()

    def _L1_ffn_setup():
        import jax, jax.numpy as jnp
        import numpy as np
        DIM = 128
        HIDDEN = 384
        SCALE = 1.0 / 127.0

        def _dequant(w_int, dtype):
            return w_int.astype(dtype) * jnp.asarray(SCALE, dtype)
        key = jax.random.key(seed)
        k_x, k_g, k_u, k_d = jax.random.split(key, 4)
        x = jax.random.normal(k_x, (4, 256, DIM), dtype=jnp.float32)
        w_gate = jax.random.randint(k_g, (HIDDEN, DIM), -127, 128, dtype=jnp.int32)
        w_up = jax.random.randint(k_u, (HIDDEN, DIM), -127, 128, dtype=jnp.int32)
        w_down = jax.random.randint(k_d, (DIM, HIDDEN), -127, 128, dtype=jnp.int32)
        return {'x': x, 'w_gate': w_gate, 'w_up': w_up, 'w_down': w_down}
    _L1_ffn_in = _L1_ffn_setup()
    _d = {'L0_attn_x': _L0_attn_in['x'], 'L0_attn_Wq': _L0_attn_in['Wq'], 'L0_attn_Wk': _L0_attn_in['Wk'], 'L0_attn_Wv': _L0_attn_in['Wv'], 'L0_ffn_router_w': _L0_ffn_in['router_w'], 'L0_ffn_router_b': _L0_ffn_in['router_b'], 'L0_ffn_gate_w': _L0_ffn_in['gate_w'], 'L0_ffn_up_w': _L0_ffn_in['up_w'], 'L0_ffn_down_w': _L0_ffn_in['down_w'], 'L1_attn_Wq': _L1_attn_in['Wq'], 'L1_attn_Wk': _L1_attn_in['Wk'], 'L1_attn_Wv': _L1_attn_in['Wv'], 'L1_attn_Wo': _L1_attn_in['Wo'], 'L1_attn_g_weight': _L1_attn_in['g_weight'], 'L1_ffn_w_gate': _L1_ffn_in['w_gate'], 'L1_ffn_w_up': _L1_ffn_in['w_up'], 'L1_ffn_w_down': _L1_ffn_in['w_down']}
    _x0 = _d['L0_attn_x']
    _d['L0_attn_x'] = jax.random.normal(jax.random.fold_in(jax.random.key(seed), 1), (2, 1024, 128), dtype=_x0.dtype)
    del _x0
    return _d

def reference(L0_attn_x, L0_attn_Wq, L0_attn_Wk, L0_attn_Wv, L0_ffn_router_w, L0_ffn_router_b, L0_ffn_gate_w, L0_ffn_up_w, L0_ffn_down_w, L1_attn_Wq, L1_attn_Wk, L1_attn_Wv, L1_attn_Wo, L1_attn_g_weight, L1_ffn_w_gate, L1_ffn_w_up, L1_ffn_w_down):

    def _L0_attn_ref(x, Wq, Wk, Wv):
        import jax, jax.numpy as jnp
        import numpy as np
        DIM_IN, DIM_K, DIM_V, NH = (128, 128, 128, 16)
        DK, DV = (DIM_K // NH, DIM_V // NH)
        B, S, _ = x.shape
        scale = 1.0 / np.sqrt(DK)
        q = (x @ Wq.T).reshape(B, S, NH, DK).transpose(0, 2, 1, 3)
        k = x @ Wk.T
        v = x @ Wv.T
        dist = jnp.einsum('bhqd,bkd->bhqk', q, k) * scale
        dist = jax.nn.softmax(dist, axis=-1)
        att = jnp.einsum('bhqk,bkd->bhqd', dist, v)
        return att.transpose(0, 2, 1, 3).reshape(B, S, DIM_V)

    def _L0_ffn_ref(x, router_w, router_b, gate_w, up_w, down_w):
        import jax, jax.numpy as jnp
        import numpy as np
        D_MODEL = 128
        D_INNER = 256
        N_EXPERTS = 8
        TOP_K = 2
        INIT_STD = 0.02
        logits = jnp.einsum('bsd,ed->bse', x, router_w) + router_b
        probs = jax.nn.softmax(logits, axis=-1)
        top_p, top_i = jax.lax.top_k(probs, TOP_K)
        top_p = top_p / jnp.sum(top_p, axis=-1, keepdims=True)
        onehot = jax.nn.one_hot(top_i, N_EXPERTS, dtype=x.dtype)
        combine = jnp.einsum('bsk,bske->bse', top_p, onehot)
        g = jnp.einsum('bsd,edf->ebsf', x, gate_w)
        u = jnp.einsum('bsd,edf->ebsf', x, up_w)
        h = jax.nn.silu(g) * u
        y = jnp.einsum('ebsf,efd->ebsd', h, down_w)
        out = jnp.einsum('ebsd,bse->bsd', y, combine)
        return out

    def _L1_attn_ref(hidden_states, Wq, Wk, Wv, Wo, g_weight):
        import jax, jax.numpy as jnp
        import numpy as np
        FEATURE_DIM = 16
        NUM_HEADS = 16
        HEAD_DIM = 64
        R2 = float(np.sqrt(2.0))
        RD = float(np.sqrt(FEATURE_DIM))
        RRD = float(np.sqrt(RD))
        RMS_EPS = 1e-05

        def taylor_exp(x):
            x2 = (x[..., :, None] * x[..., None, :]).reshape(*x.shape[:-1], FEATURE_DIM * FEATURE_DIM) / R2
            ones = jnp.ones_like(x[..., :1])
            return jnp.concatenate([ones, x / RRD, x2 / RD], axis=-1)

        def _reference_tuple_inner(hidden_states, Wq, Wk, Wv, Wo, g_weight):
            b, l, _ = hidden_states.shape
            q = (hidden_states @ Wq.T).reshape(b, l, NUM_HEADS, FEATURE_DIM).transpose(0, 2, 1, 3)
            k = (hidden_states @ Wk.T).reshape(b, l, NUM_HEADS, FEATURE_DIM).transpose(0, 2, 1, 3)
            v = (hidden_states @ Wv.T).reshape(b, l, NUM_HEADS, HEAD_DIM).transpose(0, 2, 1, 3)
            qf = taylor_exp(q)
            kf = taylor_exp(k)
            A_qk = jnp.einsum('bhnd,bhmd->bhnm', qf, kf)
            A_qk = jnp.tril(A_qk)
            y = jnp.einsum('bhnm,bhme->bhne', A_qk, v)
            kv_state = jnp.einsum('bhnd,bhnf->bhfd', kf, v)[:, :, None]
            rms = jax.lax.rsqrt(jnp.mean(y * y, axis=-1, keepdims=True) + RMS_EPS)
            y = y * rms * g_weight
            y = y.transpose(0, 2, 1, 3).reshape(b, l, NUM_HEADS * HEAD_DIM)
            out = y @ Wo.T
            return (out, kv_state)
        return _reference_tuple_inner(hidden_states, Wq, Wk, Wv, Wo, g_weight)[0]

    def _L1_ffn_ref(x, w_gate, w_up, w_down):
        import jax, jax.numpy as jnp
        import numpy as np
        DIM = 128
        HIDDEN = 384
        SCALE = 1.0 / 127.0

        def _dequant(w_int, dtype):
            return w_int.astype(dtype) * jnp.asarray(SCALE, dtype)
        wg = _dequant(w_gate, x.dtype)
        wu = _dequant(w_up, x.dtype)
        wd = _dequant(w_down, x.dtype)
        gate = jnp.einsum('bsd,hd->bsh', x, wg)
        up = jnp.einsum('bsd,hd->bsh', x, wu)
        h = jax.nn.silu(gate) * up
        return jnp.einsum('bsh,dh->bsd', h, wd)
    x = L0_attn_x
    x = x + _L0_attn_ref(_layernorm(x, axis=-1), L0_attn_Wq, L0_attn_Wk, L0_attn_Wv)
    x = x + _L0_ffn_ref(_layernorm(x, axis=-1), L0_ffn_router_w, L0_ffn_router_b, L0_ffn_gate_w, L0_ffn_up_w, L0_ffn_down_w)
    x = x + _L1_attn_ref(_layernorm(x, axis=-1), L1_attn_Wq, L1_attn_Wk, L1_attn_Wv, L1_attn_Wo, L1_attn_g_weight)
    x = x + _L1_ffn_ref(_layernorm(x, axis=-1), L1_ffn_w_gate, L1_ffn_w_up, L1_ffn_w_down)
    return x

_drawn_inputs = setup_inputs


def setup_inputs(seed=0):
    import zlib

    import numpy as np

    out = dict(_drawn_inputs(seed))
    spreads = {'L0_ffn_router_b': (0.0, 0.8), 'L1_attn_g_weight': (1.0, 0.2)}
    factors = {'L0_ffn_router_w': 8.0,
     'L0_ffn_gate_w': 5.306,
     'L0_ffn_up_w': 5.369,
     'L0_ffn_down_w': 5.582}
    for name, (base, spread) in spreads.items():
        noise = np.random.default_rng([zlib.crc32(name.encode()), seed]).standard_normal(out[name].shape)
        drawn = base * np.exp(spread * noise) if base else spread * noise
        out[name] = jnp.asarray(drawn.astype(out[name].dtype))
    for name, factor in factors.items():
        out[name] = (out[name] * factor).astype(out[name].dtype)
    return out
```

```python
from contextlib import ExitStack

import numpy as np
import concourse.bass as bass
from concourse import mybir

F32, BF16, I32 = mybir.dt.float32, mybir.dt.bfloat16, mybir.dt.int32
ALU = mybir.AluOpType
ACT = mybir.ActivationFunctionType
AX = mybir.AxisListType

P = 128
BATCH, SEQ = 2, 1024
TOKENS = BATCH * SEQ
TILES = TOKENS // P
CH = 512
CHUNKS = TOKENS // CH
TPC = CH // P
KT = SEQ // P
LN_EPS = 1e-5
LN_EXP = "natural_log_exp_and_others"

H0, DH0 = 16, 8
HG = 4
GROUPS = H0 // HG
UNITS = CHUNKS * GROUPS
STACK = 96
MROW = 64
SCALE0 = float(1.0 / np.sqrt(DH0))
PRODUCTS0 = [(n // 3, n % 3, 8 * n if n < 8 else MROW + 3) for n in range(9)]

EXPERTS, DFF0 = 8, 256
FH = DFF0 // P

H1, DF, DV1 = 16, 16, 64
PAIRS = H1 // 2
HALF = H1 // 2
PRODUCTS1 = [(0, 0), (0, 1), (1, 0), (0, 2), (2, 0), (1, 1)]
RMS_EPS = 1e-5

HID = 384
HT = HID // P
QSCALE = float(np.float32(1.0 / 127.0))


class Norm:

    def __init__(self, nc, ctx, tag, buf):
        self.nc, self.b = nc, buf
        sem = lambda n: ctx.enter_context(nc.semaphore(f"{tag}_{n}"))
        self.stats, self.moments, self.logv, self.rstd = sem("stats"), sem("moments"), sem("logv"), sem("rstd")
        self.normed, self.turned, self.done = sem("normed"), sem("turned"), sem("xnT")

    def vector(self, dve, c):
        nc, b = self.nc, self.b
        for t in range(TPC * c, TPC * (c + 1)):
            nc.vector.bn_stats(b["bn"][:, t, :], b["x"][:, t, :]).then_inc(self.stats, 1)
        dve.wait_ge(self.stats, TPC * (c + 1))
        for t in range(TPC * c, TPC * (c + 1)):
            nc.vector.bn_aggr(b["mv"][:, t, :], b["bn"][:, t, :]).then_inc(self.moments, 1)
        dve.wait_ge(self.rstd, c + 1)
        if c >= 2:
            dve.wait_ge(self.turned, c - 1)
        for t in range(TPC * c, TPC * (c + 1)):
            nc.vector.tensor_scalar(b["xn"][:, t % (2 * TPC), :], b["x"][:, t, :], b["mv"][:, t, 0:1],
                                    b["rstd"][:, t:t + 1], ALU.subtract, ALU.mult).then_inc(self.normed, 1)

    def scalar_rstd(self, act, c):
        nc, b = self.nc, self.b
        s = slice(TPC * c, TPC * (c + 1))
        act.wait_ge(self.moments, TPC * (c + 1))
        nc.scalar.activation(b["logv"][:, s], b["mv"][:, s, 1], ACT.Ln, bias=b["eps"][:, 0:1]).then_inc(self.logv, 1)
        act.wait_ge(self.logv, c + 1)
        nc.scalar.activation(b["rstd"][:, s], b["logv"][:, s], ACT.Exp, scale=-0.5).then_inc(self.rstd, 1)

    def tensor(self, pe, c, banks):
        nc, b = self.nc, self.b
        if c >= 2:
            pe.wait_ge(self.done, c - 1)
        for k in range(TPC):
            t = TPC * c + k
            pe.wait_ge(self.normed, t + 1)
            mm = nc.tensor.transpose(banks[c % 2][:, P * k:P * (k + 1)], b["xn"][:, t % (2 * TPC), :], b["ident"][:])
        mm.then_inc(self.turned, 1)

    def scalar_copy(self, act, c, banks):
        act.wait_ge(self.turned, c + 1)
        self.nc.scalar.activation(self.b["xnT"][:, CH * c:CH * (c + 1)], banks[c % 2][:, :],
                                  ACT.Copy).then_inc(self.done, 1)


def build(nc, x_in, wq0, wk0, wv0, rw, rb, gate_w, up_w, down_w, wq1, wk1, wv1, wo1, g1, wg2, wu2, wd2, out):
    ctx = ExitStack()
    with ctx:
        def sb(name, shape, dt=F32):
            return ctx.enter_context(nc.sbuf_tensor(name, shape, dt))

        def sem(name):
            return ctx.enter_context(nc.semaphore(name))

        b = {
            "x": sb("x", [P, TILES, P]), "xnT": sb("xnT", [P, TOKENS]), "xn": sb("xn", [P, 2 * TPC, P]),
            "bn": sb("bn", [P, TILES, 6]), "mv": sb("mv", [P, TILES, 2]), "logv": sb("logv", [P, TILES]),
            "rstd": sb("rstd", [P, TILES]), "eps": sb("eps", [P, 1]), "ident": sb("ident", [P, P]),
            "parts": sb("parts", [P, 2, 3, CH], BF16),
        }
        x, xnT = b["x"], b["xnT"]
        ident, ident16 = b["ident"], sb("ident16", [P, P], BF16)
        banks = [ctx.enter_context(nc.psum_tensor(f"bank{i}", [P, CH], F32)) for i in range(4)]
        pair_banks = [ctx.enter_context(nc.psum_tensor(f"pair{i}", [P, 2, CH], F32)) for i in range(2)]

        arena = sb("arena", [STACK, UNITS * HG * CH], BF16)
        w_up = sb("w_up", [P, 2, 2, DFF0])
        w_down = sb("w_down", [P, 2, FH, P])
        wv1_sb, wo1_sb = sb("wv1_sb", [P, H1 * DV1]), sb("wo1_sb", [P, PAIRS, P])
        wqk1_sb = sb("wqk1_sb", [P, 2, 2, P])
        g_half = sb("g_half", [P, 1])
        ints = sb("ints", [P, 3, HID], I32)
        probs = sb("probs", [P, 4, 2, CH])
        work = sb("work", [P, 8 * CH])

        s_x = [sem(f"s_x{c}") for c in range(CHUNKS)]
        s_w0, s_router, s_w1, s_w2 = sem("s_w0"), sem("s_router"), sem("s_w1"), sem("s_w2")
        s_exp_w = [sem("s_exp_w0"), sem("s_exp_w1")]
        x_dram = x_in.rearrange("(t p) d -> p t d", p=P)

        first_attention(nc, ctx, sb, sem, b, banks, pair_banks, arena, probs, work, ident16,
                        s_x, s_w0, x_dram, wq0, wk0, wv0)
        experts(nc, ctx, sb, sem, b, banks, pair_banks, work, w_up, w_down, s_exp_w, s_router,
                rw, rb, gate_w, up_w, down_w,
                [(wqk1_sb[:, 0, :, :], wq1, s_w1), (wqk1_sb[:, 1, :, :], wk1, s_w1), (wv1_sb[:], wv1, s_w1),
                 (wo1_sb[:], wo1, s_w1), (g_half[0:DV1, :], g1, s_w1), (g_half[DV1:P, :], g1, s_w1),
                 (ints[:, 0, :], wg2, s_w2), (ints[:, 1, :], wu2, s_w2), (ints[:, 2, :], wd2.rearrange("p j d -> p (j d)"), s_w2)])
        second_attention(nc, ctx, sb, sem, b, banks, pair_banks, arena, probs, work, wqk1_sb, wv1_sb, wo1_sb, g_half, s_w1)
        feed_forward(nc, ctx, sb, sem, b, banks, pair_banks, work, ints, s_w2, out)


def first_attention(nc, ctx, sb, sem, b, banks, pair_banks, arena, probs, work, ident16,
                    s_x, s_w0, x_dram, wq0, wk0, wv0):
    x, xnT, ident = b["x"], b["xnT"], b["ident"]
    q_op = arena[:, :].rearrange("r (u h n) -> r u h n", u=UNITS, h=HG)
    q_rows = arena[:, :].rearrange("r (c m) -> r c m", c=CHUNKS)
    k_op = sb("k_op", [STACK, TOKENS], BF16)
    v_op = sb("v_op", [P, TILES, 32])
    wq_sb, wk_sb, wv_sb = sb("wq0_sb", [P, P]), sb("wk0_sb", [P, DH0]), sb("wv0_sb", [P, DH0])
    q_parts = b["parts"]
    k_parts = sb("k_parts", [DH0, 2, 3, CH], BF16)
    q_rest = work[:, 0:CH]
    k_rest = work[0:DH0, CH:2 * CH]
    halves = sb("halves", [P, UNITS, TPC, HG, 2])
    top, zero = sb("top", [P, TPC, HG]), sb("zero", [P, TPC, HG])
    neg, neg_rest = sb("neg", [P, TPC, HG]), sb("neg_rest", [P, TPC, HG])
    neg_parts = sb("neg_parts", [P, TPC, 3, HG], BF16)
    neg_t = sb("neg_t", [3 * HG, CH], BF16)
    pv_sb = work[:, 2 * CH:3 * CH]
    recip = sb("recip", [P, TPC, HG])
    ratio = work[:, 3 * CH:4 * CH].rearrange("p (t h d) -> p t h d", t=TPC, h=HG)[:, :, :, 0:DH0]

    norm = Norm(nc, ctx, "n0", b)
    s_zeroed, s_const, s_ones = sem("s_zeroed"), sem("s_const"), sem("s_ones")
    s_qproj, s_qhi, s_qrest, s_qmid, s_qlo = (sem(f"s_q_{n}") for n in ("proj", "hi", "rest", "mid", "lo"))
    s_kproj, s_khi, s_krest, s_kmid, s_klo = (sem(f"s_k_{n}") for n in ("proj", "hi", "rest", "mid", "lo"))
    s_copied = [sem("s_copied0"), sem("s_copied1")]
    COPIES = 16 * 2 * len(PRODUCTS0)
    s_vproj, s_v = sem("s_vproj"), sem("s_v")

    with nc.Block() as block:
        @block.sync
        def _(sp):
            for c in range(CHUNKS):
                sp.dma_start(x[:, TPC * c:TPC * (c + 1), :], x_dram[:, TPC * c:TPC * (c + 1), :]).then_inc(s_x[c], 16)
                if c == 0:
                    for dst, src in ((wq_sb, wq0), (wk_sb, wk0), (wv_sb, wv0)):
                        sp.dma_start(dst[:], src).then_inc(s_w0, 16)
            sp.wait_ge(s_zeroed, 2)
            sp.wait_ge(s_ones, 1)
            for c in range(CHUNKS):
                sp.wait_ge(s_klo, c + 1)
                for qp, kp, row in PRODUCTS0:
                    sp.dma_start(k_op[row:row + DH0, CH * c:CH * (c + 1)], k_parts[:, c % 2, kp, :]).then_inc(s_copied[c % 2], 16)
                sp.wait_ge(s_qlo, c + 1)
                for qp, kp, row in PRODUCTS0:
                    sp.dma_start(q_rows[row:row + DH0, c, :], q_parts[:, c % 2, qp, :]).then_inc(s_copied[c % 2], 16)
            for s in s_copied:
                sp.wait_ge(s, COPIES * CHUNKS // 2)

        @block.gpsimd
        def _(pool):
            nc.gpsimd.memset(ident[:], 0.0).then_inc(s_const, 1)
            nc.gpsimd.memset(b["eps"][:], LN_EPS).then_inc(s_const, 1)
            nc.gpsimd.memset(zero[:], 0.0)
            pool.wait_ge(s_const, 2)
            nc.gpsimd.affine_select(out=ident[:], in_=ident[:], compare_op=ALU.not_equal, fill=1.0, base=0,
                                    pattern=[[-1, P]], channel_multiplier=1).then_inc(s_const, 1)
            pool.wait_ge(s_const, 3)
            nc.gpsimd.tensor_copy(ident16[:], ident[:]).then_inc(s_const, 1)
            nc.gpsimd.memset(v_op[:], 0.0).then_inc(s_const, 1)
            pool.wait_ge(s_const, 5)
            nc.gpsimd.memset(v_op[:, :, DH0:DH0 + 1], 1.0).then_inc(s_const, 1)
            pool.wait_ge(s_const, 6)
            nc.gpsimd.memset(k_op[MROW:STACK, :], 0.0).then_inc(s_zeroed, 1)
            nc.gpsimd.memset(arena[MROW:STACK, :].bitcast(F32), 0.0).then_inc(s_zeroed, 1)
            pool.wait_ge(s_zeroed, 2)
            nc.gpsimd.memset(k_op[MROW:MROW + 3, :], 1.0).then_inc(s_ones, 1)

        @block.vector
        def _(dve):
            for c in range(CHUNKS):
                dve.wait_ge(s_x[c], 16)
                norm.vector(dve, c)
                dve.wait_ge(s_qhi, c + 1)
                if c:
                    dve.wait_ge(s_qlo, c)
                nc.vector.tensor_tensor(q_rest, banks[2][:, :], q_parts[:, c % 2, 0, :], ALU.subtract).then_inc(s_qrest, 1)
                dve.wait_ge(s_khi, c + 1)
                if c:
                    dve.wait_ge(s_klo, c)
                nc.vector.tensor_tensor(k_rest, banks[3][0:DH0, :], k_parts[:, c % 2, 0, :], ALU.subtract).then_inc(s_krest, 1)
                dve.wait_ge(s_vproj, c + 1)
                dve.wait_ge(s_const, 6)
                nc.vector.tensor_copy(v_op[:, TPC * c:TPC * (c + 1), 0:DH0],
                                      pair_banks[0][:, 0, 0:TPC * DH0].rearrange("p (t d) -> p t d", t=TPC)).then_inc(s_v, 1)
                dve.wait_ge(s_kmid, c + 1)
                nc.vector.tensor_tensor(k_parts[:, c % 2, 2, :], k_rest, k_parts[:, c % 2, 1, :], ALU.subtract).then_inc(s_klo, 1)
                dve.wait_ge(s_qmid, c + 1)
                nc.vector.tensor_tensor(q_parts[:, c % 2, 2, :], q_rest, q_parts[:, c % 2, 1, :], ALU.subtract).then_inc(s_qlo, 1)

        @block.scalar
        def _(act):
            nc.scalar.preload_act_table_set(LN_EXP)
            act.wait_ge(s_const, 2)
            for c in range(CHUNKS):
                norm.scalar_rstd(act, c)
                norm.scalar_copy(act, c, banks)
                if c >= 2:
                    act.wait_ge(s_copied[c % 2], COPIES * (c // 2))
                act.wait_ge(s_qproj, c + 1)
                nc.scalar.activation(q_parts[:, c % 2, 0, :], banks[2][:, :], ACT.Copy).then_inc(s_qhi, 1)
                act.wait_ge(s_kproj, c + 1)
                nc.scalar.activation(k_parts[:, c % 2, 0, :], banks[3][0:DH0, :], ACT.Copy).then_inc(s_khi, 1)
                act.wait_ge(s_krest, c + 1)
                nc.scalar.activation(k_parts[:, c % 2, 1, :], k_rest, ACT.Copy).then_inc(s_kmid, 1)
                act.wait_ge(s_qrest, c + 1)
                nc.scalar.activation(q_parts[:, c % 2, 1, :], q_rest, ACT.Copy).then_inc(s_qmid, 1)

        @block.tensor
        def _(pe):
            pe.wait_ge(s_const, 3)
            for c in range(CHUNKS):
                norm.tensor(pe, c, banks)
                pe.wait_ge(s_w0, 48)
                pe.wait_ge(norm.done, c + 1)
                cols = xnT[:, CH * c:CH * (c + 1)]
                if c:
                    pe.wait_ge(s_qrest, c)
                    pe.wait_ge(s_krest, c)
                    pe.wait_ge(s_v, c)
                nc.tensor.matmul(banks[2][:, :], wq_sb[:], cols, start=True, stop=True).then_inc(s_qproj, 1)
                nc.tensor.matmul(banks[3][0:DH0, :], wk_sb[:], cols, start=True, stop=True).then_inc(s_kproj, 1)
                for k in range(TPC):
                    mm = nc.tensor.matmul(pair_banks[0][:, 0, DH0 * k:DH0 * (k + 1)],
                                          xnT[:, CH * c + P * k:CH * c + P * (k + 1)], wv_sb[:], start=True, stop=True)
                mm.then_inc(s_vproj, 1)

    s_mx, s_red = sem("s_mx"), sem("s_red")
    s_top, s_neg, s_nhi, s_nrest, s_nmid, s_nparts = (sem(f"s_n_{n}") for n in ("top", "neg", "hi", "rest", "mid", "parts"))
    s_nt, s_ncopied, s_ndma = sem("s_nt"), sem("s_ncopied"), sem("s_ndma")
    s_sc, s_exp, s_pv, s_pvcopy = sem("s_sc"), sem("s_exp"), sem("s_pv"), sem("s_pvcopy")
    s_ot, s_recip, s_ratio, s_added = sem("s_ot"), sem("s_recip"), sem("s_ratio"), sem("s_added")
    neg_bank = banks[3][:, :].bitcast(BF16)

    with nc.Block() as block:
        MAXES = TPC * HG * 2
        EXPS = 2 * KT

        @block.tensor
        def _(pe):
            def maxima(u, i, bt):
                t, h, half = i // (2 * HG), (i // 2) % HG, i % 2
                if not (isinstance(u, int) and u == 0 and i < 2):
                    pe.wait_ge(s_red, u * MAXES + i - 1)
                nc.tensor.matmul(banks[i % 2][:, :], q_op[:, u, h, P * t:P * (t + 1)],
                                 k_op[:, bt * SEQ + half * CH:bt * SEQ + (half + 1) * CH],
                                 start=True, stop=True).then_inc(s_mx, 1)

            def scores(u, kt, pr, bt):
                if not (isinstance(u, int) and u == 0 and kt == 0):
                    pe.wait_ge(s_exp, u * EXPS + 2 * kt + pr - 1)
                for h in range(2):
                    mm = nc.tensor.matmul(pair_banks[pr][:, h, :], k_op[:, bt * SEQ + P * kt:bt * SEQ + P * (kt + 1)],
                                          q_op[:, u, 2 * pr + h, :], start=True, stop=True)
                mm.then_inc(s_sc, 1)

            def values(u, kt, bt):
                pe.wait_ge(s_exp, u * EXPS + 2 * kt + 2)
                for h in range(HG):
                    mm = nc.tensor.matmul(banks[2][32 * h:32 * h + 32, :], v_op[:, bt * KT + kt, :],
                                          probs[:, 2 * (kt % 2) + h // 2, h % 2, :], start=(kt == 0), stop=(kt == KT - 1))
                mm.then_inc(s_pv, 1)

            def negated(u):
                pe.wait_ge(s_nparts, u + 1)
                if not (isinstance(u, int) and u <= 2):
                    pe.wait_ge(s_added, u - 2)
                for t in range(TPC):
                    mm = nc.tensor.transpose(neg_bank[0:3 * HG, P * t:P * (t + 1)], neg_parts[:, t, :, :].rearrange("p n h -> p (n h)"), ident16[:])
                mm.then_inc(s_nt, 1)

            def outputs(u, copied):
                pe.wait_ge(s_pvcopy, u + 1)
                if isinstance(u, int) and u >= UNITS - 2:
                    pe.wait_ge(s_added, u)
                pe.wait_ge(s_ncopied, copied)
                for t in range(TPC):
                    mm = nc.tensor.transpose(banks[3][:, P * t:P * (t + 1)], pv_sb[:, P * t:P * (t + 1)], ident[:])
                mm.then_inc(s_ot, 1)

            def unit(u, bt, bt_max, first=False):
                def maximum(i):
                    if bt_max is not None:
                        maxima(u + 2, i, bt_max)

                last_bt = bt - 1 if isinstance(u, int) and u == UNITS // 2 else bt
                for kt in range(KT):
                    maximum(4 * kt)
                    if kt == 0:
                        pe.wait_ge(s_ndma, 16 * (u + 1))
                    scores(u, kt, 0, bt)
                    maximum(4 * kt + 1)
                    scores(u, kt, 1, bt)
                    maximum(4 * kt + 2)
                    maximum(4 * kt + 3)
                    if kt == 0 and not first:
                        values(u - 1, KT - 1, last_bt)
                    if kt == 1:
                        if not (isinstance(u, int) and u == UNITS - 1):
                            negated(u + 1)
                        if not first:
                            pe.wait_ge(s_pvcopy, u)
                    if kt:
                        values(u, kt - 1, bt)
                    if kt == 4 and not first:
                        outputs(u - 1, u + 2 if not (isinstance(u, int) and u == UNITS - 1) else UNITS)

            half = UNITS // 2
            for i in range(MAXES):
                maxima(0, i, 0)
            negated(0)
            for i in range(MAXES):
                maxima(1, i, 0)
            unit(0, 0, 0, first=True)
            unit(1, 0, 0)
            with pe.Fori(2, half - 2) as u:
                unit(u, 0, 0)
            unit(half - 2, 0, 1)
            unit(half - 1, 0, 1)
            unit(half, 1, 1)
            with pe.Fori(half + 1, UNITS - 2) as u:
                unit(u, 1, 1)
            unit(UNITS - 2, 1, None)
            unit(UNITS - 1, 1, None)
            values(UNITS - 1, KT - 1, 1)
            outputs(UNITS - 1, UNITS)

        @block.scalar
        def _(act):
            def exponentials(u, kt):
                for pr in range(2):
                    e = u * EXPS + 2 * kt + pr
                    act.wait_ge(s_sc, e + 1)
                    if not (isinstance(u, int) and u == 0 and kt < 2):
                        act.wait_ge(s_pv, u * KT + kt - 1)
                    nc.scalar.activation(probs[:, 2 * (kt % 2) + pr, :, :], pair_banks[pr][:, :, :], ACT.Exp,
                                         scale=SCALE0).then_inc(s_exp, 1)

            def negated(u):
                act.wait_ge(s_nt, u + 1)
                if not (isinstance(u, int) and u == 0):
                    act.wait_ge(s_ndma, 16 * u)
                nc.scalar.activation(neg_t[:, :], neg_bank[0:3 * HG, 0:CH], ACT.Copy).then_inc(s_ncopied, 1)

            def result(u):
                act.wait_ge(s_pv, KT * (u + 1))
                if not (isinstance(u, int) and u == 0):
                    act.wait_ge(s_ot, u)
                nc.scalar.activation(pv_sb, banks[2][:, :], ACT.Copy).then_inc(s_pvcopy, 1)

            def unit(u, first=False, last=False):
                for kt in range(KT):
                    exponentials(u, kt)
                    if kt == 0 and not first:
                        result(u - 1)
                    if kt == 1 and not last:
                        negated(u + 1)

            negated(0)
            unit(0, first=True)
            with act.Fori(1, UNITS - 1) as u:
                unit(u)
            unit(UNITS - 1, last=True)
            result(UNITS - 1)

        @block.vector
        def _(dve):
            def reduce(u, i):
                dve.wait_ge(s_mx, u * MAXES + i + 1)
                nc.vector.tensor_reduce(halves[:, u, i // (2 * HG), (i // 2) % HG, i % 2:i % 2 + 1], banks[i % 2][:, :], axis=AX.X,
                                        op=ALU.max).then_inc(s_red, 1)
                if i == MAXES - 1:
                    dve.wait_ge(s_red, u * MAXES + MAXES)
                    if not (isinstance(u, int) and u == 0):
                        dve.wait_ge(s_neg, u)
                        dve.wait_ge(s_nhi, u)
                    nc.vector.tensor_tensor(top[:], halves[:, u, :, :, 0], halves[:, u, :, :, 1],
                                            ALU.max).then_inc(s_top, 1)

            def add_result(c, g):
                u = GROUPS * c + g
                bank = banks[3][:, :].rearrange("p (t h d) -> p t h d", t=TPC, h=HG)
                dve.wait_ge(s_ot, u + 1)
                nc.vector.reciprocal(recip[:, :, :], bank[:, :, :, DH0]).then_inc(s_recip, 1)
                dve.wait_ge(s_recip, u + 1)
                nc.vector.tensor_tensor(ratio, bank[:, :, :, 0:DH0],
                                        recip[:, :, :].unsqueeze(3).to_broadcast([P, TPC, HG, DH0]), ALU.mult).then_inc(s_ratio, 1)
                dve.wait_ge(s_ratio, u + 1)
                cols = x[:, TPC * c:TPC * (c + 1), bass.ds(g * (HG * DH0), HG * DH0)].rearrange("p t (h d) -> p t h d", h=HG)
                nc.vector.tensor_tensor(cols, cols, ratio, ALU.add).then_inc(s_added, 1)

            AHEAD = 3

            def step(c, g):
                for i in range(20):
                    reduce(GROUPS * c + g + AHEAD, i)
                add_result(c, g)
                for i in range(20, MAXES):
                    reduce(GROUPS * c + g + AHEAD, i)

            for u in range(AHEAD):
                for i in range(MAXES):
                    reduce(u, i)
            for c in range(CHUNKS - 1):
                with dve.Fori(0, GROUPS) as g:
                    step(c, g)
            step(CHUNKS - 1, 0)
            with dve.Fori(1, GROUPS) as g:
                add_result(CHUNKS - 1, g)

        @block.gpsimd
        def _(pool):
            def parts(u):
                view = lambda n: neg_parts[:, :, n, :]
                pool.wait_ge(s_top, u + 1)
                if not (isinstance(u, int) and u == 0):
                    pool.wait_ge(s_nt, u)
                nc.gpsimd.tensor_tensor(neg[:], zero[:], top[:], ALU.subtract).then_inc(s_neg, 1)
                nc.gpsimd.tensor_tensor(view(0), zero[:], top[:], ALU.subtract).then_inc(s_nhi, 1)
                pool.wait_ge(s_neg, u + 1)
                pool.wait_ge(s_nhi, u + 1)
                nc.gpsimd.tensor_tensor(neg_rest[:], neg[:], view(0), ALU.subtract).then_inc(s_nrest, 1)
                pool.wait_ge(s_nrest, u + 1)
                nc.gpsimd.tensor_tensor(view(1), neg_rest[:], zero[:], ALU.add).then_inc(s_nmid, 1)
                pool.wait_ge(s_nmid, u + 1)
                nc.gpsimd.tensor_tensor(view(2), neg_rest[:], view(1), ALU.subtract).then_inc(s_nparts, 1)

            parts(0)
            with pool.Fori(1, UNITS) as u:
                parts(u)

        @block.sync
        def _(sp):
            def rows(u):
                sp.wait_ge(s_ncopied, u + 1)
                sp.dma_start(q_op[MROW:MROW + 3, u, :, :], neg_t[:, :]).then_inc(s_ndma, 16)

            rows(0)
            with sp.Fori(1, UNITS) as u:
                rows(u)
            sp.wait_ge(s_ndma, 16 * UNITS)


def experts(nc, ctx, sb, sem, b, banks, pair_banks, work, w_up, w_down, s_exp_w, s_router, rw, rb, gate_w, up_w, down_w, later_loads):
    x, xnT = b["x"], b["xnT"]
    rw_sb, rb_sb, rank = sb("rw_sb", [P, EXPERTS]), sb("rb_sb", [P, EXPERTS]), sb("rank", [P, EXPERTS])
    small = {n: sb(f"router_{n}", [P, TILES, EXPERTS]) for n in ("logit", "prob", "rest", "mark", "sel1", "sel2", "combine")}
    narrow = {n: sb(f"router_{n}", [P, TILES]) for n in ("max", "sum", "inv", "p1", "p2", "first", "den", "iden")}
    combine = small["combine"]
    hidden = work[:, 0:4 * CH].rearrange("p (s f n) -> p s f n", s=2, f=FH)
    silu = work[:, 4 * CH:6 * CH].rearrange("p (s n) -> p s n", s=2)
    wide = lambda ap: ap.unsqueeze(2).to_broadcast([P, TILES, EXPERTS])
    per_tile = lambda ap: ap.unsqueeze(1).to_broadcast([P, TILES, EXPERTS])

    norm = Norm(nc, ctx, "n1", b)
    s_rank, s_logit, s_shift, s_prob, s_route, s_combine = (sem(f"s_r_{n}") for n in ("rank", "logit", "shift", "prob", "chain", "combine"))
    s_gu, s_silu, s_hid, s_down, s_acc = (sem(f"s_e_{n}") for n in ("gu", "silu", "hid", "down", "acc"))
    STEPS = CHUNKS

    with nc.Block() as block:
        @block.sync
        def _(sp):
            sp.dma_start(rw_sb[:], rw).then_inc(s_router, 16)
            sp.dma_start(rb_sb[:], rb.to_broadcast([P, EXPERTS])).then_inc(s_router, 16)

            def load(e, slot):
                sp.dma_start(w_up[:, slot, 0, :], gate_w[e, :, :]).then_inc(s_exp_w[slot], 16)
                sp.dma_start(w_up[:, slot, 1, :], up_w[e, :, :]).then_inc(s_exp_w[slot], 16)
                sp.dma_start(w_down[:, slot, :, :], down_w[e, :, :, :].rearrange("f p d -> p f d")).then_inc(s_exp_w[slot], 16)

            load(0, 0)
            load(1, 1)
            for dst, src, signal in later_loads:
                sp.dma_start(dst, src).then_inc(signal, 16)
            with sp.Fori(1, EXPERTS // 2) as pair:
                for slot in range(2):
                    sp.wait_ge(s_down, pair * 2 * STEPS + (slot - 1) * STEPS)
                    load(pair * 2 + slot, slot)

        @block.gpsimd
        def _(pool):
            for e in range(EXPERTS):
                nc.gpsimd.memset(rank[:, e:e + 1], float(EXPERTS - e)).then_inc(s_rank, 1)

        @block.tensor
        def _(pe):
            def gate_up(e, slot, c, f):
                i = (e * STEPS + c) * FH + f
                if not (isinstance(e, int) and e == 0 and c == 0):
                    pe.wait_ge(s_hid, i - 1)
                for m in range(2):
                    mm = nc.tensor.matmul(pair_banks[f][:, m, :], w_up[:, slot, m, P * f:P * (f + 1)],
                                          xnT[:, CH * c:CH * (c + 1)], start=True, stop=True)
                mm.then_inc(s_gu, 1)

            def down(e, slot, c):
                k = e * STEPS + c
                pe.wait_ge(s_hid, FH * (k + 1))
                if not (isinstance(e, int) and e == 0 and c < 2):
                    pe.wait_ge(s_acc, TPC * (k - 1))
                for t in range(TPC):
                    for f in range(FH):
                        mm = nc.tensor.matmul(banks[c % 2][:, P * t:P * (t + 1)], hidden[:, c % 2, f, P * t:P * (t + 1)],
                                              w_down[:, slot, f, :], start=(f == 0), stop=(f == FH - 1))
                mm.then_inc(s_down, 1)

            def expert(e, slot, first=False):
                pe.wait_ge(s_exp_w[slot], (e - slot) * 24 + 48)
                for c in range(STEPS):
                    for f in range(FH):
                        gate_up(e, slot, c, f)
                        if f == 0 and c:
                            down(e, slot, c - 1)
                        if f == 0 and c == 0 and not first:
                            down(e - 1, 1 - slot, STEPS - 1)

            for c in range(CHUNKS):
                norm.tensor(pe, c, banks)
            pe.wait_ge(s_router, 32)
            pe.wait_ge(norm.done, CHUNKS)
            for t in range(TILES):
                mm = nc.tensor.matmul(banks[2][:, EXPERTS * t:EXPERTS * (t + 1)], xnT[:, P * t:P * (t + 1)], rw_sb[:],
                                      start=True, stop=True)
            mm.then_inc(s_logit, 1)
            expert(0, 0, first=True)
            expert(1, 1)
            with pe.Fori(1, EXPERTS // 2) as pair:
                expert(pair * 2, 0)
                expert(pair * 2 + 1, 1)
            down(EXPERTS - 1, 1, STEPS - 1)

        @block.scalar
        def _(act):
            nc.scalar.preload_act_table_set(LN_EXP)
            for c in range(CHUNKS):
                norm.scalar_rstd(act, c)
                norm.scalar_copy(act, c, banks)
            act.wait_ge(s_shift, 1)
            nc.scalar.activation(small["prob"][:], small["logit"][:], ACT.Exp).then_inc(s_prob, 1)

            def expert(e):
                for c in range(STEPS):
                    for f in range(FH):
                        i = (e * STEPS + c) * FH + f
                        act.wait_ge(s_gu, i + 1)
                        if not (isinstance(e, int) and e == 0 and c == 0):
                            act.wait_ge(s_hid, i - 1)
                        nc.scalar.activation(silu[:, f, :], pair_banks[f][:, 0, :], ACT.Silu).then_inc(s_silu, 1)

            expert(0)
            with act.Fori(1, EXPERTS) as e:
                expert(e)

        @block.vector
        def _(dve):
            steps = [0]

            def chained(instruction):
                steps[0] += 1
                instruction.then_inc(s_route, 1)
                dve.wait_ge(s_route, steps[0])

            for c in range(CHUNKS):
                norm.vector(dve, c)
            v = nc.vector
            logit, prob, rest, mark, sel1, sel2 = (small[n][:] for n in ("logit", "prob", "rest", "mark", "sel1", "sel2"))
            dve.wait_ge(s_logit, 1)
            dve.wait_ge(s_rank, EXPERTS)
            chained(v.tensor_tensor(logit, banks[2][:, 0:TILES * EXPERTS].rearrange("p (t e) -> p t e", t=TILES),
                                    per_tile(rb_sb[:]), ALU.add))
            chained(v.tensor_reduce(narrow["max"][:], logit, axis=AX.X, op=ALU.max))
            v.tensor_tensor(logit, logit, wide(narrow["max"][:]), ALU.subtract).then_inc(s_shift, 1)
            dve.wait_ge(s_prob, 1)
            chained(v.tensor_reduce(narrow["sum"][:], prob, axis=AX.X, op=ALU.add))
            chained(v.reciprocal(narrow["inv"][:], narrow["sum"][:]))
            chained(v.tensor_tensor(prob, prob, wide(narrow["inv"][:]), ALU.mult))
            chained(v.tensor_reduce(narrow["p1"][:], prob, axis=AX.X, op=ALU.max))
            chained(v.tensor_tensor(mark, prob, wide(narrow["p1"][:]), ALU.is_equal))
            chained(v.tensor_tensor(mark, mark, per_tile(rank[:]), ALU.mult))
            chained(v.tensor_reduce(narrow["first"][:], mark, axis=AX.X, op=ALU.max))
            chained(v.tensor_tensor(sel1, mark, wide(narrow["first"][:]), ALU.is_equal))
            chained(v.scalar_tensor_tensor(out=rest, in0=sel1, scalar=-2.0, in1=prob, op0=ALU.mult, op1=ALU.add))
            chained(v.tensor_reduce(narrow["p2"][:], rest, axis=AX.X, op=ALU.max))
            chained(v.tensor_tensor(mark, rest, wide(narrow["p2"][:]), ALU.is_equal))
            chained(v.tensor_tensor(mark, mark, per_tile(rank[:]), ALU.mult))
            chained(v.tensor_reduce(narrow["first"][:], mark, axis=AX.X, op=ALU.max))
            chained(v.tensor_tensor(sel2, mark, wide(narrow["first"][:]), ALU.is_equal))
            chained(v.tensor_tensor(narrow["den"][:], narrow["p1"][:], narrow["p2"][:], ALU.add))
            chained(v.reciprocal(narrow["iden"][:], narrow["den"][:]))
            chained(v.tensor_tensor(sel1, sel1, sel2, ALU.add))
            chained(v.tensor_tensor(sel1, sel1, prob, ALU.mult))
            v.tensor_tensor(combine[:], sel1, wide(narrow["iden"][:]), ALU.mult).then_inc(s_combine, 1)
            dve.wait_ge(s_combine, 1)

            def product(e, c, f):
                i = (e * STEPS + c) * FH + f
                dve.wait_ge(s_silu, i + 1)
                if not (isinstance(e, int) and e == 0 and c < 2):
                    dve.wait_ge(s_down, e * STEPS + c - 1)
                v.tensor_tensor(hidden[:, c % 2, f, :], silu[:, f, :], pair_banks[f][:, 1, :], ALU.mult).then_inc(s_hid, 1)

            def accumulate(e, c):
                k = e * STEPS + c
                dve.wait_ge(s_down, k + 1)
                if not (isinstance(e, int) and e == 0):
                    dve.wait_ge(s_acc, TPC * (k - 3))
                for t in range(TPC):
                    tile = TPC * c + t
                    v.scalar_tensor_tensor(out=x[:, tile, :], in0=banks[c % 2][:, P * t:P * (t + 1)],
                                           scalar=combine[:, tile, bass.ds(e, 1)], in1=x[:, tile, :],
                                           op0=ALU.mult, op1=ALU.add).then_inc(s_acc, 1)

            def expert(e, first=False):
                for c in range(STEPS):
                    for f in range(FH):
                        product(e, c, f)
                    if c:
                        accumulate(e, c - 1)
                    elif not first:
                        accumulate(e - 1, STEPS - 1)

            expert(0, first=True)
            expert(1)
            with dve.Fori(2, EXPERTS) as e:
                expert(e)
            accumulate(EXPERTS - 1, STEPS - 1)


def second_attention(nc, ctx, sb, sem, b, banks, pair_banks, arena, probs, work, wqk_sb, wv_sb, wo_sb, g_half, s_w1):
    x, xnT = b["x"], b["xnT"]
    qk_op = arena[:, :].rearrange("r (s h n) -> r s h n", s=2, h=H1)
    parts = b["parts"]
    tri, means, one = sb("tri", [P, P]), sb("means", [P, P]), sb("one", [P, 1])
    v_sb = sb("v_sb", [P, KT, P])
    y_sb = sb("y_sb", [P, PAIRS, SEQ])
    rest, y_square, log_mean, rstd = (work[:, CH * n:CH * (n + 1)] for n in range(4))

    norm = Norm(nc, ctx, "n2", b)
    s_masks, s_g = sem("s_masks"), sem("s_g")
    s_proj, s_hi, s_rest, s_mid, s_lo = (sem(f"s_b_{n}") for n in ("proj", "hi", "rest", "mid", "lo"))
    s_copied = [sem("s_b_copied0"), sem("s_b_copied1")]
    s_sc, s_square, s_weight, s_sum = (sem(f"s_a_{n}") for n in ("score", "square", "weight", "sum"))
    s_v, s_vcopy = sem("s_a_v"), sem("s_a_vcopy")
    s_ysq, s_mean, s_log, s_rstd, s_y = (sem(f"s_a_{n}") for n in ("ysq", "mean", "log", "rstd", "y"))
    s_o, s_added = sem("s_a_o"), sem("s_a_added")

    ITEMS = [(c, kt) for c in range(2) for kt in range(TPC * (c + 1))]
    N = len(ITEMS)
    LAG = 2
    LAST = {0: TPC, 1: N}
    COPIES = 16 * len(PRODUCTS1)
    OPERANDS = 4

    def first_column(c, kt):
        return max(0, kt - TPC * c) * P

    with nc.Block() as block:
        @block.gpsimd
        def _(pool):
            nc.gpsimd.memset(tri[:], 1.0).then_inc(s_masks, 1)
            nc.gpsimd.memset(means[:], 0.0).then_inc(s_masks, 1)
            nc.gpsimd.memset(one[:], 1.0).then_inc(s_masks, 1)
            pool.wait_ge(s_masks, 3)
            nc.gpsimd.affine_select(out=tri[:], in_=tri[:], compare_op=ALU.is_ge, fill=0.0, base=0,
                                    pattern=[[1, P]], channel_multiplier=-1).then_inc(s_masks, 1)
            pool.wait_ge(s_masks, 4)
            for h in range(2):
                nc.gpsimd.memset(means[DV1 * h:DV1 * (h + 1), DV1 * h:DV1 * (h + 1)], 1.0 / DV1).then_inc(s_masks, 1)
                pool.wait_ge(s_masks, 5 + h)
            pool.wait_ge(s_w1, 16 * 6)
            nc.gpsimd.tensor_scalar(g_half[:], g_half[:], 0.5, None, ALU.mult).then_inc(s_g, 1)

        @block.sync
        def _(sp):
            def copies(bt, half):
                if bt:
                    sp.wait_ge(s_sc, N * (PAIRS // 2) * (half + 1))
                for n in range(OPERANDS):
                    m = (bt * 2 + half) * OPERANDS + n
                    which, c = n // 2, n % 2
                    sp.wait_ge(s_lo, m + 1)
                    for i, product in enumerate(PRODUCTS1):
                        sp.dma_start(qk_op[DF * i:DF * (i + 1), which, HALF * half:HALF * (half + 1), CH * c:CH * (c + 1)],
                                     parts[:, m % 2, product[which], :]).then_inc(s_copied[m % 2], 16)

            for bt in range(BATCH):
                for half in range(2):
                    copies(bt, half)
            for s in s_copied:
                sp.wait_ge(s, COPIES * 2 * OPERANDS)

        @block.tensor
        def _(pe):
            def build(bt, half):
                for n in range(OPERANDS):
                    m = (bt * 2 + half) * OPERANDS + n
                    which, c = n // 2, n % 2
                    if m:
                        pe.wait_ge(s_rest, m)
                    if bt and n == 0:
                        pe.wait_ge(s_vcopy, 2 * (PAIRS // 2) * (half + 1))
                    nc.tensor.matmul(banks[2][:, :], wqk_sb[:, which, half, :],
                                     xnT[:, SEQ * bt + CH * c:SEQ * bt + CH * (c + 1)], start=True, stop=True).then_inc(s_proj, 1)

            def ready(bt, half):
                done = bt * 2 + half + 1
                for s in s_copied:
                    pe.wait_ge(s, COPIES * (OPERANDS // 2) * done)

            def values(g, bt, r):
                if not (isinstance(g, int) and g == 0 and r == 0):
                    pe.wait_ge(s_vcopy, 2 * g + r)
                for k in range(4):
                    col = SEQ * bt + P * (4 * r + k)
                    mm = nc.tensor.matmul(banks[2][:, P * k:P * (k + 1)], xnT[:, col:col + P],
                                          wv_sb[:, bass.ds((g - PAIRS * bt) * P, P)], start=True, stop=True)
                mm.then_inc(s_v, 1)

            def scores(g, bt, i):
                c, kt = ITEMS[i]
                q0 = first_column(c, kt)
                if not (isinstance(g, int) and g == 0 and i < 2):
                    pe.wait_ge(s_square, N * g + i - 1)
                for h in range(2):
                    head = (g - PAIRS * bt) * 2 + h
                    mm = nc.tensor.matmul(pair_banks[i % 2][:, h, q0:CH], qk_op[:, 1, head, P * kt:P * (kt + 1)],
                                          qk_op[:, 0, head, CH * c + q0:CH * (c + 1)], start=True, stop=True)
                mm.then_inc(s_sc, 1)

            def sums(g, i):
                c, kt = ITEMS[i]
                q0 = first_column(c, kt)
                pe.wait_ge(s_weight, N * g + i + 1)
                if kt == 0 and not (isinstance(g, int) and g == 0):
                    pe.wait_ge(s_y, 2 * g + c - 1)
                if c == 0 and kt == 0:
                    pe.wait_ge(s_vcopy, 2 * g + 1)
                if kt == TPC:
                    pe.wait_ge(s_vcopy, 2 * g + 2)
                for h in range(2):
                    mm = nc.tensor.matmul(banks[c][DV1 * h:DV1 * (h + 1), q0:CH], v_sb[:, kt, DV1 * h:DV1 * (h + 1)],
                                          probs[:, i % 4, h, q0:CH], start=(kt == 0), stop=(i + 1 == LAST[c]))
                mm.then_inc(s_sum, 1)

            def mean(q):
                pe.wait_ge(s_ysq, q + 1)
                if not (isinstance(q, int) and q == 0):
                    pe.wait_ge(s_log, q)
                nc.tensor.matmul(banks[3][:, :], means[:], y_square, start=True, stop=True).then_inc(s_mean, 1)

            def pair(g, bt, first=False):
                values(g, bt, 0)
                for i in range(N):
                    scores(g, bt, i)
                    if i >= LAG:
                        sums(g, i - LAG)
                    elif not first:
                        sums(g - 1, N + i - LAG)
                    if i == LAG - 1:
                        values(g, bt, 1)
                    if i == 4 and not first:
                        mean(2 * g - 1)
                    if i == 8:
                        mean(2 * g)

            def project(bt):
                pe.wait_ge(s_y, 2 * PAIRS * (bt + 1))
                for r in range(2):
                    for t in range(4):
                        for p in range(PAIRS):
                            col = P * (4 * r + t)
                            mm = nc.tensor.matmul(banks[2 + r][:, P * t:P * (t + 1)], y_sb[:, p, col:col + P],
                                                  wo_sb[:, p, :], start=(p == 0), stop=(p == PAIRS - 1))
                    mm.then_inc(s_o, 1)

            pe.wait_ge(s_masks, 6)
            pe.wait_ge(s_w1, 16 * 6)
            for c in range(CHUNKS):
                norm.tensor(pe, c, banks)
            pe.wait_ge(norm.done, CHUNKS)
            build(0, 0)
            build(0, 1)
            pe.wait_ge(s_rest, 2 * OPERANDS)
            ready(0, 0)
            pair(0, 0, first=True)
            with pe.Fori(1, PAIRS // 2) as g:
                pair(g, 0)
            build(1, 0)
            pe.wait_ge(s_rest, 3 * OPERANDS)
            with pe.Fori(PAIRS // 2, PAIRS) as g:
                pair(g, 0)
            build(1, 1)
            pe.wait_ge(s_rest, 4 * OPERANDS)
            for i in range(N - LAG, N):
                sums(PAIRS - 1, i)
            mean(2 * PAIRS - 1)
            project(0)
            pe.wait_ge(s_added, 2)
            ready(1, 0)
            ready(1, 1)
            pair(PAIRS, 1, first=True)
            with pe.Fori(PAIRS + 1, 2 * PAIRS) as g:
                pair(g, 1)
            for i in range(N - LAG, N):
                sums(2 * PAIRS - 1, i)
            mean(4 * PAIRS - 1)
            project(1)

        @block.scalar
        def _(act):
            def build(bt, half):
                for n in range(OPERANDS):
                    m = (bt * 2 + half) * OPERANDS + n
                    act.wait_ge(s_proj, m + 1)
                    if m >= 2:
                        act.wait_ge(s_copied[m % 2], COPIES * (m // 2))
                    nc.scalar.activation(parts[:, m % 2, 0, :], banks[2][:, :], ACT.Copy).then_inc(s_hi, 1)
                    act.wait_ge(s_rest, m + 1)
                    nc.scalar.activation(parts[:, m % 2, 1, :], rest, ACT.Copy).then_inc(s_mid, 1)

            def square(g, i):
                c, kt = ITEMS[i]
                q0 = first_column(c, kt)
                act.wait_ge(s_sc, N * g + i + 1)
                if not (isinstance(g, int) and g == 0 and i < 4):
                    act.wait_ge(s_sum, N * g + i - 3)
                nc.scalar.activation(probs[:, i % 4, :, q0:CH], pair_banks[i % 2][:, :, q0:CH], ACT.Square,
                                     bias=1.0, scale=0.25).then_inc(s_square, 1)

            def result_square(g, c):
                q = 2 * g + c
                act.wait_ge(s_sum, N * g + LAST[c])
                if not (isinstance(g, int) and g == 0 and c == 0):
                    act.wait_ge(s_mean, q)
                nc.scalar.activation(y_square, banks[c][:, :], ACT.Square, scale=0.5).then_inc(s_ysq, 1)

            def result_rstd(q):
                act.wait_ge(s_mean, q + 1)
                if not (isinstance(q, int) and q == 0):
                    act.wait_ge(s_rstd, q)
                    act.wait_ge(s_y, q)
                nc.scalar.activation(log_mean, banks[3][:, :], ACT.Ln, bias=b["eps"][:, 0:1]).then_inc(s_log, 1)
                act.wait_ge(s_log, q + 1)
                nc.scalar.activation(rstd, log_mean, ACT.Exp, scale=-0.5).then_inc(s_rstd, 1)

            def pair(g, first=False):
                nc.scalar.preload_act_table_set(LN_EXP)
                for i in range(N):
                    if i == 3 and not first:
                        result_square(g - 1, 1)
                    if i == 5 and not first:
                        result_rstd(2 * g - 1)
                    if i == 7:
                        result_square(g, 0)
                    if i == 9:
                        result_rstd(2 * g)
                    square(g, i)

            for c in range(CHUNKS):
                norm.scalar_rstd(act, c)
                norm.scalar_copy(act, c, banks)
            act.wait_ge(s_masks, 3)
            build(0, 0)
            build(0, 1)
            pair(0, first=True)
            with act.Fori(1, PAIRS // 2) as g:
                pair(g)
            build(1, 0)
            with act.Fori(PAIRS // 2, PAIRS) as g:
                pair(g)
            build(1, 1)
            result_square(PAIRS - 1, 1)
            result_rstd(2 * PAIRS - 1)
            pair(PAIRS, first=True)
            with act.Fori(PAIRS + 1, 2 * PAIRS) as g:
                pair(g)
            result_square(2 * PAIRS - 1, 1)
            result_rstd(4 * PAIRS - 1)

        @block.vector
        def _(dve):
            def build(bt, half):
                for n in range(OPERANDS):
                    m = (bt * 2 + half) * OPERANDS + n
                    dve.wait_ge(s_hi, m + 1)
                    if m:
                        dve.wait_ge(s_lo, m)
                    nc.vector.tensor_tensor(rest, banks[2][:, :], parts[:, m % 2, 0, :], ALU.subtract).then_inc(s_rest, 1)
                    dve.wait_ge(s_mid, m + 1)
                    nc.vector.tensor_tensor(parts[:, m % 2, 2, :], rest, parts[:, m % 2, 1, :], ALU.subtract).then_inc(s_lo, 1)

            def copy_values(g, r):
                dve.wait_ge(s_v, 2 * g + r + 1)
                if not (isinstance(g, int) and g == 0):
                    dve.wait_ge(s_sum, N * g - (N - 8) * (1 - r))
                nc.vector.tensor_copy(v_sb[:, 4 * r:4 * r + 4, :], banks[2][:, :].rearrange("p (k n) -> p k n", k=4)).then_inc(s_vcopy, 1)

            def weights(g, i):
                c, kt = ITEMS[i]
                q0 = first_column(c, kt)
                tile = probs[:, i % 4, :, :]
                dve.wait_ge(s_square, N * g + i + 1)
                if kt >= TPC * c:
                    diagonal = tile[:, :, q0:q0 + P]
                    mm = nc.vector.scalar_tensor_tensor(out=diagonal, in0=diagonal, scalar=1.0,
                                                        in1=tri[:].unsqueeze(1).to_broadcast([P, 2, P]),
                                                        op0=ALU.add, op1=ALU.mult)
                    q0 += P
                if q0 < CH:
                    mm = nc.vector.tensor_scalar(tile[:, :, q0:CH], tile[:, :, q0:CH], 1.0, None, ALU.add)
                mm.then_inc(s_weight, 1)

            def normalise(g, bt, c):
                q = 2 * g + c
                dve.wait_ge(s_rstd, q + 1)
                nc.vector.scalar_tensor_tensor(out=y_sb[:, g - PAIRS * bt, CH * c:CH * (c + 1)], in0=banks[c][:, :],
                                               scalar=g_half[:, 0:1], in1=rstd, op0=ALU.mult, op1=ALU.mult).then_inc(s_y, 1)

            def pair(g, bt, first=False):
                copy_values(g, 0)
                for i in range(N):
                    if i == 5 and not first:
                        normalise(g - 1, bt, 1)
                    if i == 9:
                        normalise(g, bt, 0)
                    weights(g, i)
                    if i == 2:
                        copy_values(g, 1)

            def add(bt):
                for r in range(2):
                    dve.wait_ge(s_o, 2 * bt + r + 1)
                    tiles = x[:, KT * bt + 4 * r:KT * bt + 4 * r + 4, :]
                    nc.vector.tensor_tensor(tiles, banks[2 + r][:, :].rearrange("p (t d) -> p t d", t=4), tiles, ALU.add).then_inc(s_added, 1)

            for c in range(CHUNKS):
                norm.vector(dve, c)
            dve.wait_ge(s_masks, 4)
            dve.wait_ge(s_g, 1)
            build(0, 0)
            build(0, 1)
            pair(0, 0, first=True)
            with dve.Fori(1, PAIRS // 2) as g:
                pair(g, 0)
            build(1, 0)
            with dve.Fori(PAIRS // 2, PAIRS) as g:
                pair(g, 0)
            build(1, 1)
            normalise(PAIRS - 1, 0, 1)
            add(0)
            pair(PAIRS, 1, first=True)
            with dve.Fori(PAIRS + 1, 2 * PAIRS) as g:
                pair(g, 1)
            normalise(2 * PAIRS - 1, 1, 1)
            add(1)


def feed_forward(nc, ctx, sb, sem, b, banks, pair_banks, work, ints, s_w2, out):
    x, xnT = b["x"], b["xnT"]
    scaled = sb("scaled", [P, 3, HID])
    hidden = work[:, 0:6 * CH].rearrange("p (s j n) -> p s j n", s=2, j=HT)
    silu = work[:, 6 * CH:8 * CH].rearrange("p (s n) -> p s n", s=2)
    norm = Norm(nc, ctx, "n3", b)
    s_scaled, s_gu, s_silu, s_hid, s_down, s_sum = (sem(f"s_f_{n}") for n in ("scaled", "gu", "silu", "hid", "down", "sum"))
    s_out = sem("s_out")
    out_dram = out.rearrange("(t p) d -> p t d", p=P)

    with nc.Block() as block:
        @block.sync
        def _(sp):
            for c in range(CHUNKS):
                sp.wait_ge(s_sum, c + 1)
                sp.dma_start(out_dram[:, TPC * c:TPC * (c + 1), :], x[:, TPC * c:TPC * (c + 1), :]).then_inc(s_out, 16)
            sp.wait_ge(s_out, 16 * CHUNKS)

        @block.tensor
        def _(pe):
            def gate_up(c, j):
                i = HT * c + j
                if i >= 2:
                    pe.wait_ge(s_hid, i - 1)
                for m in range(2):
                    mm = nc.tensor.matmul(pair_banks[i % 2][:, m, :], scaled[:, m, P * j:P * (j + 1)],
                                          xnT[:, CH * c:CH * (c + 1)], start=True, stop=True)
                mm.then_inc(s_gu, 1)

            def down(c):
                pe.wait_ge(s_hid, HT * (c + 1))
                if c >= 2:
                    pe.wait_ge(s_sum, c - 1)
                for t in range(TPC):
                    for j in range(HT):
                        mm = nc.tensor.matmul(banks[2 + c % 2][:, P * t:P * (t + 1)], hidden[:, c % 2, j, P * t:P * (t + 1)],
                                              scaled[:, 2, P * j:P * (j + 1)], start=(j == 0), stop=(j == HT - 1))
                mm.then_inc(s_down, 1)

            for c in range(CHUNKS):
                norm.tensor(pe, c, banks)
            pe.wait_ge(s_scaled, 3)
            for c in range(CHUNKS):
                pe.wait_ge(norm.done, c + 1)
                for j in range(HT):
                    gate_up(c, j)
                    if j == 0 and c:
                        down(c - 1)
            down(CHUNKS - 1)

        @block.scalar
        def _(act):
            nc.scalar.preload_act_table_set(LN_EXP)
            for c in range(CHUNKS):
                norm.scalar_rstd(act, c)
                norm.scalar_copy(act, c, banks)
            for i in range(HT * CHUNKS):
                act.wait_ge(s_gu, i + 1)
                if i >= 2:
                    act.wait_ge(s_hid, i - 1)
                nc.scalar.activation(silu[:, i % 2, :], pair_banks[i % 2][:, 0, :], ACT.Silu).then_inc(s_silu, 1)

        @block.vector
        def _(dve):
            dve.wait_ge(s_w2, 48)
            for m in range(3):
                nc.vector.tensor_scalar(scaled[:, m, :], ints[:, m, :], QSCALE, None, ALU.mult).then_inc(s_scaled, 1)
            for c in range(CHUNKS):
                norm.vector(dve, c)

            def add(c):
                dve.wait_ge(s_down, c + 1)
                tiles = x[:, TPC * c:TPC * (c + 1), :]
                nc.vector.tensor_tensor(tiles, banks[2 + c % 2][:, :].rearrange("p (t d) -> p t d", t=TPC), tiles,
                                        ALU.add).then_inc(s_sum, 1)

            for c in range(CHUNKS):
                for j in range(HT):
                    i = HT * c + j
                    dve.wait_ge(s_silu, i + 1)
                    if c >= 2:
                        dve.wait_ge(s_down, c - 1)
                    nc.vector.tensor_tensor(hidden[:, c % 2, j, :], silu[:, i % 2, :], pair_banks[i % 2][:, 1, :],
                                            ALU.mult).then_inc(s_hid, 1)
                if c:
                    add(c - 1)
            add(CHUNKS - 1)


def kernel(L0_attn_x, L0_attn_Wq, L0_attn_Wk, L0_attn_Wv, L0_ffn_router_w, L0_ffn_router_b, L0_ffn_gate_w,
           L0_ffn_up_w, L0_ffn_down_w, L1_attn_Wq, L1_attn_Wk, L1_attn_Wv, L1_attn_Wo, L1_attn_g_weight,
           L1_ffn_w_gate, L1_ffn_w_up, L1_ffn_w_down):
    import concourse.bacc as bacc
    from concourse.bass_utils import run_bass_kernel_spmd

    by_feature0 = L0_attn_Wq.reshape(H0, DH0, P).transpose(2, 1, 0).reshape(P, P)
    by_feature1 = [w.reshape(2, HALF, DF, P).transpose(3, 0, 2, 1).reshape(P, 2, P) for w in (L1_attn_Wq, L1_attn_Wk)]
    arrays = {
        "x_in": L0_attn_x.reshape(TOKENS, P), "wq0": by_feature0, "wk0": L0_attn_Wk.T, "wv0": L0_attn_Wv.T,
        "rw": L0_ffn_router_w.T, "rb": L0_ffn_router_b.reshape(1, EXPERTS),
        "gate_w": L0_ffn_gate_w, "up_w": L0_ffn_up_w, "down_w": L0_ffn_down_w.reshape(EXPERTS, FH, P, P),
        "wq1": by_feature1[0], "wk1": by_feature1[1], "wv1": L1_attn_Wv.T,
        "wo1": L1_attn_Wo.T.reshape(PAIRS, P, P).transpose(1, 0, 2), "g1": L1_attn_g_weight.reshape(DV1, 1),
        "wg2": L1_ffn_w_gate.T, "wu2": L1_ffn_w_up.T, "wd2": L1_ffn_w_down.T.reshape(HT, P, P).transpose(1, 0, 2),
    }
    arrays = {name: np.ascontiguousarray(a) for name, a in arrays.items()}
    nc = bacc.Bacc("TRN2", target_bir_lowering=False, num_devices=1)
    aps = [nc.dram_tensor(name, a.shape, mybir.dt.from_np(a.dtype), kind="ExternalInput").ap() for name, a in arrays.items()]
    aps.append(nc.dram_tensor("out", (TOKENS, P), F32, kind="ExternalOutput").ap())
    build(nc, *aps)
    result = run_bass_kernel_spmd(nc, [arrays], core_ids=[0])
    return result.results[0]["out"].reshape(BATCH, SEQ, P)
```

```python
from contextlib import ExitStack

import numpy as np
import concourse.bass as bass
from concourse import mybir

F32, BF16, I32 = mybir.dt.float32, mybir.dt.bfloat16, mybir.dt.int32
ALU = mybir.AluOpType
ACT = mybir.ActivationFunctionType
AX = mybir.AxisListType

P = 128
BATCH, SEQ = 2, 1024
TOKENS = BATCH * SEQ
TILES = TOKENS // P
CH = 512
CHUNKS = TOKENS // CH
TPC = CH // P
KT = SEQ // P
LN_EPS = 1e-5
LN_EXP = "natural_log_exp_and_others"

H0, DH0 = 16, 8
HG = 4
GROUPS = H0 // HG
UNITS = CHUNKS * GROUPS
STACK = 96
SCALE0 = float(1.0 / np.sqrt(DH0))
PRODUCTS0 = [(n // 3, n % 3) for n in range(9)]
MROW = DH0 * len(PRODUCTS0)

EXPERTS, DFF0 = 8, 256
FH = DFF0 // P

H1, DF, DV1 = 16, 16, 64
PAIRS = H1 // 2
HALF = H1 // 2
PRODUCTS1 = [(0, 0), (0, 1), (1, 0), (0, 2), (2, 0), (1, 1)]
RMS_EPS = 1e-5

HID = 384
HT = HID // P
QSCALE = float(np.float32(1.0 / 127.0))


class Norm:

    def __init__(self, nc, ctx, tag, buf):
        self.nc, self.b = nc, buf
        sem = lambda n: ctx.enter_context(nc.semaphore(f"{tag}_{n}"))
        self.stats, self.moments, self.logv, self.rstd = sem("stats"), sem("moments"), sem("logv"), sem("rstd")
        self.normed, self.turned, self.done = sem("normed"), sem("turned"), sem("xnT")

    def vector(self, dve, c):
        nc, b = self.nc, self.b
        for t in range(TPC * c, TPC * (c + 1)):
            nc.vector.bn_stats(b["bn"][:, t, :], b["x"][:, t, :]).then_inc(self.stats, 1)
        dve.wait_ge(self.stats, TPC * (c + 1))
        for t in range(TPC * c, TPC * (c + 1)):
            nc.vector.bn_aggr(b["mv"][:, t, :], b["bn"][:, t, :]).then_inc(self.moments, 1)
        dve.wait_ge(self.rstd, c + 1)
        if c >= 2:
            dve.wait_ge(self.turned, c - 1)
        for t in range(TPC * c, TPC * (c + 1)):
            nc.vector.tensor_scalar(b["xn"][:, t % (2 * TPC), :], b["x"][:, t, :], b["mv"][:, t, 0:1],
                                    b["rstd"][:, t:t + 1], ALU.subtract, ALU.mult).then_inc(self.normed, 1)

    def scalar_rstd(self, act, c):
        nc, b = self.nc, self.b
        s = slice(TPC * c, TPC * (c + 1))
        act.wait_ge(self.moments, TPC * (c + 1))
        nc.scalar.activation(b["logv"][:, s], b["mv"][:, s, 1], ACT.Ln, bias=b["eps"][:, 0:1]).then_inc(self.logv, 1)
        act.wait_ge(self.logv, c + 1)
        nc.scalar.activation(b["rstd"][:, s], b["logv"][:, s], ACT.Exp, scale=-0.5).then_inc(self.rstd, 1)

    def tensor(self, pe, c, banks):
        nc, b = self.nc, self.b
        if c >= 2:
            pe.wait_ge(self.done, c - 1)
        for k in range(TPC):
            t = TPC * c + k
            pe.wait_ge(self.normed, t + 1)
            mm = nc.tensor.transpose(banks[c % 2][:, P * k:P * (k + 1)], b["xn"][:, t % (2 * TPC), :], b["ident"][:])
        mm.then_inc(self.turned, 1)

    def scalar_copy(self, act, c, banks):
        act.wait_ge(self.turned, c + 1)
        self.nc.scalar.activation(self.b["xnT"][:, CH * c:CH * (c + 1)], banks[c % 2][:, :],
                                  ACT.Copy).then_inc(self.done, 1)


def build(nc, x_in, wq0, wk0, wv0, marks0, rw, rb, gate_w, up_w, down_w, wq1, wk1, wv1, wo1, g1, wg2, wu2, wd2, out):
    ctx = ExitStack()
    with ctx:
        def sb(name, shape, dt=F32):
            return ctx.enter_context(nc.sbuf_tensor(name, shape, dt))

        def sem(name):
            return ctx.enter_context(nc.semaphore(name))

        b = {
            "x": sb("x", [P, TILES, P]), "xnT": sb("xnT", [P, TOKENS]), "xn": sb("xn", [P, 2 * TPC, P]),
            "bn": sb("bn", [P, TILES, 6]), "mv": sb("mv", [P, TILES, 2]), "logv": sb("logv", [P, TILES]),
            "rstd": sb("rstd", [P, TILES]), "eps": sb("eps", [P, 1]), "ident": sb("ident", [P, P]),
            "parts": sb("parts", [P, 2, 3, CH], BF16),
        }
        x, xnT = b["x"], b["xnT"]
        ident, ident16 = b["ident"], sb("ident16", [P, P], BF16)
        banks = [ctx.enter_context(nc.psum_tensor(f"bank{i}", [P, CH], F32)) for i in range(4)]
        pair_banks = [ctx.enter_context(nc.psum_tensor(f"pair{i}", [P, 2, CH], F32)) for i in range(2)]

        arena = sb("arena", [STACK, UNITS * HG * CH], BF16)
        w_up = sb("w_up", [P, 2, 2, DFF0])
        w_down = sb("w_down", [P, 2, FH, P])
        wv1_sb, wo1_sb = sb("wv1_sb", [P, H1 * DV1]), sb("wo1_sb", [P, PAIRS, P])
        wqk1_sb = sb("wqk1_sb", [P, 2, 2, P])
        g_half = sb("g_half", [P, 1])
        ints = sb("ints", [P, 3, HID], I32)
        probs = sb("probs", [P, 4, 2, CH])
        work = sb("work", [P, 8 * CH])

        s_x = [sem(f"s_x{c}") for c in range(CHUNKS)]
        s_w0, s_router, s_w1, s_w2 = sem("s_w0"), sem("s_router"), sem("s_w1"), sem("s_w2")
        s_exp_w = [sem("s_exp_w0"), sem("s_exp_w1")]
        x_dram = x_in.rearrange("(t p) d -> p t d", p=P)

        first_attention(nc, ctx, sb, sem, b, banks, pair_banks, arena, probs, work, ident16,
                        s_x, s_w0, x_dram, wq0, wk0, wv0, marks0)
        experts(nc, ctx, sb, sem, b, banks, pair_banks, work, w_up, w_down, s_exp_w, s_router,
                rw, rb, gate_w, up_w, down_w,
                [(wqk1_sb[:, 0, :, :], wq1, s_w1), (wqk1_sb[:, 1, :, :], wk1, s_w1), (wv1_sb[:], wv1, s_w1),
                 (wo1_sb[:], wo1, s_w1), (g_half[0:DV1, :], g1, s_w1), (g_half[DV1:P, :], g1, s_w1),
                 (ints[:, 0, :], wg2, s_w2), (ints[:, 1, :], wu2, s_w2), (ints[:, 2, :], wd2.rearrange("p j d -> p (j d)"), s_w2)])
        second_attention(nc, ctx, sb, sem, b, banks, pair_banks, arena, probs, work, wqk1_sb, wv1_sb, wo1_sb, g_half, s_w1)
        feed_forward(nc, ctx, sb, sem, b, banks, pair_banks, work, ints, s_w2, out)


def first_attention(nc, ctx, sb, sem, b, banks, pair_banks, arena, probs, work, ident16,
                    s_x, s_w0, x_dram, wq0, wk0, wv0, marks0):
    x, xnT, ident = b["x"], b["xnT"], b["ident"]
    q_op = arena[:, :].rearrange("r (u h n) -> r u h n", u=UNITS, h=HG)
    q_rows = arena[:, :].rearrange("r (c m) -> r c m", c=CHUNKS)
    k_op = sb("k_op", [STACK, TOKENS], BF16)
    v_op = sb("v_op", [P, TILES, 32])
    wq_sb, wk_sb, wv_sb = sb("wq0_sb", [P, P]), sb("wk0_sb", [P, STACK]), sb("wv0_sb", [P, DH0])
    k_marks = sb("k_marks", [STACK, 3])
    q_parts = b["parts"]
    k_high, k_middle = (sb(f"k_{n}", [STACK, CH], BF16) for n in ("high", "middle"))
    q_rest = work[:, 0:CH]
    k_rest = work[0:STACK, CH:2 * CH]
    tops = sb("tops", [P, UNITS, TPC, HG])
    zero = sb("zero", [P, TPC, HG])
    neg, neg_rest = sb("neg", [P, TPC, HG]), sb("neg_rest", [P, TPC, HG])
    neg_parts = sb("neg_parts", [P, TPC, 3, HG], BF16)
    neg_t = sb("neg_t", [3 * HG, CH], BF16)
    pv_sb = work[:, 2 * CH:3 * CH]
    recip = sb("recip", [P, TPC, HG])
    ratio = work[:, 3 * CH:4 * CH].rearrange("p (t h d) -> p t h d", t=TPC, h=HG)[:, :, :, 0:DH0]

    norm = Norm(nc, ctx, "n0", b)
    s_zeroed, s_const = sem("s_zeroed"), sem("s_const")
    s_qproj, s_qhi, s_qrest, s_qmid, s_qlo = (sem(f"s_q_{n}") for n in ("proj", "hi", "rest", "mid", "lo"))
    s_kproj, s_khi, s_krest, s_kmid, s_k = (sem(f"s_k_{n}") for n in ("proj", "hi", "rest", "mid", "op"))
    s_copied = [sem("s_copied0"), sem("s_copied1")]
    COPIES = 16 * len(PRODUCTS0)
    s_vproj, s_v = sem("s_vproj"), sem("s_v")

    s_mx, s_red = sem("s_mx"), sem("s_red")
    s_neg, s_nhi, s_nrest, s_nmid, s_nparts = (sem(f"s_n_{n}") for n in ("neg", "hi", "rest", "mid", "parts"))
    s_nt, s_ncopied, s_ndma = sem("s_nt"), sem("s_ncopied"), sem("s_ndma")
    s_sc, s_exp, s_pv, s_pvcopy = sem("s_sc"), sem("s_exp"), sem("s_pv"), sem("s_pvcopy")
    s_ot, s_recip, s_ratio, s_added = sem("s_ot"), sem("s_recip"), sem("s_ratio"), sem("s_added")
    neg_bank = banks[3][:, :].bitcast(BF16)

    with nc.Block() as block:
        MAXES = TPC * HG
        PROJECT_K, PROJECT_Q = 3, 6
        K_HIGH, Q_HIGH, K_MIDDLE = 5, 9, 11
        EARLY = 4
        EXPS = HG * KT

        @block.tensor
        def _(pe):
            def project_k(c):
                pe.wait_ge(norm.done, c + 1)
                if c:
                    pe.wait_ge(s_krest, c)
                nc.tensor.matmul(banks[3][0:STACK, :], wk_sb[:], xnT[:, CH * c:CH * (c + 1)],
                                 start=True, stop=True).then_inc(s_kproj, 1)

            def project_q_v(c):
                if c:
                    pe.wait_ge(s_qrest, c)
                nc.tensor.matmul(banks[2][:, :], wq_sb[:], xnT[:, CH * c:CH * (c + 1)], start=True, stop=True).then_inc(s_qproj, 1)
                for k in range(TPC):
                    mm = nc.tensor.matmul(banks[c % 2][:, DH0 * k:DH0 * (k + 1)],
                                          xnT[:, CH * c + P * k:CH * c + P * (k + 1)], wv_sb[:], start=True, stop=True)
                mm.then_inc(s_vproj, 1)

            def maximum(u, i, half, bt):
                t, h = i // HG, i % HG
                if half == 0 and not (isinstance(u, int) and u == 0 and i < 2):
                    pe.wait_ge(s_red, u * MAXES + i - 1)
                mm = nc.tensor.matmul(pair_banks[i % 2][:, half, :], q_op[:, u, h, P * t:P * (t + 1)],
                                      k_op[:, bt * SEQ + half * CH:bt * SEQ + (half + 1) * CH], start=True, stop=True)
                if half:
                    mm.then_inc(s_mx, 1)

            def scores(u, kt, h, bt):
                if not (isinstance(u, int) and u == 0 and kt == 0 and h < 2):
                    pe.wait_ge(s_exp, u * EXPS + HG * kt + h - 1)
                nc.tensor.matmul(banks[h % 2][:, :], k_op[:, bt * SEQ + P * kt:bt * SEQ + P * (kt + 1)],
                                 q_op[:, u, h, :], start=True, stop=True).then_inc(s_sc, 1)

            def values(u, kt, bt):
                pe.wait_ge(s_exp, u * EXPS + HG * (kt + 1))
                for h in range(HG):
                    mm = nc.tensor.matmul(banks[2][32 * h:32 * h + 32, :], v_op[:, bt * KT + kt, :],
                                          probs[:, 2 * (kt % 2) + h // 2, h % 2, :], start=(kt == 0), stop=(kt == KT - 1))
                mm.then_inc(s_pv, 1)

            def negated(u):
                pe.wait_ge(s_nparts, u + 1)
                if not (isinstance(u, int) and u <= 1):
                    pe.wait_ge(s_added, u - 1)
                for t in range(TPC):
                    mm = nc.tensor.transpose(neg_bank[0:3 * HG, P * t:P * (t + 1)],
                                             neg_parts[:, t, :, :].rearrange("p n h -> p (n h)"), ident16[:])
                mm.then_inc(s_nt, 1)

            def outputs(u, final=False):
                pe.wait_ge(s_pvcopy, u + 1)
                if final:
                    pe.wait_ge(s_added, u)
                else:
                    pe.wait_ge(s_ncopied, u + 2)
                for t in range(TPC):
                    mm = nc.tensor.transpose(banks[3][:, P * t:P * (t + 1)], pv_sb[:, P * t:P * (t + 1)], ident[:])
                mm.then_inc(s_ot, 1)

            def unit(u, bt, bt_1, bt_2, first=False):
                last_bt = bt - 1 if isinstance(u, int) and u == UNITS // 2 else bt

                def part_of_maximum(kt, n):
                    i = EARLY + 2 * kt + n // 2
                    if i < MAXES and bt_1 is not None:
                        maximum(u + 1, i, n % 2, bt_1)
                    elif i >= MAXES and bt_2 is not None:
                        maximum(u + 2, i - MAXES, n % 2, bt_2)

                for kt in range(KT):
                    if kt == 0:
                        pe.wait_ge(s_ndma, 16 * (u + 1))
                    for h in range(HG):
                        scores(u, kt, h, bt)
                        part_of_maximum(kt, h)
                        if h == 1:
                            if kt:
                                if kt == 1 and not first:
                                    pe.wait_ge(s_pvcopy, u)
                                values(u, kt - 1, bt)
                            elif not first:
                                values(u - 1, KT - 1, last_bt)
                    if kt == 2 and not first:
                        outputs(u - 1)
                    if kt == 6 and bt_1 is not None:
                        negated(u + 1)

            half = UNITS // 2
            pe.wait_ge(s_const, 3)
            for c in range(2):
                norm.tensor(pe, c, banks)
            pe.wait_ge(s_w0, 64)
            for c in range(2):
                project_k(c)
                project_q_v(c)
            for c in range(2, CHUNKS):
                pe.wait_ge(s_v, c - 1)
                norm.tensor(pe, c, banks)
            project_k(2)
            project_q_v(2)
            pe.wait_ge(s_k, 2)
            pe.wait_ge(s_copied[0], COPIES)
            for i in range(MAXES + EARLY):
                if i == PROJECT_K:
                    project_k(3)
                if i == PROJECT_Q:
                    project_q_v(3)
                for n in range(2):
                    maximum(i // MAXES, i % MAXES, n, 0)
                if i == MAXES - 1:
                    pe.wait_ge(s_krest, CHUNKS)
                    pe.wait_ge(s_qrest, CHUNKS)
                    pe.wait_ge(s_v, CHUNKS)
            negated(0)
            unit(0, 0, 0, 0, first=True)
            pe.wait_ge(s_k, CHUNKS)
            for s in s_copied:
                pe.wait_ge(s, COPIES * CHUNKS // 2)
            with pe.Fori(1, half - 2) as u:
                unit(u, 0, 0, 0)
            unit(half - 2, 0, 0, 1)
            unit(half - 1, 0, 1, 1)
            unit(half, 1, 1, 1)
            with pe.Fori(half + 1, UNITS - 2) as u:
                unit(u, 1, 1, 1)
            unit(UNITS - 2, 1, 1, None)
            unit(UNITS - 1, 1, None, None)
            values(UNITS - 1, KT - 1, 1)
            outputs(UNITS - 1, final=True)

        @block.scalar
        def _(act):
            def split(c):
                act.wait_ge(s_kproj, c + 1)
                if c:
                    act.wait_ge(s_krest, c)
                nc.scalar.activation(k_high[:], banks[3][0:STACK, :], ACT.Identity, bias=k_marks[:, 2:3]).then_inc(s_khi, 1)
                if c >= 2:
                    act.wait_ge(s_copied[c % 2], COPIES * (c // 2))
                act.wait_ge(s_qproj, c + 1)
                nc.scalar.activation(q_parts[:, c % 2, 0, :], banks[2][:, :], ACT.Copy).then_inc(s_qhi, 1)
                act.wait_ge(s_krest, c + 1)
                if c:
                    act.wait_ge(s_k, c)
                nc.scalar.activation(k_middle[:], k_rest, ACT.Copy).then_inc(s_kmid, 1)
                act.wait_ge(s_qrest, c + 1)
                nc.scalar.activation(q_parts[:, c % 2, 1, :], q_rest, ACT.Copy).then_inc(s_qmid, 1)
                act.wait_ge(s_vproj, c + 1)
                nc.scalar.activation(v_op[:, TPC * c:TPC * (c + 1), 0:DH0],
                                     banks[c % 2][:, 0:TPC * DH0].rearrange("p (t d) -> p t d", t=TPC),
                                     ACT.Copy).then_inc(s_v, 1)

            def exponentials(u, kt):
                for h in range(HG):
                    act.wait_ge(s_sc, u * EXPS + HG * kt + h + 1)
                    if h == 0 and not (isinstance(u, int) and u == 0 and kt < 2):
                        act.wait_ge(s_pv, u * KT + kt - 1)
                    nc.scalar.activation(probs[:, 2 * (kt % 2) + h // 2, h % 2, :], banks[h % 2][:, :], ACT.Exp,
                                         scale=SCALE0).then_inc(s_exp, 1)

            def negated(u):
                act.wait_ge(s_nt, u + 1)
                if not (isinstance(u, int) and u == 0):
                    act.wait_ge(s_ndma, 16 * u)
                nc.scalar.activation(neg_t[:, :], neg_bank[0:3 * HG, 0:CH], ACT.Copy).then_inc(s_ncopied, 1)

            def result(u):
                act.wait_ge(s_pv, KT * (u + 1))
                if not (isinstance(u, int) and u == 0):
                    act.wait_ge(s_ot, u)
                nc.scalar.activation(pv_sb, banks[2][:, :], ACT.Copy).then_inc(s_pvcopy, 1)

            def unit(u, first=False, last=False):
                for kt in range(KT):
                    exponentials(u, kt)
                    if kt == 0 and not first:
                        result(u - 1)
                    if kt == 6 and not last:
                        negated(u + 1)

            nc.scalar.preload_act_table_set(LN_EXP)
            act.wait_ge(s_const, 6)
            act.wait_ge(s_w0, 64)
            for c in range(2):
                norm.scalar_rstd(act, c)
                norm.scalar_copy(act, c, banks)
            split(0)
            norm.scalar_rstd(act, 2)
            split(1)
            norm.scalar_copy(act, 2, banks)
            norm.scalar_rstd(act, 3)
            norm.scalar_copy(act, 3, banks)
            split(2)
            split(3)
            negated(0)
            unit(0, first=True)
            with act.Fori(1, UNITS - 1) as u:
                unit(u)
            unit(UNITS - 1, last=True)
            result(UNITS - 1)

        @block.vector
        def _(dve):
            def take_k_high(c):
                dve.wait_ge(s_khi, c + 1)
                nc.vector.scalar_tensor_tensor(out=k_rest, in0=k_high[:], scalar=k_marks[:, 0:1], in1=banks[3][0:STACK, :],
                                               op0=ALU.mult, op1=ALU.add).then_inc(s_krest, 1)

            def take_q_high(c):
                dve.wait_ge(s_qhi, c + 1)
                if c:
                    dve.wait_ge(s_qlo, c)
                nc.vector.tensor_tensor(q_rest, banks[2][:, :], q_parts[:, c % 2, 0, :], ALU.subtract).then_inc(s_qrest, 1)

            def take_k_middle(c):
                dve.wait_ge(s_kmid, c + 1)
                nc.vector.scalar_tensor_tensor(out=k_op[:, CH * c:CH * (c + 1)], in0=k_middle[:], scalar=k_marks[:, 1:2],
                                               in1=k_rest, op0=ALU.mult, op1=ALU.add).then_inc(s_k, 1)

            def split(c):
                take_k_high(c)
                take_q_high(c)
                take_k_middle(c)

            def reduce(u, i):
                dve.wait_ge(s_mx, u * MAXES + i + 1)
                nc.vector.tensor_reduce(tops[:, u, i // HG, i % HG:i % HG + 1], pair_banks[i % 2][:, :, :], axis=AX.XY,
                                        op=ALU.max).then_inc(s_red, 1)
                if i == MAXES - 1:
                    dve.wait_ge(s_red, u * MAXES + MAXES)
                    if not (isinstance(u, int) and u == 0):
                        dve.wait_ge(s_nhi, u)
                        dve.wait_ge(s_nrest, u)
                    nc.vector.tensor_scalar(neg[:], tops[:, u, :, :], -1.0, None, ALU.mult).then_inc(s_neg, 1)

            def add_result(c, g):
                u = GROUPS * c + g
                bank = banks[3][:, :].rearrange("p (t h d) -> p t h d", t=TPC, h=HG)
                dve.wait_ge(s_ot, u + 1)
                nc.vector.reciprocal(recip[:, :, :], bank[:, :, :, DH0]).then_inc(s_recip, 1)
                dve.wait_ge(s_recip, u + 1)
                nc.vector.tensor_tensor(ratio, bank[:, :, :, 0:DH0],
                                        recip[:, :, :].unsqueeze(3).to_broadcast([P, TPC, HG, DH0]), ALU.mult).then_inc(s_ratio, 1)
                dve.wait_ge(s_ratio, u + 1)
                cols = x[:, TPC * c:TPC * (c + 1), bass.ds(g * (HG * DH0), HG * DH0)].rearrange("p t (h d) -> p t h d", h=HG)
                nc.vector.tensor_tensor(cols, cols, ratio, ALU.add).then_inc(s_added, 1)

            def step(c, g, two_ahead=True):
                u = GROUPS * c + g
                for i in range(EARLY, MAXES):
                    reduce(u + 2, i)
                    if i == EARLY + 5:
                        add_result(c, g)
                if two_ahead:
                    for i in range(EARLY):
                        reduce(u + 3, i)

            def load_and_normalise(c):
                dve.wait_ge(s_x[c], 16)
                norm.vector(dve, c)

            load_and_normalise(0)
            load_and_normalise(1)
            dve.wait_ge(s_w0, 64)
            split(0)
            load_and_normalise(2)
            split(1)
            load_and_normalise(3)
            split(2)
            for i in range(2 * MAXES + EARLY):
                if i == K_HIGH:
                    take_k_high(3)
                if i == Q_HIGH:
                    take_q_high(3)
                if i == K_MIDDLE:
                    take_k_middle(3)
                reduce(i // MAXES, i % MAXES)
            for c in range(CHUNKS - 1):
                with dve.Fori(0, GROUPS) as g:
                    step(c, g)
            step(CHUNKS - 1, 0)
            step(CHUNKS - 1, 1, two_ahead=False)
            with dve.Fori(2, GROUPS) as g:
                add_result(CHUNKS - 1, g)

        @block.gpsimd
        def _(pool):
            def low(c):
                pool.wait_ge(s_qmid, c + 1)
                nc.gpsimd.tensor_tensor(q_parts[:, c % 2, 2, :], q_rest, q_parts[:, c % 2, 1, :], ALU.subtract).then_inc(s_qlo, 1)
                pool.wait_ge(s_qlo, c + 1)

            def zeros(c):
                nc.gpsimd.memset(q_rows[64:STACK, c, :].bitcast(F32), 0.0).then_inc(s_zeroed, 1)
                pool.wait_ge(s_zeroed, c + 1)

            def parts(u):
                view = lambda n: neg_parts[:, :, n, :]
                pool.wait_ge(s_neg, u + 1)
                if not (isinstance(u, int) and u == 0):
                    pool.wait_ge(s_nt, u)
                nc.gpsimd.tensor_tensor(view(0), neg[:], zero[:], ALU.add).then_inc(s_nhi, 1)
                pool.wait_ge(s_nhi, u + 1)
                nc.gpsimd.tensor_tensor(neg_rest[:], neg[:], view(0), ALU.subtract).then_inc(s_nrest, 1)
                pool.wait_ge(s_nrest, u + 1)
                nc.gpsimd.tensor_tensor(view(1), neg_rest[:], zero[:], ALU.add).then_inc(s_nmid, 1)
                pool.wait_ge(s_nmid, u + 1)
                nc.gpsimd.tensor_tensor(view(2), neg_rest[:], view(1), ALU.subtract).then_inc(s_nparts, 1)

            nc.gpsimd.memset(ident[:], 0.0).then_inc(s_const, 1)
            nc.gpsimd.memset(b["eps"][:], LN_EPS).then_inc(s_const, 1)
            nc.gpsimd.memset(zero[:], 0.0)
            pool.wait_ge(s_const, 2)
            nc.gpsimd.affine_select(out=ident[:], in_=ident[:], compare_op=ALU.not_equal, fill=1.0, base=0,
                                    pattern=[[-1, P]], channel_multiplier=1).then_inc(s_const, 1)
            nc.gpsimd.memset(v_op[:], 0.0).then_inc(s_const, 1)
            pool.wait_ge(s_const, 4)
            nc.gpsimd.tensor_copy(ident16[:], ident[:]).then_inc(s_const, 1)
            nc.gpsimd.memset(v_op[:, :, DH0:DH0 + 1], 1.0).then_inc(s_const, 1)
            pool.wait_ge(s_const, 6)
            zeros(0)
            zeros(1)
            zeros(2)
            low(0)
            low(1)
            zeros(3)
            low(2)
            low(3)
            parts(0)
            with pool.Fori(1, UNITS) as u:
                parts(u)

        @block.sync
        def _(sp):
            def copies(c):
                sp.wait_ge(s_zeroed, c + 1)
                sp.wait_ge(s_qlo, c + 1)
                for n, (part, _) in enumerate(PRODUCTS0):
                    sp.dma_start(q_rows[DH0 * n:DH0 * (n + 1), c, :], q_parts[:, c % 2, part, :]).then_inc(s_copied[c % 2], 16)

            def rows(u):
                sp.wait_ge(s_ncopied, u + 1)
                sp.dma_start(q_op[MROW:MROW + 3, u, :, :], neg_t[:, :]).then_inc(s_ndma, 16)

            for c in range(CHUNKS):
                sp.dma_start(x[:, TPC * c:TPC * (c + 1), :], x_dram[:, TPC * c:TPC * (c + 1), :]).then_inc(s_x[c], 16)
                if c == 0:
                    for dst, src in ((wk_sb, wk0), (wq_sb, wq0), (wv_sb, wv0), (k_marks, marks0)):
                        sp.dma_start(dst[:], src).then_inc(s_w0, 16)
            copies(0)
            copies(1)
            copies(2)
            rows(0)
            copies(3)
            with sp.Fori(1, UNITS) as u:
                rows(u)
            sp.wait_ge(s_ndma, 16 * UNITS)


def experts(nc, ctx, sb, sem, b, banks, pair_banks, work, w_up, w_down, s_exp_w, s_router, rw, rb, gate_w, up_w, down_w, later_loads):
    x, xnT = b["x"], b["xnT"]
    rw_sb, rb_sb, rank = sb("rw_sb", [P, EXPERTS]), sb("rb_sb", [P, EXPERTS]), sb("rank", [P, EXPERTS])
    small = {n: sb(f"router_{n}", [P, TILES, EXPERTS]) for n in ("logit", "prob", "rest", "mark", "sel1", "sel2", "combine")}
    narrow = {n: sb(f"router_{n}", [P, TILES]) for n in ("max", "sum", "inv", "p1", "p2", "first", "den", "iden")}
    combine = small["combine"]
    hidden = work[:, 0:4 * CH].rearrange("p (s f n) -> p s f n", s=2, f=FH)
    silu = work[:, 4 * CH:6 * CH].rearrange("p (s n) -> p s n", s=2)
    wide = lambda ap: ap.unsqueeze(2).to_broadcast([P, TILES, EXPERTS])
    per_tile = lambda ap: ap.unsqueeze(1).to_broadcast([P, TILES, EXPERTS])

    norm = Norm(nc, ctx, "n1", b)
    s_rank, s_logit, s_shift, s_prob, s_route, s_combine = (sem(f"s_r_{n}") for n in ("rank", "logit", "shift", "prob", "chain", "combine"))
    s_gu, s_silu, s_hid, s_down, s_acc = (sem(f"s_e_{n}") for n in ("gu", "silu", "hid", "down", "acc"))
    STEPS = CHUNKS

    with nc.Block() as block:
        @block.sync
        def _(sp):
            sp.dma_start(rw_sb[:], rw).then_inc(s_router, 16)
            sp.dma_start(rb_sb[:], rb.to_broadcast([P, EXPERTS])).then_inc(s_router, 16)

            def load(e, slot):
                sp.dma_start(w_up[:, slot, 0, :], gate_w[e, :, :]).then_inc(s_exp_w[slot], 16)
                sp.dma_start(w_up[:, slot, 1, :], up_w[e, :, :]).then_inc(s_exp_w[slot], 16)
                sp.dma_start(w_down[:, slot, :, :], down_w[e, :, :, :].rearrange("f p d -> p f d")).then_inc(s_exp_w[slot], 16)

            load(0, 0)
            load(1, 1)
            for dst, src, signal in later_loads:
                sp.dma_start(dst, src).then_inc(signal, 16)
            with sp.Fori(1, EXPERTS // 2) as pair:
                for slot in range(2):
                    sp.wait_ge(s_down, pair * 2 * STEPS + (slot - 1) * STEPS)
                    load(pair * 2 + slot, slot)

        @block.gpsimd
        def _(pool):
            for e in range(EXPERTS):
                nc.gpsimd.memset(rank[:, e:e + 1], float(EXPERTS - e)).then_inc(s_rank, 1)

        @block.tensor
        def _(pe):
            def gate_up(e, slot, c, f):
                i = (e * STEPS + c) * FH + f
                if not (isinstance(e, int) and e == 0 and c == 0):
                    pe.wait_ge(s_hid, i - 1)
                for m in range(2):
                    mm = nc.tensor.matmul(pair_banks[f][:, m, :], w_up[:, slot, m, P * f:P * (f + 1)],
                                          xnT[:, CH * c:CH * (c + 1)], start=True, stop=True)
                mm.then_inc(s_gu, 1)

            def down(e, slot, c):
                k = e * STEPS + c
                pe.wait_ge(s_hid, FH * (k + 1))
                if not (isinstance(e, int) and e == 0 and c < 2):
                    pe.wait_ge(s_acc, TPC * (k - 1))
                for t in range(TPC):
                    for f in range(FH):
                        mm = nc.tensor.matmul(banks[c % 2][:, P * t:P * (t + 1)], hidden[:, c % 2, f, P * t:P * (t + 1)],
                                              w_down[:, slot, f, :], start=(f == 0), stop=(f == FH - 1))
                mm.then_inc(s_down, 1)

            def expert(e, slot, first=False):
                pe.wait_ge(s_exp_w[slot], (e - slot) * 24 + 48)
                for c in range(STEPS):
                    for f in range(FH):
                        gate_up(e, slot, c, f)
                        if f == 0 and c:
                            down(e, slot, c - 1)
                        if f == 0 and c == 0 and not first:
                            down(e - 1, 1 - slot, STEPS - 1)

            for c in range(CHUNKS):
                norm.tensor(pe, c, banks)
            pe.wait_ge(s_router, 32)
            pe.wait_ge(norm.done, CHUNKS)
            for t in range(TILES):
                mm = nc.tensor.matmul(banks[2][:, EXPERTS * t:EXPERTS * (t + 1)], xnT[:, P * t:P * (t + 1)], rw_sb[:],
                                      start=True, stop=True)
            mm.then_inc(s_logit, 1)
            expert(0, 0, first=True)
            expert(1, 1)
            with pe.Fori(1, EXPERTS // 2) as pair:
                expert(pair * 2, 0)
                expert(pair * 2 + 1, 1)
            down(EXPERTS - 1, 1, STEPS - 1)

        @block.scalar
        def _(act):
            nc.scalar.preload_act_table_set(LN_EXP)
            for c in range(CHUNKS):
                norm.scalar_rstd(act, c)
                norm.scalar_copy(act, c, banks)
            act.wait_ge(s_shift, 1)
            nc.scalar.activation(small["prob"][:], small["logit"][:], ACT.Exp).then_inc(s_prob, 1)

            def expert(e):
                for c in range(STEPS):
                    for f in range(FH):
                        i = (e * STEPS + c) * FH + f
                        act.wait_ge(s_gu, i + 1)
                        if not (isinstance(e, int) and e == 0 and c == 0):
                            act.wait_ge(s_hid, i - 1)
                        nc.scalar.activation(silu[:, f, :], pair_banks[f][:, 0, :], ACT.Silu).then_inc(s_silu, 1)

            expert(0)
            with act.Fori(1, EXPERTS) as e:
                expert(e)

        @block.vector
        def _(dve):
            steps = [0]

            def chained(instruction):
                steps[0] += 1
                instruction.then_inc(s_route, 1)
                dve.wait_ge(s_route, steps[0])

            for c in range(CHUNKS):
                norm.vector(dve, c)
            v = nc.vector
            logit, prob, rest, mark, sel1, sel2 = (small[n][:] for n in ("logit", "prob", "rest", "mark", "sel1", "sel2"))
            dve.wait_ge(s_logit, 1)
            dve.wait_ge(s_rank, EXPERTS)
            chained(v.tensor_tensor(logit, banks[2][:, 0:TILES * EXPERTS].rearrange("p (t e) -> p t e", t=TILES),
                                    per_tile(rb_sb[:]), ALU.add))
            chained(v.tensor_reduce(narrow["max"][:], logit, axis=AX.X, op=ALU.max))
            v.tensor_tensor(logit, logit, wide(narrow["max"][:]), ALU.subtract).then_inc(s_shift, 1)
            dve.wait_ge(s_prob, 1)
            chained(v.tensor_reduce(narrow["sum"][:], prob, axis=AX.X, op=ALU.add))
            chained(v.reciprocal(narrow["inv"][:], narrow["sum"][:]))
            chained(v.tensor_tensor(prob, prob, wide(narrow["inv"][:]), ALU.mult))
            chained(v.tensor_reduce(narrow["p1"][:], prob, axis=AX.X, op=ALU.max))
            chained(v.tensor_tensor(mark, prob, wide(narrow["p1"][:]), ALU.is_equal))
            chained(v.tensor_tensor(mark, mark, per_tile(rank[:]), ALU.mult))
            chained(v.tensor_reduce(narrow["first"][:], mark, axis=AX.X, op=ALU.max))
            chained(v.tensor_tensor(sel1, mark, wide(narrow["first"][:]), ALU.is_equal))
            chained(v.scalar_tensor_tensor(out=rest, in0=sel1, scalar=-2.0, in1=prob, op0=ALU.mult, op1=ALU.add))
            chained(v.tensor_reduce(narrow["p2"][:], rest, axis=AX.X, op=ALU.max))
            chained(v.tensor_tensor(mark, rest, wide(narrow["p2"][:]), ALU.is_equal))
            chained(v.tensor_tensor(mark, mark, per_tile(rank[:]), ALU.mult))
            chained(v.tensor_reduce(narrow["first"][:], mark, axis=AX.X, op=ALU.max))
            chained(v.tensor_tensor(sel2, mark, wide(narrow["first"][:]), ALU.is_equal))
            chained(v.tensor_tensor(narrow["den"][:], narrow["p1"][:], narrow["p2"][:], ALU.add))
            chained(v.reciprocal(narrow["iden"][:], narrow["den"][:]))
            chained(v.tensor_tensor(sel1, sel1, sel2, ALU.add))
            chained(v.tensor_tensor(sel1, sel1, prob, ALU.mult))
            v.tensor_tensor(combine[:], sel1, wide(narrow["iden"][:]), ALU.mult).then_inc(s_combine, 1)
            dve.wait_ge(s_combine, 1)

            def product(e, c, f):
                i = (e * STEPS + c) * FH + f
                dve.wait_ge(s_silu, i + 1)
                if not (isinstance(e, int) and e == 0 and c < 2):
                    dve.wait_ge(s_down, e * STEPS + c - 1)
                v.tensor_tensor(hidden[:, c % 2, f, :], silu[:, f, :], pair_banks[f][:, 1, :], ALU.mult).then_inc(s_hid, 1)

            def accumulate(e, c):
                k = e * STEPS + c
                dve.wait_ge(s_down, k + 1)
                if not (isinstance(e, int) and e == 0):
                    dve.wait_ge(s_acc, TPC * (k - 3))
                for t in range(TPC):
                    tile = TPC * c + t
                    v.scalar_tensor_tensor(out=x[:, tile, :], in0=banks[c % 2][:, P * t:P * (t + 1)],
                                           scalar=combine[:, tile, bass.ds(e, 1)], in1=x[:, tile, :],
                                           op0=ALU.mult, op1=ALU.add).then_inc(s_acc, 1)

            def expert(e, first=False):
                for c in range(STEPS):
                    for f in range(FH):
                        product(e, c, f)
                    if c:
                        accumulate(e, c - 1)
                    elif not first:
                        accumulate(e - 1, STEPS - 1)

            expert(0, first=True)
            expert(1)
            with dve.Fori(2, EXPERTS) as e:
                expert(e)
            accumulate(EXPERTS - 1, STEPS - 1)


def second_attention(nc, ctx, sb, sem, b, banks, pair_banks, arena, probs, work, wqk_sb, wv_sb, wo_sb, g_half, s_w1):
    x, xnT = b["x"], b["xnT"]
    qk_op = arena[:, :].rearrange("r (s h n) -> r s h n", s=2, h=H1)
    parts = b["parts"]
    tri, means, one = sb("tri", [P, P]), sb("means", [P, P]), sb("one", [P, 1])
    v_sb = sb("v_sb", [P, KT, P])
    y_sb = sb("y_sb", [P, PAIRS, SEQ])
    rest, y_square, log_mean, rstd = (work[:, CH * n:CH * (n + 1)] for n in range(4))

    norm = Norm(nc, ctx, "n2", b)
    s_masks, s_g = sem("s_masks"), sem("s_g")
    s_proj, s_hi, s_rest, s_mid, s_lo = (sem(f"s_b_{n}") for n in ("proj", "hi", "rest", "mid", "lo"))
    s_copied = [sem("s_b_copied0"), sem("s_b_copied1")]
    s_sc, s_square, s_weight, s_sum = (sem(f"s_a_{n}") for n in ("score", "square", "weight", "sum"))
    s_v, s_vcopy = sem("s_a_v"), sem("s_a_vcopy")
    s_ysq, s_mean, s_log, s_rstd, s_y = (sem(f"s_a_{n}") for n in ("ysq", "mean", "log", "rstd", "y"))
    s_o, s_added = sem("s_a_o"), sem("s_a_added")

    ITEMS = [(c, kt) for c in range(2) for kt in range(TPC * (c + 1))]
    N = len(ITEMS)
    LAG = 2
    LAST = {0: TPC, 1: N}
    COPIES = 16 * len(PRODUCTS1)
    OPERANDS = 4

    def first_column(c, kt):
        return max(0, kt - TPC * c) * P

    with nc.Block() as block:
        @block.gpsimd
        def _(pool):
            nc.gpsimd.memset(tri[:], 1.0).then_inc(s_masks, 1)
            nc.gpsimd.memset(means[:], 0.0).then_inc(s_masks, 1)
            nc.gpsimd.memset(one[:], 1.0).then_inc(s_masks, 1)
            pool.wait_ge(s_masks, 3)
            nc.gpsimd.affine_select(out=tri[:], in_=tri[:], compare_op=ALU.is_ge, fill=0.0, base=0,
                                    pattern=[[1, P]], channel_multiplier=-1).then_inc(s_masks, 1)
            pool.wait_ge(s_masks, 4)
            for h in range(2):
                nc.gpsimd.memset(means[DV1 * h:DV1 * (h + 1), DV1 * h:DV1 * (h + 1)], 1.0 / DV1).then_inc(s_masks, 1)
                pool.wait_ge(s_masks, 5 + h)
            pool.wait_ge(s_w1, 16 * 6)
            nc.gpsimd.tensor_scalar(g_half[:], g_half[:], 0.5, None, ALU.mult).then_inc(s_g, 1)

        @block.sync
        def _(sp):
            def copies(bt, half):
                if bt:
                    sp.wait_ge(s_sc, N * (PAIRS // 2) * (half + 1))
                for n in range(OPERANDS):
                    m = (bt * 2 + half) * OPERANDS + n
                    which, c = n // 2, n % 2
                    sp.wait_ge(s_lo, m + 1)
                    for i, product in enumerate(PRODUCTS1):
                        sp.dma_start(qk_op[DF * i:DF * (i + 1), which, HALF * half:HALF * (half + 1), CH * c:CH * (c + 1)],
                                     parts[:, m % 2, product[which], :]).then_inc(s_copied[m % 2], 16)

            for bt in range(BATCH):
                for half in range(2):
                    copies(bt, half)
            for s in s_copied:
                sp.wait_ge(s, COPIES * 2 * OPERANDS)

        @block.tensor
        def _(pe):
            def build(bt, half):
                for n in range(OPERANDS):
                    m = (bt * 2 + half) * OPERANDS + n
                    which, c = n // 2, n % 2
                    if m:
                        pe.wait_ge(s_rest, m)
                    if bt and n == 0:
                        pe.wait_ge(s_vcopy, 2 * (PAIRS // 2) * (half + 1))
                    nc.tensor.matmul(banks[2][:, :], wqk_sb[:, which, half, :],
                                     xnT[:, SEQ * bt + CH * c:SEQ * bt + CH * (c + 1)], start=True, stop=True).then_inc(s_proj, 1)

            def ready(bt, half):
                done = bt * 2 + half + 1
                for s in s_copied:
                    pe.wait_ge(s, COPIES * (OPERANDS // 2) * done)

            def values(g, bt, r):
                if not (isinstance(g, int) and g == 0 and r == 0):
                    pe.wait_ge(s_vcopy, 2 * g + r)
                for k in range(4):
                    col = SEQ * bt + P * (4 * r + k)
                    mm = nc.tensor.matmul(banks[2][:, P * k:P * (k + 1)], xnT[:, col:col + P],
                                          wv_sb[:, bass.ds((g - PAIRS * bt) * P, P)], start=True, stop=True)
                mm.then_inc(s_v, 1)

            def scores(g, bt, i):
                c, kt = ITEMS[i]
                q0 = first_column(c, kt)
                if not (isinstance(g, int) and g == 0 and i < 2):
                    pe.wait_ge(s_square, N * g + i - 1)
                for h in range(2):
                    head = (g - PAIRS * bt) * 2 + h
                    mm = nc.tensor.matmul(pair_banks[i % 2][:, h, q0:CH], qk_op[:, 1, head, P * kt:P * (kt + 1)],
                                          qk_op[:, 0, head, CH * c + q0:CH * (c + 1)], start=True, stop=True)
                mm.then_inc(s_sc, 1)

            def sums(g, i):
                c, kt = ITEMS[i]
                q0 = first_column(c, kt)
                pe.wait_ge(s_weight, N * g + i + 1)
                if kt == 0 and not (isinstance(g, int) and g == 0):
                    pe.wait_ge(s_y, 2 * g + c - 1)
                if c == 0 and kt == 0:
                    pe.wait_ge(s_vcopy, 2 * g + 1)
                if kt == TPC:
                    pe.wait_ge(s_vcopy, 2 * g + 2)
                for h in range(2):
                    mm = nc.tensor.matmul(banks[c][DV1 * h:DV1 * (h + 1), q0:CH], v_sb[:, kt, DV1 * h:DV1 * (h + 1)],
                                          probs[:, i % 4, h, q0:CH], start=(kt == 0), stop=(i + 1 == LAST[c]))
                mm.then_inc(s_sum, 1)

            def mean(q):
                pe.wait_ge(s_ysq, q + 1)
                if not (isinstance(q, int) and q == 0):
                    pe.wait_ge(s_log, q)
                nc.tensor.matmul(banks[3][:, :], means[:], y_square, start=True, stop=True).then_inc(s_mean, 1)

            def pair(g, bt, first=False):
                values(g, bt, 0)
                for i in range(N):
                    scores(g, bt, i)
                    if i >= LAG:
                        sums(g, i - LAG)
                    elif not first:
                        sums(g - 1, N + i - LAG)
                    if i == LAG - 1:
                        values(g, bt, 1)
                    if i == 4 and not first:
                        mean(2 * g - 1)
                    if i == 8:
                        mean(2 * g)

            def project(bt):
                pe.wait_ge(s_y, 2 * PAIRS * (bt + 1))
                for r in range(2):
                    for t in range(4):
                        for p in range(PAIRS):
                            col = P * (4 * r + t)
                            mm = nc.tensor.matmul(banks[2 + r][:, P * t:P * (t + 1)], y_sb[:, p, col:col + P],
                                                  wo_sb[:, p, :], start=(p == 0), stop=(p == PAIRS - 1))
                    mm.then_inc(s_o, 1)

            pe.wait_ge(s_masks, 6)
            pe.wait_ge(s_w1, 16 * 6)
            for c in range(CHUNKS):
                norm.tensor(pe, c, banks)
            pe.wait_ge(norm.done, CHUNKS)
            build(0, 0)
            build(0, 1)
            pe.wait_ge(s_rest, 2 * OPERANDS)
            ready(0, 0)
            pair(0, 0, first=True)
            with pe.Fori(1, PAIRS // 2) as g:
                pair(g, 0)
            build(1, 0)
            pe.wait_ge(s_rest, 3 * OPERANDS)
            with pe.Fori(PAIRS // 2, PAIRS) as g:
                pair(g, 0)
            build(1, 1)
            pe.wait_ge(s_rest, 4 * OPERANDS)
            for i in range(N - LAG, N):
                sums(PAIRS - 1, i)
            mean(2 * PAIRS - 1)
            project(0)
            pe.wait_ge(s_added, 2)
            ready(1, 0)
            ready(1, 1)
            pair(PAIRS, 1, first=True)
            with pe.Fori(PAIRS + 1, 2 * PAIRS) as g:
                pair(g, 1)
            for i in range(N - LAG, N):
                sums(2 * PAIRS - 1, i)
            mean(4 * PAIRS - 1)
            project(1)

        @block.scalar
        def _(act):
            def build(bt, half):
                for n in range(OPERANDS):
                    m = (bt * 2 + half) * OPERANDS + n
                    act.wait_ge(s_proj, m + 1)
                    if m >= 2:
                        act.wait_ge(s_copied[m % 2], COPIES * (m // 2))
                    nc.scalar.activation(parts[:, m % 2, 0, :], banks[2][:, :], ACT.Copy).then_inc(s_hi, 1)
                    act.wait_ge(s_rest, m + 1)
                    nc.scalar.activation(parts[:, m % 2, 1, :], rest, ACT.Copy).then_inc(s_mid, 1)

            def square(g, i):
                c, kt = ITEMS[i]
                q0 = first_column(c, kt)
                act.wait_ge(s_sc, N * g + i + 1)
                if not (isinstance(g, int) and g == 0 and i < 4):
                    act.wait_ge(s_sum, N * g + i - 3)
                nc.scalar.activation(probs[:, i % 4, :, q0:CH], pair_banks[i % 2][:, :, q0:CH], ACT.Square,
                                     bias=1.0, scale=0.25).then_inc(s_square, 1)

            def result_square(g, c):
                q = 2 * g + c
                act.wait_ge(s_sum, N * g + LAST[c])
                if not (isinstance(g, int) and g == 0 and c == 0):
                    act.wait_ge(s_mean, q)
                nc.scalar.activation(y_square, banks[c][:, :], ACT.Square, scale=0.5).then_inc(s_ysq, 1)

            def result_rstd(q):
                act.wait_ge(s_mean, q + 1)
                if not (isinstance(q, int) and q == 0):
                    act.wait_ge(s_rstd, q)
                    act.wait_ge(s_y, q)
                nc.scalar.activation(log_mean, banks[3][:, :], ACT.Ln, bias=b["eps"][:, 0:1]).then_inc(s_log, 1)
                act.wait_ge(s_log, q + 1)
                nc.scalar.activation(rstd, log_mean, ACT.Exp, scale=-0.5).then_inc(s_rstd, 1)

            def pair(g, first=False):
                nc.scalar.preload_act_table_set(LN_EXP)
                for i in range(N):
                    if i == 3 and not first:
                        result_square(g - 1, 1)
                    if i == 5 and not first:
                        result_rstd(2 * g - 1)
                    if i == 7:
                        result_square(g, 0)
                    if i == 9:
                        result_rstd(2 * g)
                    square(g, i)

            for c in range(CHUNKS):
                norm.scalar_rstd(act, c)
                norm.scalar_copy(act, c, banks)
            act.wait_ge(s_masks, 3)
            build(0, 0)
            build(0, 1)
            pair(0, first=True)
            with act.Fori(1, PAIRS // 2) as g:
                pair(g)
            build(1, 0)
            with act.Fori(PAIRS // 2, PAIRS) as g:
                pair(g)
            build(1, 1)
            result_square(PAIRS - 1, 1)
            result_rstd(2 * PAIRS - 1)
            pair(PAIRS, first=True)
            with act.Fori(PAIRS + 1, 2 * PAIRS) as g:
                pair(g)
            result_square(2 * PAIRS - 1, 1)
            result_rstd(4 * PAIRS - 1)

        @block.vector
        def _(dve):
            def build(bt, half):
                for n in range(OPERANDS):
                    m = (bt * 2 + half) * OPERANDS + n
                    dve.wait_ge(s_hi, m + 1)
                    if m:
                        dve.wait_ge(s_lo, m)
                    nc.vector.tensor_tensor(rest, banks[2][:, :], parts[:, m % 2, 0, :], ALU.subtract).then_inc(s_rest, 1)
                    dve.wait_ge(s_mid, m + 1)
                    nc.vector.tensor_tensor(parts[:, m % 2, 2, :], rest, parts[:, m % 2, 1, :], ALU.subtract).then_inc(s_lo, 1)

            def copy_values(g, r):
                dve.wait_ge(s_v, 2 * g + r + 1)
                if not (isinstance(g, int) and g == 0):
                    dve.wait_ge(s_sum, N * g - (N - 8) * (1 - r))
                nc.vector.tensor_copy(v_sb[:, 4 * r:4 * r + 4, :], banks[2][:, :].rearrange("p (k n) -> p k n", k=4)).then_inc(s_vcopy, 1)

            def weights(g, i):
                c, kt = ITEMS[i]
                q0 = first_column(c, kt)
                tile = probs[:, i % 4, :, :]
                dve.wait_ge(s_square, N * g + i + 1)
                if kt >= TPC * c:
                    diagonal = tile[:, :, q0:q0 + P]
                    mm = nc.vector.scalar_tensor_tensor(out=diagonal, in0=diagonal, scalar=1.0,
                                                        in1=tri[:].unsqueeze(1).to_broadcast([P, 2, P]),
                                                        op0=ALU.add, op1=ALU.mult)
                    q0 += P
                if q0 < CH:
                    mm = nc.vector.tensor_scalar(tile[:, :, q0:CH], tile[:, :, q0:CH], 1.0, None, ALU.add)
                mm.then_inc(s_weight, 1)

            def normalise(g, bt, c):
                q = 2 * g + c
                dve.wait_ge(s_rstd, q + 1)
                nc.vector.scalar_tensor_tensor(out=y_sb[:, g - PAIRS * bt, CH * c:CH * (c + 1)], in0=banks[c][:, :],
                                               scalar=g_half[:, 0:1], in1=rstd, op0=ALU.mult, op1=ALU.mult).then_inc(s_y, 1)

            def pair(g, bt, first=False):
                copy_values(g, 0)
                for i in range(N):
                    if i == 5 and not first:
                        normalise(g - 1, bt, 1)
                    if i == 9:
                        normalise(g, bt, 0)
                    weights(g, i)
                    if i == 2:
                        copy_values(g, 1)

            def add(bt):
                for r in range(2):
                    dve.wait_ge(s_o, 2 * bt + r + 1)
                    tiles = x[:, KT * bt + 4 * r:KT * bt + 4 * r + 4, :]
                    nc.vector.tensor_tensor(tiles, banks[2 + r][:, :].rearrange("p (t d) -> p t d", t=4), tiles, ALU.add).then_inc(s_added, 1)

            for c in range(CHUNKS):
                norm.vector(dve, c)
            dve.wait_ge(s_masks, 4)
            dve.wait_ge(s_g, 1)
            build(0, 0)
            build(0, 1)
            pair(0, 0, first=True)
            with dve.Fori(1, PAIRS // 2) as g:
                pair(g, 0)
            build(1, 0)
            with dve.Fori(PAIRS // 2, PAIRS) as g:
                pair(g, 0)
            build(1, 1)
            normalise(PAIRS - 1, 0, 1)
            add(0)
            pair(PAIRS, 1, first=True)
            with dve.Fori(PAIRS + 1, 2 * PAIRS) as g:
                pair(g, 1)
            normalise(2 * PAIRS - 1, 1, 1)
            add(1)


def feed_forward(nc, ctx, sb, sem, b, banks, pair_banks, work, ints, s_w2, out):
    x, xnT = b["x"], b["xnT"]
    scaled = sb("scaled", [P, 3, HID])
    hidden = work[:, 0:6 * CH].rearrange("p (s j n) -> p s j n", s=2, j=HT)
    silu = work[:, 6 * CH:8 * CH].rearrange("p (s n) -> p s n", s=2)
    norm = Norm(nc, ctx, "n3", b)
    s_scaled, s_gu, s_silu, s_hid, s_down, s_sum = (sem(f"s_f_{n}") for n in ("scaled", "gu", "silu", "hid", "down", "sum"))
    s_out = sem("s_out")
    out_dram = out.rearrange("(t p) d -> p t d", p=P)

    with nc.Block() as block:
        @block.sync
        def _(sp):
            for c in range(CHUNKS):
                sp.wait_ge(s_sum, c + 1)
                sp.dma_start(out_dram[:, TPC * c:TPC * (c + 1), :], x[:, TPC * c:TPC * (c + 1), :]).then_inc(s_out, 16)
            sp.wait_ge(s_out, 16 * CHUNKS)

        @block.tensor
        def _(pe):
            def gate_up(c, j):
                i = HT * c + j
                if i >= 2:
                    pe.wait_ge(s_hid, i - 1)
                for m in range(2):
                    mm = nc.tensor.matmul(pair_banks[i % 2][:, m, :], scaled[:, m, P * j:P * (j + 1)],
                                          xnT[:, CH * c:CH * (c + 1)], start=True, stop=True)
                mm.then_inc(s_gu, 1)

            def down(c):
                pe.wait_ge(s_hid, HT * (c + 1))
                if c >= 2:
                    pe.wait_ge(s_sum, c - 1)
                for t in range(TPC):
                    for j in range(HT):
                        mm = nc.tensor.matmul(banks[2 + c % 2][:, P * t:P * (t + 1)], hidden[:, c % 2, j, P * t:P * (t + 1)],
                                              scaled[:, 2, P * j:P * (j + 1)], start=(j == 0), stop=(j == HT - 1))
                mm.then_inc(s_down, 1)

            for c in range(CHUNKS):
                norm.tensor(pe, c, banks)
            pe.wait_ge(s_scaled, 3)
            for c in range(CHUNKS):
                pe.wait_ge(norm.done, c + 1)
                for j in range(HT):
                    gate_up(c, j)
                    if j == 0 and c:
                        down(c - 1)
            down(CHUNKS - 1)

        @block.scalar
        def _(act):
            nc.scalar.preload_act_table_set(LN_EXP)
            for c in range(CHUNKS):
                norm.scalar_rstd(act, c)
                norm.scalar_copy(act, c, banks)
            for i in range(HT * CHUNKS):
                act.wait_ge(s_gu, i + 1)
                if i >= 2:
                    act.wait_ge(s_hid, i - 1)
                nc.scalar.activation(silu[:, i % 2, :], pair_banks[i % 2][:, 0, :], ACT.Silu).then_inc(s_silu, 1)

        @block.vector
        def _(dve):
            dve.wait_ge(s_w2, 48)
            for m in range(3):
                nc.vector.tensor_scalar(scaled[:, m, :], ints[:, m, :], QSCALE, None, ALU.mult).then_inc(s_scaled, 1)
            for c in range(CHUNKS):
                norm.vector(dve, c)

            def add(c):
                dve.wait_ge(s_down, c + 1)
                tiles = x[:, TPC * c:TPC * (c + 1), :]
                nc.vector.tensor_tensor(tiles, banks[2 + c % 2][:, :].rearrange("p (t d) -> p t d", t=TPC), tiles,
                                        ALU.add).then_inc(s_sum, 1)

            for c in range(CHUNKS):
                for j in range(HT):
                    i = HT * c + j
                    dve.wait_ge(s_silu, i + 1)
                    if c >= 2:
                        dve.wait_ge(s_down, c - 1)
                    nc.vector.tensor_tensor(hidden[:, c % 2, j, :], silu[:, i % 2, :], pair_banks[i % 2][:, 1, :],
                                            ALU.mult).then_inc(s_hid, 1)
                if c:
                    add(c - 1)
            add(CHUNKS - 1)


def kernel(L0_attn_x, L0_attn_Wq, L0_attn_Wk, L0_attn_Wv, L0_ffn_router_w, L0_ffn_router_b, L0_ffn_gate_w,
           L0_ffn_up_w, L0_ffn_down_w, L1_attn_Wq, L1_attn_Wk, L1_attn_Wv, L1_attn_Wo, L1_attn_g_weight,
           L1_ffn_w_gate, L1_ffn_w_up, L1_ffn_w_down):
    import concourse.bacc as bacc
    from concourse.bass_utils import run_bass_kernel_spmd

    by_feature0 = L0_attn_Wq.reshape(H0, DH0, P).transpose(2, 1, 0).reshape(P, P)
    by_feature1 = [w.reshape(2, HALF, DF, P).transpose(3, 0, 2, 1).reshape(P, 2, P) for w in (L1_attn_Wq, L1_attn_Wk)]
    stacked_key = np.zeros((P, STACK), L0_attn_Wk.dtype)
    marks = np.zeros((STACK, 3), np.float32)
    for n, (_, part) in enumerate(PRODUCTS0):
        rows = slice(DH0 * n, DH0 * (n + 1))
        stacked_key[:, rows] = L0_attn_Wk.T
        marks[rows, 0:part] = -1.0
    marks[MROW:MROW + 3, 0] = marks[MROW:MROW + 3, 2] = 1.0
    arrays = {
        "x_in": L0_attn_x.reshape(TOKENS, P), "wq0": by_feature0, "wk0": stacked_key, "wv0": L0_attn_Wv.T,
        "marks0": marks,
        "rw": L0_ffn_router_w.T, "rb": L0_ffn_router_b.reshape(1, EXPERTS),
        "gate_w": L0_ffn_gate_w, "up_w": L0_ffn_up_w, "down_w": L0_ffn_down_w.reshape(EXPERTS, FH, P, P),
        "wq1": by_feature1[0], "wk1": by_feature1[1], "wv1": L1_attn_Wv.T,
        "wo1": L1_attn_Wo.T.reshape(PAIRS, P, P).transpose(1, 0, 2), "g1": L1_attn_g_weight.reshape(DV1, 1),
        "wg2": L1_ffn_w_gate.T, "wu2": L1_ffn_w_up.T, "wd2": L1_ffn_w_down.T.reshape(HT, P, P).transpose(1, 0, 2),
    }
    arrays = {name: np.ascontiguousarray(a) for name, a in arrays.items()}
    nc = bacc.Bacc("TRN2", target_bir_lowering=False, num_devices=1)
    aps = [nc.dram_tensor(name, a.shape, mybir.dt.from_np(a.dtype), kind="ExternalInput").ap() for name, a in arrays.items()]
    aps.append(nc.dram_tensor("out", (TOKENS, P), F32, kind="ExternalOutput").ap())
    build(nc, *aps)
    result = run_bass_kernel_spmd(nc, [arrays], core_ids=[0])
    return result.results[0]["out"].reshape(BATCH, SEQ, P)
```

```python
from contextlib import ExitStack

import numpy as np
import concourse.bass as bass
from concourse import mybir

F32, F32R, BF16, I32 = mybir.dt.float32, mybir.dt.float32r, mybir.dt.bfloat16, mybir.dt.int32
ALU = mybir.AluOpType
ACT = mybir.ActivationFunctionType
AX = mybir.AxisListType

P = 128
BATCH, SEQ = 2, 1024
TOKENS = BATCH * SEQ
TILES = TOKENS // P
CH = 512
CHUNKS = TOKENS // CH
TPC = CH // P
KT = SEQ // P
LN_EPS = 1e-5
LN_EXP = "natural_log_exp_and_others"

H0, DH0 = 16, 8
HG = 4
GROUPS = H0 // HG
UNITS = CHUNKS * GROUPS
STACK = 96
SCALE0 = float(1.0 / np.sqrt(DH0))
PRODUCTS0 = [(n // 3, n % 3) for n in range(9)]
MROW = DH0 * len(PRODUCTS0)

EXPERTS, DFF0 = 8, 256
FH = DFF0 // P
SPLIT = float(2 ** 12 + 1)

H1, DF, DV1 = 16, 16, 64
PAIRS = H1 // 2
HALF = H1 // 2
PRODUCTS1 = [(0, 0), (0, 1), (1, 0), (0, 2), (2, 0), (1, 1)]
RMS_EPS = 1e-5

HID = 384
HT = HID // P
QSCALE = float(np.float32(1.0 / 127.0))


class Norm:

    def __init__(self, nc, ctx, tag, buf):
        self.nc, self.b = nc, buf
        sem = lambda n: ctx.enter_context(nc.semaphore(f"{tag}_{n}"))
        self.stats, self.moments, self.logv, self.rstd = sem("stats"), sem("moments"), sem("logv"), sem("rstd")
        self.normed, self.turned, self.done = sem("normed"), sem("turned"), sem("xnT")

    def statistics(self, dve, c):
        nc, b = self.nc, self.b
        for t in range(TPC * c, TPC * (c + 1)):
            nc.vector.bn_stats(b["bn"][:, t, :], b["x"][:, t, :]).then_inc(self.stats, 1)
        dve.wait_ge(self.stats, TPC * (c + 1))
        for t in range(TPC * c, TPC * (c + 1)):
            nc.vector.bn_aggr(b["mv"][:, t, :], b["bn"][:, t, :]).then_inc(self.moments, 1)

    def normalise(self, dve, c):
        nc, b = self.nc, self.b
        dve.wait_ge(self.moments, TPC * (c + 1))
        dve.wait_ge(self.rstd, c + 1)
        if c >= 2:
            dve.wait_ge(self.turned, c - 1)
        for t in range(TPC * c, TPC * (c + 1)):
            nc.vector.tensor_scalar(b["xn"][:, t % (2 * TPC), :], b["x"][:, t, :], b["mv"][:, t, 0:1],
                                    b["rstd"][:, t:t + 1], ALU.subtract, ALU.mult).then_inc(self.normed, 1)

    def vector(self, dve, c):
        self.statistics(dve, c)
        self.normalise(dve, c)

    def scalar_rstd(self, act, c):
        nc, b = self.nc, self.b
        s = slice(TPC * c, TPC * (c + 1))
        act.wait_ge(self.moments, TPC * (c + 1))
        nc.scalar.activation(b["logv"][:, s], b["mv"][:, s, 1], ACT.Ln, bias=b["eps"][:, 0:1]).then_inc(self.logv, 1)
        act.wait_ge(self.logv, c + 1)
        nc.scalar.activation(b["rstd"][:, s], b["logv"][:, s], ACT.Exp, scale=-0.5).then_inc(self.rstd, 1)

    def tensor(self, pe, c, banks):
        nc, b = self.nc, self.b
        if c >= 2:
            pe.wait_ge(self.done, c - 1)
        for k in range(TPC):
            t = TPC * c + k
            pe.wait_ge(self.normed, t + 1)
            mm = nc.tensor.transpose(banks[c % 2][:, P * k:P * (k + 1)], b["xn"][:, t % (2 * TPC), :], b["ident"][:])
        mm.then_inc(self.turned, 1)

    def scalar_copy(self, act, c, banks):
        act.wait_ge(self.turned, c + 1)
        self.nc.scalar.activation(self.b["xnT"][:, CH * c:CH * (c + 1)], banks[c % 2][:, :],
                                  ACT.Copy).then_inc(self.done, 1)


class SplitOperands:

    def __init__(self, nc, sem, sb, xnT, norm):
        self.nc, self.xnT, self.norm = nc, xnT, norm
        weights = 2 * DFF0
        self.x = sb("x_parts", [P, 2, TOKENS], F32R)
        self.w = sb("w_parts", [P, 2, 2, weights], F32R)
        self.scaled, self.excess, self.x_excess = sb("w_scaled", [P, weights]), sb("w_excess", [P, weights]), sb("x_excess", [P, CH])
        self.factor = sb("split_factor", [P, 1])
        self.s_x_excess, self.s_x_high, self.s_x = sem("s_x_excess"), sem("s_x_high"), sem("s_x_parts")
        self.s_w_scaled, self.s_w_excess, self.s_w_high, self.s_w = (
            sem("s_w_scaled"), sem("s_w_excess"), sem("s_w_high"), sem("s_w_parts"))

    def vector_x(self, dve, c):
        nc, cols = self.nc, slice(CH * c, CH * (c + 1))
        x = self.xnT[:, cols]
        dve.wait_ge(self.norm.done, c + 1)
        if c:
            dve.wait_ge(self.s_x_high, c)
        nc.vector.scalar_tensor_tensor(out=self.x_excess[:], in0=x, scalar=SPLIT, in1=x,
                                       op0=ALU.mult, op1=ALU.subtract).then_inc(self.s_x_excess, 1)
        dve.wait_ge(self.s_x_excess, c + 1)
        nc.vector.scalar_tensor_tensor(out=self.x[:, 0, cols], in0=x, scalar=SPLIT, in1=self.x_excess[:],
                                       op0=ALU.mult, op1=ALU.subtract).then_inc(self.s_x_high, 1)
        dve.wait_ge(self.s_x_high, c + 1)
        nc.vector.tensor_tensor(self.x[:, 1, cols], x, self.x[:, 0, cols].bitcast(F32), ALU.subtract).then_inc(self.s_x, 1)

    def gpsimd_weights(self, pool, e, slot, w_up, loaded, used):
        nc = self.nc
        w = w_up[:, slot, :, :].rearrange("p m n -> p (m n)")
        pool.wait_ge(loaded[slot], (e - slot) * 24 + 48)
        if not (isinstance(e, int) and e < 2):
            pool.wait_ge(used, (e - 1) * CHUNKS * FH)
        nc.gpsimd.tensor_tensor(self.scaled[:], w, self.factor[:, 0:1].to_broadcast([P, 2 * DFF0]), ALU.mult).then_inc(self.s_w_scaled, 1)
        pool.wait_ge(self.s_w_scaled, e + 1)
        nc.gpsimd.tensor_tensor(self.excess[:], self.scaled[:], w, ALU.subtract).then_inc(self.s_w_excess, 1)
        pool.wait_ge(self.s_w_excess, e + 1)
        nc.gpsimd.tensor_tensor(self.w[:, slot, 0, :], self.scaled[:], self.excess[:], ALU.subtract).then_inc(self.s_w_high, 1)
        pool.wait_ge(self.s_w_high, e + 1)
        nc.gpsimd.tensor_tensor(self.w[:, slot, 1, :], w, self.w[:, slot, 0, :].bitcast(F32), ALU.subtract).then_inc(self.s_w, 1)
        pool.wait_ge(self.s_w, e + 1)


def build(nc, x_in, wq0, wk0, wv0, marks0, rw, rb, gate_w, up_w, down_w, wqk1, wv1, wo1, g1, wg2, wu2, wd2, out):
    ctx = ExitStack()
    with ctx:
        def sb(name, shape, dt=F32):
            return ctx.enter_context(nc.sbuf_tensor(name, shape, dt))

        def sem(name):
            return ctx.enter_context(nc.semaphore(name))

        b = {
            "x": sb("x", [P, TILES, P]), "xnT": sb("xnT", [P, TOKENS]), "xn": sb("xn", [P, 2 * TPC, P]),
            "bn": sb("bn", [P, TILES, 6]), "mv": sb("mv", [P, TILES, 2]), "logv": sb("logv", [P, TILES]),
            "rstd": sb("rstd", [P, TILES]), "eps": sb("eps", [P, 1]), "ident": sb("ident", [P, P]),
            "parts": sb("parts", [P, 4, 3, CH], BF16),
        }
        x, xnT = b["x"], b["xnT"]
        ident, ident16 = b["ident"], sb("ident16", [P, P], BF16)
        banks = [ctx.enter_context(nc.psum_tensor(f"bank{i}", [P, CH], F32)) for i in range(4)]
        pair_banks = [ctx.enter_context(nc.psum_tensor(f"pair{i}", [P, 2, CH], F32)) for i in range(2)]

        norms = [Norm(nc, ctx, f"n{n}", b) for n in range(4)]
        arena = sb("arena", [STACK, UNITS * HG * CH], BF16)
        w_up = sb("w_up", [P, 2, 2, DFF0])
        w_down = sb("w_down", [P, 2, FH, P])
        wv1_sb, wo1_sb = sb("wv1_sb", [P, H1 * DV1]), sb("wo1_sb", [P, PAIRS, P])
        wqk1_sb = sb("wqk1_sb", [P, 2, P])
        g_half = sb("g_half", [P, 1])
        ints = sb("ints", [P, 3, HID], I32)
        probs = sb("probs", [P, 4, 2, CH])
        scaled = b["parts"][:, 1:3, :, :].rearrange("p s n c -> p (s n c)").bitcast(F32)[:, 0:3 * HID].rearrange("p (m n) -> p m n", m=3)
        s_scaled = sem("s_scaled")
        work = sb("work", [P, 8 * CH])

        s_x = [sem(f"s_x{c}") for c in range(CHUNKS)]
        s_w0, s_router, s_w1, s_w2 = sem("s_w0"), sem("s_router"), sem("s_w1"), sem("s_w2")
        s_exp_w, s_gu = [sem("s_exp_w0"), sem("s_exp_w1")], sem("s_e_gu")
        x_dram = x_in.rearrange("(t p) d -> p t d", p=P)
        def expert_loads(e, slot):
            return [(w_up[:, slot, 0, :], gate_w[e, :, :], s_exp_w[slot]),
                    (w_up[:, slot, 1, :], up_w[e, :, :], s_exp_w[slot]),
                    (w_down[:, slot, :, :], down_w[e, :, :, :].rearrange("f p d -> p f d"), s_exp_w[slot])]

        norm_banks = [pair_banks[0][:, 0, :], pair_banks[1][:, 0, :]]
        first_layer = ExitStack()

        def sb_first(name, shape, dt=F32):
            return first_layer.enter_context(nc.sbuf_tensor(name, shape, dt))

        rw_sb, rb_sb = sb_first("rw_sb", [P, EXPERTS]), sb_first("rb_sb", [P, EXPERTS])
        split = SplitOperands(nc, sem, sb_first, xnT, norms[1])

        def router_products(pe, tiles):
            pe.wait_ge(s_router, 32)
            pe.wait_ge(norms[1].done, tiles[-1] // TPC + 1)
            for t in tiles:
                mm = nc.tensor.matmul(banks[0][:, EXPERTS * t:EXPERTS * (t + 1)], xnT[:, P * t:P * (t + 1)], rw_sb[:],
                                      start=True, stop=True)
            return mm

        first_attention(nc, ctx, sb_first, sem, b, norms, norm_banks, banks, pair_banks, arena, split,
                        router_products, w_up, s_exp_w, s_gu, probs, work, ident16,
                        s_x, s_w0, x_dram, wq0, wk0, wv0, marks0,
                        [(rw_sb[:], rw, s_router), (rb_sb[:], rb.to_broadcast([P, EXPERTS]), s_router)]
                        + expert_loads(0, 0) + expert_loads(1, 1))
        experts(nc, ctx, sb_first, sem, b, norms, norm_banks, banks, pair_banks, split, router_products, s_gu, work, w_up, w_down, s_exp_w, s_router,
                rw_sb, rb_sb, expert_loads,
                [(wqk1_sb[:], wqk1[:, :, 0, :], s_w1), (wv1_sb[:], wv1, s_w1),
                 (wo1_sb[:], wo1, s_w1), (g_half[0:DV1, :], g1, s_w1), (g_half[DV1:P, :], g1, s_w1),
                 (ints[:, 0, :], wg2, s_w2), (ints[:, 1, :], wu2, s_w2), (ints[:, 2, :], wd2.rearrange("p j d -> p (j d)"), s_w2)])
        first_layer.close()
        y_sb = sb("y_sb", [P, PAIRS + 1, SEQ])
        second_attention(nc, ctx, sb, sem, b, norms, norm_banks, banks, pair_banks, arena, probs, work,
                         wqk1_sb, wqk1, wv1_sb, wo1_sb, g_half, s_w1, y_sb, ints, scaled, s_w2, s_scaled)
        feed_forward(nc, ctx, sb, sem, b, norms, norm_banks, banks, pair_banks, work, scaled, s_scaled, out)


def first_attention(nc, ctx, sb, sem, b, norms, norm_banks, banks, pair_banks, arena, split_ops, router_products, w_up,
                    s_exp_w, s_gu, probs, work, ident16,
                    s_x, s_w0, x_dram, wq0, wk0, wv0, marks0, later_loads):
    x, xnT, ident = b["x"], b["xnT"], b["ident"]
    q_op = arena[:, :].rearrange("r (u h n) -> r u h n", u=UNITS, h=HG)
    q_rows = arena[:, :].rearrange("r (c m) -> r c m", c=CHUNKS)
    k_op = sb("k_op", [STACK, TOKENS], BF16)
    v_op = sb("v_op", [P, TILES, 32])
    wq_sb, wk_sb, wv_sb = sb("wq0_sb", [P, P]), sb("wk0_sb", [P, STACK]), sb("wv0_sb", [P, DH0])
    k_marks = sb("k_marks", [STACK, 3])
    q_parts = b["parts"]
    k_high, k_middle = (sb(f"k_{n}", [STACK, CH], BF16) for n in ("high", "middle"))
    q_rest = work[:, 0:CH]
    k_rest = work[0:STACK, CH:2 * CH]
    tops = sb("tops", [P, UNITS, TPC, HG])
    zero = sb("zero", [P, TPC, HG])
    neg, neg_rest = sb("neg", [P, TPC, HG]), sb("neg_rest", [P, TPC, HG])
    neg_parts = sb("neg_parts", [P, TPC, 3, HG], BF16)
    neg_t = sb("neg_t", [3 * HG, CH], BF16)
    pv_sb = work[:, 2 * CH:3 * CH]
    recip = sb("recip", [P, TPC, HG])
    ratio = work[:, 3 * CH:4 * CH].rearrange("p (t h d) -> p t h d", t=TPC, h=HG)[:, :, :, 0:DH0]

    norm, next_norm = norms[0], norms[1]
    s_zeroed, s_const = sem("s_zeroed"), sem("s_const")
    s_qproj, s_qhi, s_qrest, s_qmid, s_qlo = (sem(f"s_q_{n}") for n in ("proj", "hi", "rest", "mid", "lo"))
    s_kproj, s_khi, s_krest, s_kmid, s_k = (sem(f"s_k_{n}") for n in ("proj", "hi", "rest", "mid", "op"))
    s_copied = [sem("s_copied0"), sem("s_copied1")]
    COPIES = 16 * len(PRODUCTS0)
    s_vproj, s_v = sem("s_vproj"), sem("s_v")

    s_mx, s_red = sem("s_mx"), sem("s_red")
    s_neg, s_nhi, s_nrest, s_nmid, s_nparts = (sem(f"s_n_{n}") for n in ("neg", "hi", "rest", "mid", "parts"))
    s_nt, s_ncopied, s_ndma = sem("s_nt"), sem("s_ncopied"), sem("s_ndma")
    s_sc, s_exp, s_pv, s_pvcopy = sem("s_sc"), sem("s_exp"), sem("s_pv"), sem("s_pvcopy")
    s_ot, s_recip, s_ratio, s_added = sem("s_ot"), sem("s_recip"), sem("s_ratio"), sem("s_added")
    neg_bank = banks[3][:, :].bitcast(BF16)

    with nc.Block() as block:
        MAXES = TPC * HG
        PROJECT_K, PROJECT_Q = 3, 6
        NORM_TURNS, NORM_RSTDS = (3, 4, 6), (1, 2, 5)
        K_HIGH, Q_HIGH, K_MIDDLE = 5, 9, 11
        EARLY = 4
        EXPS = HG * KT

        def score_bank(u, h):
            if isinstance(u, int) and u == UNITS - 1 and h >= 2:
                return pair_banks[h - 2][:, 1, :]
            return banks[h % 2][:, :]

        @block.tensor
        def _(pe):
            def project_k(c):
                pe.wait_ge(norm.done, c + 1)
                if c:
                    pe.wait_ge(s_krest, c)
                nc.tensor.matmul(banks[3][0:STACK, :], wk_sb[:], xnT[:, CH * c:CH * (c + 1)],
                                 start=True, stop=True).then_inc(s_kproj, 1)

            def project_q_v(c):
                if c:
                    pe.wait_ge(s_qrest, c)
                nc.tensor.matmul(banks[2][:, :], wq_sb[:], xnT[:, CH * c:CH * (c + 1)], start=True, stop=True).then_inc(s_qproj, 1)
                for k in range(TPC):
                    mm = nc.tensor.matmul(banks[c % 2][:, DH0 * k:DH0 * (k + 1)],
                                          xnT[:, CH * c + P * k:CH * c + P * (k + 1)], wv_sb[:], start=True, stop=True)
                mm.then_inc(s_vproj, 1)

            def maximum(u, i, half, bt):
                t, h = i // HG, i % HG
                if half == 0 and not (isinstance(u, int) and u == 0 and i < 2):
                    pe.wait_ge(s_red, u * MAXES + i - 1)
                mm = nc.tensor.matmul(pair_banks[i % 2][:, half, :], q_op[:, u, h, P * t:P * (t + 1)],
                                      k_op[:, bt * SEQ + half * CH:bt * SEQ + (half + 1) * CH], start=True, stop=True)
                if half:
                    mm.then_inc(s_mx, 1)

            def scores(u, kt, h, bt):
                if isinstance(u, int) and u == UNITS - 1 and (kt or h >= 2):
                    if kt:
                        pe.wait_ge(s_exp, u * EXPS + HG * (kt - 1) + h + 1)
                elif not (isinstance(u, int) and u == 0 and kt == 0 and h < 2):
                    pe.wait_ge(s_exp, u * EXPS + HG * kt + h - 1)
                nc.tensor.matmul(score_bank(u, h), k_op[:, bt * SEQ + P * kt:bt * SEQ + P * (kt + 1)],
                                 q_op[:, u, h, :], start=True, stop=True).then_inc(s_sc, 1)

            def values(u, kt, bt):
                pe.wait_ge(s_exp, u * EXPS + HG * (kt + 1))
                for h in range(HG):
                    mm = nc.tensor.matmul(banks[2][32 * h:32 * h + 32, :], v_op[:, bt * KT + kt, :],
                                          probs[:, 2 * (kt % 2) + h // 2, h % 2, :], start=(kt == 0), stop=(kt == KT - 1))
                mm.then_inc(s_pv, 1)

            def negated(u):
                pe.wait_ge(s_nparts, u + 1)
                if not (isinstance(u, int) and u <= 1):
                    pe.wait_ge(s_added, u - 1)
                for t in range(TPC):
                    mm = nc.tensor.transpose(neg_bank[0:3 * HG, P * t:P * (t + 1)],
                                             neg_parts[:, t, :, :].rearrange("p n h -> p (n h)"), ident16[:])
                mm.then_inc(s_nt, 1)

            def outputs(u, final=False):
                pe.wait_ge(s_pvcopy, u + 1)
                if final:
                    pe.wait_ge(s_added, u)
                else:
                    pe.wait_ge(s_ncopied, u + 2)
                for t in range(TPC):
                    mm = nc.tensor.transpose(banks[3][:, P * t:P * (t + 1)], pv_sb[:, P * t:P * (t + 1)], ident[:])
                mm.then_inc(s_ot, 1)

            def unit(u, bt, bt_1, bt_2, first=False):
                u_is_last = isinstance(u, int) and u == UNITS - 1
                if u_is_last:
                    pe.wait_ge(s_red, UNITS * MAXES)
                last_bt = bt - 1 if isinstance(u, int) and u == UNITS // 2 else bt

                def part_of_maximum(kt, n):
                    i = EARLY + 2 * kt + n // 2
                    if i < MAXES and bt_1 is not None:
                        maximum(u + 1, i, n % 2, bt_1)
                    elif i >= MAXES and bt_2 is not None:
                        maximum(u + 2, i - MAXES, n % 2, bt_2)

                for kt in range(KT):
                    if kt == 0:
                        pe.wait_ge(s_ndma, 16 * (u + 1))
                    for h in range(HG):
                        scores(u, kt, h, bt)
                        for n in ((0, 1), (), (2,), (3,))[h]:
                            part_of_maximum(kt, n)
                        if h == 1:
                            if kt:
                                if kt == 1 and not first:
                                    pe.wait_ge(s_pvcopy, u)
                                values(u, kt - 1, bt)
                            elif not first:
                                values(u - 1, KT - 1, last_bt)
                    if kt == 2 and not first:
                        outputs(u - 1)
                    if kt == 6 and bt_1 is not None:
                        negated(u + 1)
                    if u_is_last and kt in NORM_TURNS:
                        next_norm.tensor(pe, NORM_TURNS.index(kt), norm_banks)

            half = UNITS // 2
            pe.wait_ge(s_const, 3)
            for c in range(2):
                norm.tensor(pe, c, banks)
            pe.wait_ge(s_w0, 64)
            for c in range(2):
                project_k(c)
                project_q_v(c)
            for c in range(2, CHUNKS):
                pe.wait_ge(s_v, c - 1)
                norm.tensor(pe, c, banks)
            project_k(2)
            project_q_v(2)
            pe.wait_ge(s_k, 2)
            pe.wait_ge(s_copied[0], COPIES)
            for i in range(MAXES + EARLY):
                if i == PROJECT_K:
                    project_k(3)
                if i == PROJECT_Q:
                    project_q_v(3)
                for n in range(2):
                    maximum(i // MAXES, i % MAXES, n, 0)
                if i == MAXES - 1:
                    pe.wait_ge(s_krest, CHUNKS)
                    pe.wait_ge(s_qrest, CHUNKS)
                    pe.wait_ge(s_v, CHUNKS)
            negated(0)
            unit(0, 0, 0, 0, first=True)
            pe.wait_ge(s_k, CHUNKS)
            for s in s_copied:
                pe.wait_ge(s, COPIES * CHUNKS // 2)
            with pe.Fori(1, half - 2) as u:
                unit(u, 0, 0, 0)
            unit(half - 2, 0, 0, 1)
            unit(half - 1, 0, 1, 1)
            unit(half, 1, 1, 1)
            with pe.Fori(half + 1, UNITS - 2) as u:
                unit(u, 1, 1, 1)
            unit(UNITS - 2, 1, 1, None)
            unit(UNITS - 1, 1, None, None)
            values(UNITS - 1, KT - 1, 1)
            router_products(pe, range(0, TPC))
            outputs(UNITS - 1, final=True)
            router_products(pe, range(TPC, TILES - TPC))

        @block.scalar
        def _(act):
            def split(c):
                act.wait_ge(s_kproj, c + 1)
                if c:
                    act.wait_ge(s_krest, c)
                nc.scalar.activation(k_high[:], banks[3][0:STACK, :], ACT.Identity, bias=k_marks[:, 2:3]).then_inc(s_khi, 1)
                if c >= 2:
                    act.wait_ge(s_copied[c % 2], COPIES * (c // 2))
                act.wait_ge(s_qproj, c + 1)
                nc.scalar.activation(q_parts[:, c % 2, 0, :], banks[2][:, :], ACT.Copy).then_inc(s_qhi, 1)
                act.wait_ge(s_krest, c + 1)
                if c:
                    act.wait_ge(s_k, c)
                nc.scalar.activation(k_middle[:], k_rest, ACT.Copy).then_inc(s_kmid, 1)
                act.wait_ge(s_qrest, c + 1)
                nc.scalar.activation(q_parts[:, c % 2, 1, :], q_rest, ACT.Copy).then_inc(s_qmid, 1)
                act.wait_ge(s_vproj, c + 1)
                nc.scalar.activation(v_op[:, TPC * c:TPC * (c + 1), 0:DH0],
                                     banks[c % 2][:, 0:TPC * DH0].rearrange("p (t d) -> p t d", t=TPC),
                                     ACT.Copy).then_inc(s_v, 1)

            def exponentials(u, kt):
                for h in range(HG):
                    act.wait_ge(s_sc, u * EXPS + HG * kt + h + 1)
                    if h == 0 and not (isinstance(u, int) and u == 0 and kt < 2):
                        act.wait_ge(s_pv, u * KT + kt - 1)
                    nc.scalar.activation(probs[:, 2 * (kt % 2) + h // 2, h % 2, :], score_bank(u, h), ACT.Exp,
                                         scale=SCALE0).then_inc(s_exp, 1)

            def negated(u):
                act.wait_ge(s_nt, u + 1)
                if not (isinstance(u, int) and u == 0):
                    act.wait_ge(s_ndma, 16 * u)
                nc.scalar.activation(neg_t[:, :], neg_bank[0:3 * HG, 0:CH], ACT.Copy).then_inc(s_ncopied, 1)

            def result(u):
                act.wait_ge(s_pv, KT * (u + 1))
                if not (isinstance(u, int) and u == 0):
                    act.wait_ge(s_ot, u)
                nc.scalar.activation(pv_sb, banks[2][:, :], ACT.Copy).then_inc(s_pvcopy, 1)

            def unit(u, first=False, last=False):
                for kt in range(KT):
                    exponentials(u, kt)
                    if kt == 0 and not first:
                        result(u - 1)
                    if kt == 6 and not last:
                        negated(u + 1)
                    if last and kt in NORM_RSTDS:
                        next_norm.scalar_rstd(act, NORM_RSTDS.index(kt))
                    if last and kt in NORM_TURNS:
                        next_norm.scalar_copy(act, NORM_TURNS.index(kt), norm_banks)

            nc.scalar.preload_act_table_set(LN_EXP)
            act.wait_ge(s_const, 6)
            act.wait_ge(s_w0, 64)
            for c in range(2):
                norm.scalar_rstd(act, c)
                norm.scalar_copy(act, c, banks)
            split(0)
            norm.scalar_rstd(act, 2)
            split(1)
            norm.scalar_copy(act, 2, banks)
            norm.scalar_rstd(act, 3)
            norm.scalar_copy(act, 3, banks)
            split(2)
            split(3)
            negated(0)
            unit(0, first=True)
            with act.Fori(1, UNITS - 1) as u:
                unit(u)
            unit(UNITS - 1, last=True)
            result(UNITS - 1)
            next_norm.scalar_rstd(act, CHUNKS - 1)

        @block.vector
        def _(dve):
            def take_k_high(c):
                dve.wait_ge(s_khi, c + 1)
                nc.vector.scalar_tensor_tensor(out=k_rest, in0=k_high[:], scalar=k_marks[:, 0:1], in1=banks[3][0:STACK, :],
                                               op0=ALU.mult, op1=ALU.add).then_inc(s_krest, 1)

            def take_q_high(c):
                dve.wait_ge(s_qhi, c + 1)
                if c:
                    dve.wait_ge(s_qlo, c)
                nc.vector.tensor_tensor(q_rest, banks[2][:, :], q_parts[:, c % 2, 0, :], ALU.subtract).then_inc(s_qrest, 1)

            def take_k_middle(c):
                dve.wait_ge(s_kmid, c + 1)
                nc.vector.scalar_tensor_tensor(out=k_op[:, CH * c:CH * (c + 1)], in0=k_middle[:], scalar=k_marks[:, 1:2],
                                               in1=k_rest, op0=ALU.mult, op1=ALU.add).then_inc(s_k, 1)

            def split(c):
                take_k_high(c)
                take_q_high(c)
                take_k_middle(c)

            def reduce(u, i):
                dve.wait_ge(s_mx, u * MAXES + i + 1)
                nc.vector.tensor_reduce(tops[:, u, i // HG, i % HG:i % HG + 1], pair_banks[i % 2][:, :, :], axis=AX.XY,
                                        op=ALU.max).then_inc(s_red, 1)
                if i == MAXES - 1:
                    dve.wait_ge(s_red, u * MAXES + MAXES)
                    if not (isinstance(u, int) and u == 0):
                        dve.wait_ge(s_nhi, u)
                        dve.wait_ge(s_nrest, u)
                    nc.vector.tensor_scalar(neg[:], tops[:, u, :, :], -1.0, None, ALU.mult).then_inc(s_neg, 1)

            def add_result(c, g):
                u = GROUPS * c + g
                bank = banks[3][:, :].rearrange("p (t h d) -> p t h d", t=TPC, h=HG)
                dve.wait_ge(s_ot, u + 1)
                nc.vector.reciprocal(recip[:, :, :], bank[:, :, :, DH0]).then_inc(s_recip, 1)
                dve.wait_ge(s_recip, u + 1)
                nc.vector.tensor_tensor(ratio, bank[:, :, :, 0:DH0],
                                        recip[:, :, :].unsqueeze(3).to_broadcast([P, TPC, HG, DH0]), ALU.mult).then_inc(s_ratio, 1)
                dve.wait_ge(s_ratio, u + 1)
                cols = x[:, TPC * c:TPC * (c + 1), bass.ds(g * (HG * DH0), HG * DH0)].rearrange("p t (h d) -> p t h d", h=HG)
                nc.vector.tensor_tensor(cols, cols, ratio, ALU.add).then_inc(s_added, 1)

            def step(c, g, two_ahead=True):
                u = GROUPS * c + g
                for i in range(EARLY, MAXES):
                    reduce(u + 2, i)
                    if i == EARLY + 5:
                        add_result(c, g)
                if two_ahead:
                    for i in range(EARLY):
                        reduce(u + 3, i)

            def load_and_normalise(c):
                dve.wait_ge(s_x[c], 16)
                norm.vector(dve, c)

            load_and_normalise(0)
            load_and_normalise(1)
            dve.wait_ge(s_w0, 64)
            split(0)
            load_and_normalise(2)
            split(1)
            load_and_normalise(3)
            split(2)
            for i in range(2 * MAXES + EARLY):
                if i == K_HIGH:
                    take_k_high(3)
                if i == Q_HIGH:
                    take_q_high(3)
                if i == K_MIDDLE:
                    take_k_middle(3)
                reduce(i // MAXES, i % MAXES)
            for c in range(CHUNKS - 1):
                with dve.Fori(0, GROUPS) as g:
                    step(c, g)
            step(CHUNKS - 1, 0)
            step(CHUNKS - 1, 1, two_ahead=False)
            next_norm.vector(dve, 0)
            next_norm.vector(dve, 1)
            add_result(CHUNKS - 1, 2)
            split_ops.vector_x(dve, 0)
            next_norm.vector(dve, 2)
            split_ops.vector_x(dve, 1)
            split_ops.vector_x(dve, 2)
            add_result(CHUNKS - 1, 3)
            dve.wait_ge(s_added, UNITS)
            next_norm.statistics(dve, CHUNKS - 1)

        @block.gpsimd
        def _(pool):
            def low(c):
                pool.wait_ge(s_qmid, c + 1)
                nc.gpsimd.tensor_tensor(q_parts[:, c % 2, 2, :], q_rest, q_parts[:, c % 2, 1, :], ALU.subtract).then_inc(s_qlo, 1)
                pool.wait_ge(s_qlo, c + 1)

            def zeros(c):
                nc.gpsimd.memset(q_rows[64:STACK, c, :].bitcast(F32), 0.0).then_inc(s_zeroed, 1)
                pool.wait_ge(s_zeroed, c + 1)

            def parts(u):
                view = lambda n: neg_parts[:, :, n, :]
                pool.wait_ge(s_neg, u + 1)
                if not (isinstance(u, int) and u == 0):
                    pool.wait_ge(s_nt, u)
                nc.gpsimd.tensor_tensor(view(0), neg[:], zero[:], ALU.add).then_inc(s_nhi, 1)
                pool.wait_ge(s_nhi, u + 1)
                nc.gpsimd.tensor_tensor(neg_rest[:], neg[:], view(0), ALU.subtract).then_inc(s_nrest, 1)
                pool.wait_ge(s_nrest, u + 1)
                nc.gpsimd.tensor_tensor(view(1), neg_rest[:], zero[:], ALU.add).then_inc(s_nmid, 1)
                pool.wait_ge(s_nmid, u + 1)
                nc.gpsimd.tensor_tensor(view(2), neg_rest[:], view(1), ALU.subtract).then_inc(s_nparts, 1)

            nc.gpsimd.memset(ident[:], 0.0).then_inc(s_const, 1)
            nc.gpsimd.memset(b["eps"][:], LN_EPS).then_inc(s_const, 1)
            nc.gpsimd.memset(zero[:], 0.0)
            nc.gpsimd.memset(split_ops.factor[:], SPLIT)
            pool.wait_ge(s_const, 2)
            nc.gpsimd.affine_select(out=ident[:], in_=ident[:], compare_op=ALU.not_equal, fill=1.0, base=0,
                                    pattern=[[-1, P]], channel_multiplier=1).then_inc(s_const, 1)
            nc.gpsimd.memset(v_op[:], 0.0).then_inc(s_const, 1)
            pool.wait_ge(s_const, 4)
            nc.gpsimd.tensor_copy(ident16[:], ident[:]).then_inc(s_const, 1)
            nc.gpsimd.memset(v_op[:, :, DH0:DH0 + 1], 1.0).then_inc(s_const, 1)
            pool.wait_ge(s_const, 6)
            zeros(0)
            zeros(1)
            zeros(2)
            low(0)
            low(1)
            zeros(3)
            low(2)
            low(3)
            parts(0)
            with pool.Fori(1, UNITS) as u:
                parts(u)
            for e in range(2):
                split_ops.gpsimd_weights(pool, e, e, w_up, s_exp_w, s_gu)

        @block.sync
        def _(sp):
            def copies(c):
                sp.wait_ge(s_zeroed, c + 1)
                sp.wait_ge(s_qlo, c + 1)
                for n, (part, _) in enumerate(PRODUCTS0):
                    sp.dma_start(q_rows[DH0 * n:DH0 * (n + 1), c, :], q_parts[:, c % 2, part, :]).then_inc(s_copied[c % 2], 16)

            def rows(u):
                sp.wait_ge(s_ncopied, u + 1)
                sp.dma_start(q_op[MROW:MROW + 3, u, :, :], neg_t[:, :]).then_inc(s_ndma, 16)

            for c in range(CHUNKS):
                sp.dma_start(x[:, TPC * c:TPC * (c + 1), :], x_dram[:, TPC * c:TPC * (c + 1), :]).then_inc(s_x[c], 16)
                if c == 0:
                    for dst, src in ((wk_sb, wk0), (wq_sb, wq0), (wv_sb, wv0), (k_marks, marks0)):
                        sp.dma_start(dst[:], src).then_inc(s_w0, 16)
            copies(0)
            copies(1)
            copies(2)
            rows(0)
            copies(3)
            with sp.Fori(1, UNITS) as u:
                rows(u)
            sp.wait_ge(s_ndma, 16 * UNITS)
            for dst, src, signal in later_loads:
                sp.dma_start(dst, src).then_inc(signal, 16)


def experts(nc, ctx, sb, sem, b, norms, norm_banks, banks, pair_banks, split, router_products, s_gu, work,
            w_up, w_down, s_exp_w, s_router, rw_sb, rb_sb,
            expert_loads, later_loads):
    x, xnT = b["x"], b["xnT"]
    rank = sb("rank", [P, EXPERTS])
    small = {n: sb(f"router_{n}", [P, TILES, EXPERTS]) for n in ("logit", "prob", "rest", "mark", "sel1", "sel2", "combine")}
    narrow = {n: sb(f"router_{n}", [P, TILES]) for n in ("max", "sum", "inv", "p1", "p2", "first", "den", "iden")}
    combine = small["combine"]
    hidden = work[:, 0:4 * CH].rearrange("p (s f n) -> p s f n", s=2, f=FH)
    silu = work[:, 4 * CH:6 * CH].rearrange("p (s n) -> p s n", s=2)
    wide = lambda ap: ap.unsqueeze(2).to_broadcast([P, TILES, EXPERTS])
    per_tile = lambda ap: ap.unsqueeze(1).to_broadcast([P, TILES, EXPERTS])

    norm, next_norm = norms[1], norms[2]
    s_rank, s_logit, s_shift, s_prob, s_route, s_combine = (sem(f"s_r_{n}") for n in ("rank", "logit", "shift", "prob", "chain", "combine"))
    s_silu, s_hid, s_down, s_acc = (sem(f"s_e_{n}") for n in ("silu", "hid", "down", "acc"))
    STEPS = CHUNKS

    with nc.Block() as block:
        @block.sync
        def _(sp):
            for dst, src, signal in later_loads:
                sp.dma_start(dst, src).then_inc(signal, 16)
            with sp.Fori(1, EXPERTS // 2) as pair:
                for slot in range(2):
                    sp.wait_ge(s_down, pair * 2 * STEPS + (slot - 1) * STEPS)
                    for dst, src, signal in expert_loads(pair * 2 + slot, slot):
                        sp.dma_start(dst, src).then_inc(signal, 16)

        @block.gpsimd
        def _(pool):
            for e in range(EXPERTS):
                nc.gpsimd.memset(rank[:, e:e + 1], float(EXPERTS - e)).then_inc(s_rank, 1)
            with pool.Fori(1, EXPERTS // 2) as pair:
                for slot in range(2):
                    split.gpsimd_weights(pool, pair * 2 + slot, slot, w_up, s_exp_w, s_gu)

        @block.tensor
        def _(pe):
            def gate_up(e, slot, c, f):
                i = (e * STEPS + c) * FH + f
                if not (isinstance(e, int) and e == 0 and c == 0):
                    pe.wait_ge(s_hid, i - 1)
                if isinstance(e, int) and e == 0 and f == 0:
                    pe.wait_ge(split.s_x, c + 1)
                for m in range(2):
                    for n, (wp, xp) in enumerate(((0, 0), (0, 1), (1, 0))):
                        mm = nc.tensor.matmul(pair_banks[f][:, m, :], split.w[:, slot, wp, DFF0 * m + P * f:DFF0 * m + P * (f + 1)],
                                              split.x[:, xp, CH * c:CH * (c + 1)], start=(n == 0), stop=(n == 2))
                mm.then_inc(s_gu, 1)

            def down(e, slot, c):
                k = e * STEPS + c
                pe.wait_ge(s_hid, FH * (k + 1))
                if not (isinstance(e, int) and e == 0 and c < 2):
                    pe.wait_ge(s_acc, TPC * (k - 1))
                for t in range(TPC):
                    for f in range(FH):
                        mm = nc.tensor.matmul(banks[c % 2][:, P * t:P * (t + 1)], hidden[:, c % 2, f, P * t:P * (t + 1)],
                                              w_down[:, slot, f, :], start=(f == 0), stop=(f == FH - 1))
                mm.then_inc(s_down, 1)

            def expert(e, slot, first=False):
                pe.wait_ge(split.s_w, e + 1)
                pe.wait_ge(s_exp_w[slot], (e - slot) * 24 + 48)
                for c in range(STEPS):
                    for f in range(FH):
                        if not (first and c == 0 and f == 0):
                            gate_up(e, slot, c, f)
                    if c:
                        down(e, slot, c - 1)
                    elif not first:
                        down(e - 1, 1 - slot, STEPS - 1)

            pe.wait_ge(split.s_w, 1)
            gate_up(0, 0, 0, 0)
            norm.tensor(pe, CHUNKS - 1, [None, banks[3]])
            router_products(pe, range(TILES - TPC, TILES)).then_inc(s_logit, 1)
            expert(0, 0, first=True)
            expert(1, 1)
            with pe.Fori(1, EXPERTS // 2) as pair:
                expert(pair * 2, 0)
                expert(pair * 2 + 1, 1)
            down(EXPERTS - 1, 1, STEPS - 1)
            for c in range(2):
                next_norm.tensor(pe, c, norm_banks)

        @block.scalar
        def _(act):
            nc.scalar.preload_act_table_set(LN_EXP)
            norm.scalar_copy(act, CHUNKS - 1, [None, banks[3]])
            act.wait_ge(s_shift, 1)
            nc.scalar.activation(small["prob"][:], small["logit"][:], ACT.Exp).then_inc(s_prob, 1)

            def expert(e):
                for c in range(STEPS):
                    for f in range(FH):
                        i = (e * STEPS + c) * FH + f
                        act.wait_ge(s_gu, i + 1)
                        if not (isinstance(e, int) and e == 0 and c == 0):
                            act.wait_ge(s_hid, i - 1)
                        nc.scalar.activation(silu[:, f, :], pair_banks[f][:, 0, :], ACT.Silu).then_inc(s_silu, 1)

            expert(0)
            with act.Fori(1, EXPERTS) as e:
                expert(e)
            nc.scalar.preload_act_table_set(LN_EXP)
            for c in range(CHUNKS - 1):
                next_norm.scalar_rstd(act, c)
            for c in range(2):
                next_norm.scalar_copy(act, c, norm_banks)

        @block.vector
        def _(dve):
            steps = [0]

            def chained(instruction):
                steps[0] += 1
                instruction.then_inc(s_route, 1)
                dve.wait_ge(s_route, steps[0])

            v = nc.vector

            def product(e, c, f):
                i = (e * STEPS + c) * FH + f
                dve.wait_ge(s_silu, i + 1)
                if not (isinstance(e, int) and e == 0 and c < 2):
                    dve.wait_ge(s_down, e * STEPS + c - 1)
                v.tensor_tensor(hidden[:, c % 2, f, :], silu[:, f, :], pair_banks[f][:, 1, :], ALU.mult).then_inc(s_hid, 1)

            def accumulate(e, c):
                k = e * STEPS + c
                dve.wait_ge(s_down, k + 1)
                if not (isinstance(e, int) and e == 0):
                    dve.wait_ge(s_acc, TPC * (k - 3))
                for t in range(TPC):
                    tile = TPC * c + t
                    v.scalar_tensor_tensor(out=x[:, tile, :], in0=banks[c % 2][:, P * t:P * (t + 1)],
                                           scalar=combine[:, tile, bass.ds(e, 1)], in1=x[:, tile, :],
                                           op0=ALU.mult, op1=ALU.add).then_inc(s_acc, 1)

            def expert(e, last=False):
                for c in range(STEPS):
                    for f in range(FH):
                        product(e, c, f)
                    if c:
                        accumulate(e, c - 1)
                    else:
                        accumulate(e - 1, STEPS - 1)
                    if last and c:
                        dve.wait_ge(s_acc, TPC * (e * STEPS + c))
                        next_norm.statistics(dve, c - 1)

            norm.normalise(dve, CHUNKS - 1)
            logit, prob, rest, mark, sel1, sel2 = (small[n][:] for n in ("logit", "prob", "rest", "mark", "sel1", "sel2"))
            dve.wait_ge(s_logit, 1)
            dve.wait_ge(s_rank, EXPERTS)
            chained(v.tensor_tensor(logit, banks[0][:, 0:TILES * EXPERTS].rearrange("p (t e) -> p t e", t=TILES),
                                    per_tile(rb_sb[:]), ALU.add))
            chained(v.tensor_reduce(narrow["max"][:], logit, axis=AX.X, op=ALU.max))
            v.tensor_tensor(logit, logit, wide(narrow["max"][:]), ALU.subtract).then_inc(s_shift, 1)
            for f in range(FH):
                product(0, 0, f)
            dve.wait_ge(s_prob, 1)
            chained(v.tensor_reduce(narrow["sum"][:], prob, axis=AX.X, op=ALU.add))
            chained(v.reciprocal(narrow["inv"][:], narrow["sum"][:]))
            chained(v.tensor_tensor(prob, prob, wide(narrow["inv"][:]), ALU.mult))
            chained(v.tensor_reduce(narrow["p1"][:], prob, axis=AX.X, op=ALU.max))
            chained(v.tensor_tensor(mark, prob, wide(narrow["p1"][:]), ALU.is_equal))
            chained(v.tensor_tensor(mark, mark, per_tile(rank[:]), ALU.mult))
            chained(v.tensor_reduce(narrow["first"][:], mark, axis=AX.X, op=ALU.max))
            chained(v.tensor_tensor(sel1, mark, wide(narrow["first"][:]), ALU.is_equal))
            for f in range(FH):
                product(0, 1, f)
            chained(v.scalar_tensor_tensor(out=rest, in0=sel1, scalar=-2.0, in1=prob, op0=ALU.mult, op1=ALU.add))
            chained(v.tensor_reduce(narrow["p2"][:], rest, axis=AX.X, op=ALU.max))
            chained(v.tensor_tensor(mark, rest, wide(narrow["p2"][:]), ALU.is_equal))
            chained(v.tensor_tensor(mark, mark, per_tile(rank[:]), ALU.mult))
            chained(v.tensor_reduce(narrow["first"][:], mark, axis=AX.X, op=ALU.max))
            chained(v.tensor_tensor(sel2, mark, wide(narrow["first"][:]), ALU.is_equal))
            split.vector_x(dve, CHUNKS - 1)
            for f in range(FH):
                product(0, 2, f)
            chained(v.tensor_tensor(narrow["den"][:], narrow["p1"][:], narrow["p2"][:], ALU.add))
            chained(v.reciprocal(narrow["iden"][:], narrow["den"][:]))
            chained(v.tensor_tensor(sel1, sel1, sel2, ALU.add))
            chained(v.tensor_tensor(sel1, sel1, prob, ALU.mult))
            v.tensor_tensor(combine[:], sel1, wide(narrow["iden"][:]), ALU.mult).then_inc(s_combine, 1)
            dve.wait_ge(s_combine, 1)

            for c in range(2):
                accumulate(0, c)
            for f in range(FH):
                product(0, STEPS - 1, f)
            accumulate(0, STEPS - 2)
            expert(1)
            with dve.Fori(2, EXPERTS - 1) as e:
                expert(e)
            expert(EXPERTS - 1, last=True)
            next_norm.normalise(dve, 0)
            next_norm.normalise(dve, 1)
            accumulate(EXPERTS - 1, STEPS - 1)


def second_attention(nc, ctx, sb, sem, b, norms, norm_banks, banks, pair_banks, arena, probs, work,
                     wqk_sb, wqk_dram, wv_sb, wo_sb, g_half, s_w1, y_sb, ints, scaled, s_w2, s_scaled):
    x, xnT = b["x"], b["xnT"]
    qk_op = arena[:, :].rearrange("r (s h n) -> r s h n", s=2, h=H1)
    parts = b["parts"]
    tri, means, one = sb("tri", [P, P]), sb("means", [P, P]), sb("one", [P, 1])
    v_sb = sb("v_sb", [P, KT, P])
    w_next = sb("w_next", [P, P])
    y_square, log_mean, rstd = (work[:, CH * n:CH * (n + 1)] for n in range(3))
    rests = [work[:, CH * n:CH * (n + 1)] for n in range(3, 5)]

    norm, next_norm = norms[2], norms[3]
    s_masks, s_g = sem("s_masks"), sem("s_g")
    s_proj, s_hi, s_rest, s_mid, s_lo = (sem(f"s_b_{n}") for n in ("proj", "hi", "rest", "mid", "lo"))
    s_copied, s_built, s_w_next = [sem("s_b_copied0"), sem("s_b_copied1")], sem("s_b_built"), sem("s_b_w")
    s_sc, s_square, s_weight, s_sum = (sem(f"s_a_{n}") for n in ("score", "square", "weight", "sum"))
    s_v, s_vcopy = sem("s_a_v"), sem("s_a_vcopy")
    s_ysq, s_mean, s_log, s_rstd, s_y = (sem(f"s_a_{n}") for n in ("ysq", "mean", "log", "rstd", "y"))
    s_o, s_added = sem("s_a_o"), sem("s_a_added")

    ITEMS = [(c, kt) for c in range(2) for kt in range(TPC * (c + 1))]
    N = len(ITEMS)
    LAG = 3
    LAST = {0: TPC, 1: N}
    COPIES = 16 * len(PRODUCTS1)
    OPERANDS = 4
    GROUP_PAIRS = PAIRS // 2

    def operand(m):
        return m // (2 * OPERANDS), (m // OPERANDS) % 2, (m % OPERANDS) // 2, m % 2

    def slot(m):
        return m if isinstance(m, int) and m < OPERANDS else 0

    def first_column(c, kt):
        return max(0, kt - TPC * c) * P

    with nc.Block() as block:
        @block.gpsimd
        def _(pool):
            nc.gpsimd.memset(tri[:], 1.0).then_inc(s_masks, 1)
            nc.gpsimd.memset(means[:], 0.0).then_inc(s_masks, 1)
            nc.gpsimd.memset(one[:], 1.0).then_inc(s_masks, 1)
            pool.wait_ge(s_masks, 3)
            nc.gpsimd.affine_select(out=tri[:], in_=tri[:], compare_op=ALU.is_ge, fill=0.0, base=0,
                                    pattern=[[1, P]], channel_multiplier=-1).then_inc(s_masks, 1)
            pool.wait_ge(s_masks, 4)
            for h in range(2):
                nc.gpsimd.memset(means[DV1 * h:DV1 * (h + 1), DV1 * h:DV1 * (h + 1)], 1.0 / DV1).then_inc(s_masks, 1)
                pool.wait_ge(s_masks, 5 + h)
            pool.wait_ge(s_w1, 16 * 5)
            nc.gpsimd.tensor_scalar(g_half[:], g_half[:], 0.5, None, ALU.mult).then_inc(s_g, 1)

            def low(m):
                pool.wait_ge(s_mid, m + 1)
                nc.gpsimd.tensor_tensor(parts[:, slot(m), 2, :], rests[slot(m) % 2], parts[:, slot(m), 1, :],
                                        ALU.subtract).then_inc(s_lo, 1)

            for m in range(OPERANDS):
                low(m)
            with pool.Fori(OPERANDS, 4 * OPERANDS) as m:
                low(m)

        @block.sync
        def _(sp):
            def copies(m, signal):
                _, half, c, which = operand(m)
                sp.wait_ge(s_lo, m + 1)
                for i, product in enumerate(PRODUCTS1):
                    sp.dma_start(qk_op[DF * i:DF * (i + 1), which, HALF * half:HALF * (half + 1), CH * c:CH * (c + 1)],
                                 parts[:, slot(m), product[which], :]).then_inc(signal, 16)

            for m in range(OPERANDS):
                copies(m, s_copied[m // 2])
            for group in range(1, 4):
                _, half, _, _ = operand(OPERANDS * group)
                with sp.Fori(0, 2) as c:
                    for which in range(2):
                        m = OPERANDS * group + 2 * c + which
                        sp.wait_ge(s_proj, m)
                        sp.dma_start(w_next[:], wqk_dram[:, which, half, :]).then_inc(s_w_next, 16)
                        if group > 1:
                            sp.wait_ge(s_sc, N * GROUP_PAIRS * (group - 1))
                        sp.wait_ge(s_lo, m + 1)
                        for i, product in enumerate(PRODUCTS1):
                            sp.dma_start(qk_op[DF * i:DF * (i + 1), which, HALF * half:HALF * (half + 1), bass.ds(c * CH, CH)],
                                         parts[:, 0, product[which], :]).then_inc(s_built, 16)
            for s in s_copied:
                sp.wait_ge(s, COPIES * 2)
            sp.wait_ge(s_built, COPIES * OPERANDS * 3)

        @block.tensor
        def _(pe):
            def build(m):
                bt, _, c, which = operand(m)
                if isinstance(m, int) and m < OPERANDS:
                    bank, weight = banks[2 + m % 2], wqk_sb[:, which, :]
                    if m >= 2:
                        pe.wait_ge(s_rest, m - 1)
                else:
                    bank, weight = banks[2], w_next[:]
                    pe.wait_ge(s_w_next, 16 * (m - OPERANDS + 1))
                    pe.wait_ge(s_vcopy, 2 * (m - OPERANDS) + 2)
                nc.tensor.matmul(bank[:, :], weight, xnT[:, bass.ds(bt * SEQ + c * CH, CH)],
                                 start=True, stop=True).then_inc(s_proj, 1)

            def values(g, bt, r):
                if not (isinstance(g, int) and g == 0 and r == 0):
                    pe.wait_ge(s_vcopy, 2 * g + r)
                for k in range(4):
                    col = SEQ * bt + P * (4 * r + k)
                    mm = nc.tensor.matmul(banks[2][:, P * k:P * (k + 1)], xnT[:, col:col + P],
                                          wv_sb[:, bass.ds((g - PAIRS * bt) * P, P)], start=True, stop=True)
                mm.then_inc(s_v, 1)

            def scores(g, bt, i):
                c, kt = ITEMS[i]
                q0 = first_column(c, kt)
                if not (isinstance(g, int) and g == 0 and i < 2):
                    pe.wait_ge(s_square, N * g + i - 1)
                for h in range(2):
                    head = (g - PAIRS * bt) * 2 + h
                    mm = nc.tensor.matmul(pair_banks[i % 2][:, h, q0:CH], qk_op[:, 1, head, P * kt:P * (kt + 1)],
                                          qk_op[:, 0, head, CH * c + q0:CH * (c + 1)], start=True, stop=True)
                mm.then_inc(s_sc, 1)

            def sums(g, i):
                c, kt = ITEMS[i]
                q0 = first_column(c, kt)
                pe.wait_ge(s_weight, N * g + i + 1)
                if kt == 0 and not (isinstance(g, int) and g == 0):
                    pe.wait_ge(s_y, 2 * g + c - 1)
                if c == 0 and kt == 0:
                    pe.wait_ge(s_vcopy, 2 * g + 1)
                if kt == TPC:
                    pe.wait_ge(s_vcopy, 2 * g + 2)
                for h in range(2):
                    mm = nc.tensor.matmul(banks[c][DV1 * h:DV1 * (h + 1), q0:CH], v_sb[:, kt, DV1 * h:DV1 * (h + 1)],
                                          probs[:, i % 4, h, q0:CH], start=(kt == 0), stop=(i + 1 == LAST[c]))
                mm.then_inc(s_sum, 1)

            def mean(q):
                pe.wait_ge(s_ysq, q + 1)
                if not (isinstance(q, int) and q == 0):
                    pe.wait_ge(s_log, q)
                nc.tensor.matmul(banks[3][:, :], means[:], y_square, start=True, stop=True).then_inc(s_mean, 1)

            def pair(g, bt, first=False, builds=True):
                values(g, bt, 0)
                for i in range(N):
                    if first and i == LAST[0]:
                        pe.wait_ge(s_copied[1], COPIES * 2)
                    scores(g, bt, i)
                    if i >= LAG:
                        sums(g, i - LAG)
                    elif not first:
                        sums(g - 1, N + i - LAG)
                    if i == 1:
                        values(g, bt, 1)
                    if i == 3 and not first:
                        mean(2 * g - 1)
                    if i == 4 and builds:
                        build(g + OPERANDS)
                    if i == 7 and isinstance(g, int) and g == PAIRS:
                        pe.wait_ge(s_y, 2 * PAIRS)
                        project(0, 1, range(PAIRS), lambda t: banks[3][:, P * t:P * (t + 1)])
                        pe.wait_ge(s_rest, g + OPERANDS + 1)
                        project(0, 0, range(PAIRS), lambda t: banks[2][:, P * t:P * (t + 1)])
                        pe.wait_ge(s_added, 1)
                    if i == 8:
                        mean(2 * g)

            def project(bt, r, pairs, region):
                for t in range(4):
                    for p in pairs:
                        col = P * (4 * r + t)
                        y = y_sb[:, (PAIRS * bt + p) % (PAIRS + 1), col:col + P]
                        mm = nc.tensor.matmul(region(t), y, wo_sb[:, p, :],
                                              start=(p == 0), stop=(p == PAIRS - 1))
                if pairs[-1] == PAIRS - 1:
                    mm.then_inc(s_o, 1)

            for m in range(OPERANDS):
                build(m)
                if m % 2:
                    norm.tensor(pe, 2 + m // 2, banks)
            pe.wait_ge(norm.done, CHUNKS)
            pe.wait_ge(s_rest, OPERANDS)
            pe.wait_ge(s_copied[0], COPIES * 2)
            pair(0, 0, first=True)
            with pe.Fori(1, GROUP_PAIRS) as g:
                pair(g, 0)
            pe.wait_ge(s_built, COPIES * OPERANDS)
            with pe.Fori(GROUP_PAIRS, PAIRS) as g:
                pair(g, 0)
            pe.wait_ge(s_built, COPIES * OPERANDS * 2)
            pair(PAIRS, 1)
            pe.wait_ge(s_added, 2)
            with pe.Fori(PAIRS + 1, PAIRS + GROUP_PAIRS) as g:
                pair(g, 1)
            pe.wait_ge(s_built, COPIES * OPERANDS * 3)
            with pe.Fori(PAIRS + GROUP_PAIRS, 2 * PAIRS) as g:
                pair(g, 1, builds=False)
            for i in range(N - LAG, N):
                sums(2 * PAIRS - 1, i)
            for c in range(2):
                next_norm.tensor(pe, c, norm_banks)
            pe.wait_ge(s_y, 4 * PAIRS - 1)
            project(1, 0, range(PAIRS), lambda t: banks[2][:, P * t:P * (t + 1)])
            mean(4 * PAIRS - 1)
            pe.wait_ge(next_norm.done, 2)
            project(1, 1, range(PAIRS - 1), lambda t: pair_banks[t // 2][:, t % 2, 0:P])
            pe.wait_ge(s_y, 4 * PAIRS)
            project(1, 1, [PAIRS - 1], lambda t: pair_banks[t // 2][:, t % 2, 0:P])

        @block.scalar
        def _(act):
            def high(m):
                act.wait_ge(s_proj, m + 1)
                if isinstance(m, int) and m == OPERANDS:
                    act.wait_ge(s_copied[0], COPIES * 2)
                elif not (isinstance(m, int) and m < OPERANDS):
                    act.wait_ge(s_built, COPIES * (m - OPERANDS))
                bank = banks[2 + m % 2] if isinstance(m, int) and m < OPERANDS else banks[2]
                nc.scalar.activation(parts[:, slot(m), 0, :], bank[:, :], ACT.Copy).then_inc(s_hi, 1)

            def middle(m):
                act.wait_ge(s_rest, m + 1)
                nc.scalar.activation(parts[:, slot(m), 1, :], rests[slot(m) % 2], ACT.Copy).then_inc(s_mid, 1)

            def square(g, i):
                c, kt = ITEMS[i]
                q0 = first_column(c, kt)
                act.wait_ge(s_sc, N * g + i + 1)
                if not (isinstance(g, int) and g == 0 and i < 4):
                    act.wait_ge(s_sum, N * g + i - 3)
                nc.scalar.activation(probs[:, i % 4, :, q0:CH], pair_banks[i % 2][:, :, q0:CH], ACT.Square,
                                     bias=1.0, scale=0.25).then_inc(s_square, 1)

            def result_square(g, c):
                q = 2 * g + c
                act.wait_ge(s_sum, N * g + LAST[c])
                if not (isinstance(g, int) and g == 0 and c == 0):
                    act.wait_ge(s_mean, q)
                nc.scalar.activation(y_square, banks[c][:, :], ACT.Square, scale=0.5).then_inc(s_ysq, 1)

            def result_rstd(q):
                act.wait_ge(s_mean, q + 1)
                if not (isinstance(q, int) and q == 0):
                    act.wait_ge(s_rstd, q)
                    act.wait_ge(s_y, q)
                nc.scalar.activation(log_mean, banks[3][:, :], ACT.Ln, bias=b["eps"][:, 0:1]).then_inc(s_log, 1)
                act.wait_ge(s_log, q + 1)
                nc.scalar.activation(rstd, log_mean, ACT.Exp, scale=-0.5).then_inc(s_rstd, 1)

            def pair(g, first=False, builds=True):
                for i in range(N):
                    if i == 2 and not first:
                        result_square(g - 1, 1)
                    if i == 4 and not first:
                        result_rstd(2 * g - 1)
                    if i == 6 and builds:
                        high(g + OPERANDS)
                    if i == 7:
                        result_square(g, 0)
                    if i == 7 and builds:
                        middle(g + OPERANDS)
                    if i == 10:
                        result_rstd(2 * g)
                    square(g, i)

            nc.scalar.preload_act_table_set(LN_EXP)
            act.wait_ge(s_masks, 3)
            for m in range(OPERANDS):
                high(m)
                middle(m)
                if m == 1:
                    norm.scalar_rstd(act, CHUNKS - 1)
                if m >= 2:
                    norm.scalar_copy(act, m, banks)
            pair(0, first=True)
            with act.Fori(1, PAIRS) as g:
                pair(g)
            pair(PAIRS)
            for c in range(2):
                next_norm.scalar_rstd(act, c)
            with act.Fori(PAIRS + 1, PAIRS + GROUP_PAIRS) as g:
                pair(g)
            with act.Fori(PAIRS + GROUP_PAIRS, 2 * PAIRS) as g:
                pair(g, builds=False)
            result_square(2 * PAIRS - 1, 1)
            for c in range(2):
                next_norm.scalar_copy(act, c, norm_banks)
            result_rstd(4 * PAIRS - 1)
            next_norm.scalar_rstd(act, 2)

        @block.vector
        def _(dve):
            def take_high(m):
                dve.wait_ge(s_hi, m + 1)
                if not (isinstance(m, int) and m < OPERANDS):
                    dve.wait_ge(s_lo, m)
                elif m >= 2:
                    dve.wait_ge(s_lo, m - 1)
                bank = banks[2 + m % 2] if isinstance(m, int) and m < OPERANDS else banks[2]
                nc.vector.tensor_tensor(rests[slot(m) % 2], bank[:, :], parts[:, slot(m), 0, :], ALU.subtract).then_inc(s_rest, 1)

            def copy_values(g, r):
                dve.wait_ge(s_v, 2 * g + r + 1)
                if not (isinstance(g, int) and g == 0):
                    dve.wait_ge(s_sum, N * g - (N - 8) * (1 - r))
                nc.vector.tensor_copy(v_sb[:, 4 * r:4 * r + 4, :], banks[2][:, :].rearrange("p (k n) -> p k n", k=4)).then_inc(s_vcopy, 1)

            def weights(g, i):
                c, kt = ITEMS[i]
                q0 = first_column(c, kt)
                tile = probs[:, i % 4, :, :]
                dve.wait_ge(s_square, N * g + i + 1)
                if kt >= TPC * c:
                    diagonal = tile[:, :, q0:q0 + P]
                    mm = nc.vector.scalar_tensor_tensor(out=diagonal, in0=diagonal, scalar=1.0,
                                                        in1=tri[:].unsqueeze(1).to_broadcast([P, 2, P]),
                                                        op0=ALU.add, op1=ALU.mult)
                    q0 += P
                if q0 < CH:
                    mm = nc.vector.tensor_scalar(tile[:, :, q0:CH], tile[:, :, q0:CH], 1.0, None, ALU.add)
                mm.then_inc(s_weight, 1)

            def normalise(g, c):
                q = 2 * g + c
                dve.wait_ge(s_rstd, q + 1)
                nc.vector.scalar_tensor_tensor(out=y_sb[:, g % (PAIRS + 1), CH * c:CH * (c + 1)], in0=banks[c][:, :],
                                               scalar=g_half[:, 0:1], in1=rstd, op0=ALU.mult, op1=ALU.mult).then_inc(s_y, 1)

            def pair(g, first=False, builds=True):
                copy_values(g, 0)
                for i in range(N):
                    if i == 4 and not first:
                        normalise(g - 1, 1)
                    if i == 6 and builds:
                        take_high(g + OPERANDS)
                    if i == 10:
                        normalise(g, 0)
                    weights(g, i)
                    if i == 2:
                        copy_values(g, 1)
                    if i == 7 and isinstance(g, int) and g == PAIRS:
                        add(0, 1, banks[3], 1)
                        add(0, 0, banks[2], 2)
                        dve.wait_ge(s_added, 2)
                        next_norm.statistics(dve, 0)
                        next_norm.statistics(dve, 1)

            def add(bt, r, bank, count):
                dve.wait_ge(s_o, count)
                tiles = x[:, KT * bt + 4 * r:KT * bt + 4 * r + 4, :]
                nc.vector.tensor_tensor(tiles, bank[:, :].rearrange("p (t d) -> p t d", t=4), tiles, ALU.add).then_inc(s_added, 1)

            for m in range(OPERANDS):
                take_high(m)
                if m == 1:
                    norm.statistics(dve, CHUNKS - 1)
                    norm.normalise(dve, 2)
                if m == 3:
                    norm.normalise(dve, 3)
            dve.wait_ge(s_masks, 4)
            dve.wait_ge(s_g, 1)
            pair(0, first=True)
            with dve.Fori(1, PAIRS) as g:
                pair(g)
            pair(PAIRS)
            next_norm.normalise(dve, 0)
            next_norm.normalise(dve, 1)
            dve.wait_ge(s_w2, 48)
            for m in range(3):
                nc.vector.tensor_scalar(scaled[:, m, :], ints[:, m, :], QSCALE, None, ALU.mult).then_inc(s_scaled, 1)
            with dve.Fori(PAIRS + 1, PAIRS + GROUP_PAIRS) as g:
                pair(g)
            with dve.Fori(PAIRS + GROUP_PAIRS, 2 * PAIRS) as g:
                pair(g, builds=False)
            normalise(2 * PAIRS - 1, 1)
            add(1, 0, banks[2], 3)
            dve.wait_ge(s_added, 3)
            next_norm.statistics(dve, 2)
            dve.wait_ge(s_o, 4)
            for i in range(2):
                tiles = x[:, 2 * KT - 4 + 2 * i:2 * KT - 2 + 2 * i, :]
                nc.vector.tensor_tensor(tiles, pair_banks[i][:, :, 0:P], tiles, ALU.add).then_inc(s_added, 1)


def feed_forward(nc, ctx, sb, sem, b, norms, norm_banks, banks, pair_banks, work, scaled, s_scaled, out):
    x, xnT = b["x"], b["xnT"]
    hidden = work[:, 0:6 * CH].rearrange("p (s j n) -> p s j n", s=2, j=HT)
    silu = work[:, 6 * CH:8 * CH].rearrange("p (s n) -> p s n", s=2)
    norm = norms[3]
    s_gu, s_silu, s_hid, s_down, s_sum = (sem(f"s_f_{n}") for n in ("gu", "silu", "hid", "down", "sum"))
    s_out = sem("s_out")
    out_dram = out.rearrange("(t p) d -> p t d", p=P)

    with nc.Block() as block:
        @block.sync
        def _(sp):
            for c in range(CHUNKS):
                sp.wait_ge(s_sum, c + 1)
                sp.dma_start(out_dram[:, TPC * c:TPC * (c + 1), :], x[:, TPC * c:TPC * (c + 1), :]).then_inc(s_out, 16)
            sp.wait_ge(s_out, 16 * CHUNKS)

        @block.tensor
        def _(pe):
            def gate_up(c, j):
                i = HT * c + j
                if i >= 2:
                    pe.wait_ge(s_hid, i - 1)
                for m in range(2):
                    mm = nc.tensor.matmul(pair_banks[i % 2][:, m, :], scaled[:, m, P * j:P * (j + 1)],
                                          xnT[:, CH * c:CH * (c + 1)], start=True, stop=True)
                mm.then_inc(s_gu, 1)

            def down(c):
                pe.wait_ge(s_hid, HT * (c + 1))
                if c >= 2:
                    pe.wait_ge(s_sum, c - 1)
                for t in range(TPC):
                    for j in range(HT):
                        mm = nc.tensor.matmul(banks[2 + c % 2][:, P * t:P * (t + 1)], hidden[:, c % 2, j, P * t:P * (t + 1)],
                                              scaled[:, 2, P * j:P * (j + 1)], start=(j == 0), stop=(j == HT - 1))
                mm.then_inc(s_down, 1)

            pe.wait_ge(s_scaled, 3)
            for c in range(CHUNKS):
                pe.wait_ge(norm.done, c + 1)
                for j in range(HT):
                    gate_up(c, j)
                    if j == 0 and c:
                        down(c - 1)
                    if c == 0 and j:
                        norm.tensor(pe, 1 + j, banks)
            down(CHUNKS - 1)

        @block.scalar
        def _(act):
            nc.scalar.preload_act_table_set(LN_EXP)
            norm.scalar_rstd(act, 3)
            for i in range(HT * CHUNKS):
                if i in (2, 3):
                    norm.scalar_copy(act, i, banks)
                act.wait_ge(s_gu, i + 1)
                if i >= 2:
                    act.wait_ge(s_hid, i - 1)
                nc.scalar.activation(silu[:, i % 2, :], pair_banks[i % 2][:, 0, :], ACT.Silu).then_inc(s_silu, 1)

        @block.vector
        def _(dve):
            norm.statistics(dve, 3)
            norm.normalise(dve, 2)

            def add(c):
                dve.wait_ge(s_down, c + 1)
                tiles = x[:, TPC * c:TPC * (c + 1), :]
                nc.vector.tensor_tensor(tiles, banks[2 + c % 2][:, :].rearrange("p (t d) -> p t d", t=TPC), tiles,
                                        ALU.add).then_inc(s_sum, 1)

            for c in range(CHUNKS):
                for j in range(HT):
                    i = HT * c + j
                    if i == 1:
                        norm.normalise(dve, 3)
                    dve.wait_ge(s_silu, i + 1)
                    if c >= 2:
                        dve.wait_ge(s_down, c - 1)
                    nc.vector.tensor_tensor(hidden[:, c % 2, j, :], silu[:, i % 2, :], pair_banks[i % 2][:, 1, :],
                                            ALU.mult).then_inc(s_hid, 1)
                if c:
                    add(c - 1)
            add(CHUNKS - 1)


def kernel(L0_attn_x, L0_attn_Wq, L0_attn_Wk, L0_attn_Wv, L0_ffn_router_w, L0_ffn_router_b, L0_ffn_gate_w,
           L0_ffn_up_w, L0_ffn_down_w, L1_attn_Wq, L1_attn_Wk, L1_attn_Wv, L1_attn_Wo, L1_attn_g_weight,
           L1_ffn_w_gate, L1_ffn_w_up, L1_ffn_w_down):
    import concourse.bacc as bacc
    from concourse.bass_utils import run_bass_kernel_spmd

    by_feature0 = L0_attn_Wq.reshape(H0, DH0, P).transpose(2, 1, 0).reshape(P, P)
    by_feature1 = [w.reshape(2, HALF, DF, P).transpose(3, 0, 2, 1).reshape(P, 2, P) for w in (L1_attn_Wq, L1_attn_Wk)]
    stacked_key = np.zeros((P, STACK), L0_attn_Wk.dtype)
    marks = np.zeros((STACK, 3), np.float32)
    for n, (_, part) in enumerate(PRODUCTS0):
        rows = slice(DH0 * n, DH0 * (n + 1))
        stacked_key[:, rows] = L0_attn_Wk.T
        marks[rows, 0:part] = -1.0
    marks[MROW:MROW + 3, 0] = marks[MROW:MROW + 3, 2] = 1.0
    arrays = {
        "x_in": L0_attn_x.reshape(TOKENS, P), "wq0": by_feature0, "wk0": stacked_key, "wv0": L0_attn_Wv.T,
        "marks0": marks,
        "rw": L0_ffn_router_w.T, "rb": L0_ffn_router_b.reshape(1, EXPERTS),
        "gate_w": L0_ffn_gate_w, "up_w": L0_ffn_up_w, "down_w": L0_ffn_down_w.reshape(EXPERTS, FH, P, P),
        "wqk1": np.stack(by_feature1, axis=1), "wv1": L1_attn_Wv.T,
        "wo1": L1_attn_Wo.T.reshape(PAIRS, P, P).transpose(1, 0, 2), "g1": L1_attn_g_weight.reshape(DV1, 1),
        "wg2": L1_ffn_w_gate.T, "wu2": L1_ffn_w_up.T, "wd2": L1_ffn_w_down.T.reshape(HT, P, P).transpose(1, 0, 2),
    }
    arrays = {name: np.ascontiguousarray(a) for name, a in arrays.items()}
    nc = bacc.Bacc("TRN2", target_bir_lowering=False, num_devices=1)
    aps = [nc.dram_tensor(name, a.shape, mybir.dt.from_np(a.dtype), kind="ExternalInput").ap() for name, a in arrays.items()]
    aps.append(nc.dram_tensor("out", (TOKENS, P), F32, kind="ExternalOutput").ap())
    build(nc, *aps)
    result = run_bass_kernel_spmd(nc, [arrays], core_ids=[0])
    return result.results[0]["out"].reshape(BATCH, SEQ, P)
```
